# Optimizing a Trainium2 kernel written in Bass

```python
import numpy as np
import jax
import jax.numpy as jnp

def _softmax(x, axis=-1):
    return jax.nn.softmax(x, axis=axis)

def _gelu(x):
    return jax.nn.gelu(x, approximate=True)

def _silu(x):
    return jax.nn.silu(x)

def _sigmoid(x):
    return jax.nn.sigmoid(x)

def _layernorm(x, axis=-1, eps=1e-05):
    m = jnp.mean(x, axis=axis, keepdims=True)
    v = jnp.var(x, axis=axis, keepdims=True)
    return (x - m) / jnp.sqrt(v + eps)

def _scatter_add(tgt, idx, src, axis=0):
    return tgt.at[idx].add(src)

def _segment_sum(src, seg, n):
    return jax.ops.segment_sum(src, seg, n)
kernel_name = 'mk_adaln_d2_jaxref_r8_0219d5'

def setup_inputs(seed: int=0):
    np.random.seed(seed)
    _w = jnp.asarray

    def _L0_attn_setup():
        import jax, jax.numpy as jnp
        import numpy as np
        DIM = 128
        HEADS = 16
        HIDDEN = 512
        EPS_ATTN = 1e-06
        EPS_LN = 1e-05

        def layer_norm(x, g, b):
            mu = jnp.mean(x, axis=-1, keepdims=True)
            var = jnp.var(x, axis=-1, keepdims=True)
            return (x - mu) * jax.lax.rsqrt(var + EPS_LN) * g + b
        key = jax.random.key(seed)
        ks = jax.random.split(key, 8)
        s = 0.02
        return {'x': jax.random.normal(ks[0], (4, 512, DIM), jnp.float32), 'norm1_g': jnp.ones((DIM,), jnp.float32), 'norm1_b': jnp.zeros((DIM,), jnp.float32), 'qkv_w': jax.random.normal(ks[1], (3 * DIM, DIM), jnp.float32) * s, 'proj_w': jax.random.normal(ks[2], (DIM, DIM), jnp.float32) * s, 'proj_b': jnp.zeros((DIM,), jnp.float32), 'norm2_g': jnp.ones((DIM,), jnp.float32), 'norm2_b': jnp.zeros((DIM,), jnp.float32), 'fc1_w': jax.random.normal(ks[3], (HIDDEN, DIM), jnp.float32) * s, 'fc1_b': jnp.zeros((HIDDEN,), jnp.float32), 'fc2_w': jax.random.normal(ks[4], (DIM, HIDDEN), jnp.float32) * s, 'fc2_b': jnp.zeros((DIM,), jnp.float32)}
    _L0_attn_in = _L0_attn_setup()

    def _L0_ffn_setup():
        import jax, jax.numpy as jnp
        import numpy as np
        NUM_EXPERTS = 8
        HIDDEN = 128
        FFN = 512
        BATCH = 2
        SEQ = 256
        key = jax.random.key(seed)
        k_x, k_g, k_u, k_d = jax.random.split(key, 4)
        scale_in = 1.0 / np.sqrt(HIDDEN)
        scale_mid = 1.0 / np.sqrt(FFN)
        return {'hidden_states': jax.random.normal(k_x, (BATCH, SEQ, HIDDEN), dtype=jnp.float32), 'Wg': jax.random.normal(k_g, (NUM_EXPERTS, HIDDEN, FFN), dtype=jnp.float32) * scale_in, 'Wu': jax.random.normal(k_u, (NUM_EXPERTS, HIDDEN, FFN), dtype=jnp.float32) * scale_in, 'Wd': jax.random.normal(k_d, (NUM_EXPERTS, FFN, HIDDEN), dtype=jnp.float32) * scale_mid}
    _L0_ffn_in = _L0_ffn_setup()
    _L0_c = _w((lambda *s: np.random.randn(*s).astype(np.float32) * 0.05)(8, 128))
    _L0_wmod = _w((lambda *s: np.random.randn(*s).astype(np.float32) * 0.05)(128, 6 * 128) * 128 ** (-0.5))

    def _L1_attn_setup():
        import math
        import jax, jax.numpy as jnp
        import numpy as np
        B, T, D, H = (4, 128, 128, 8)
        HD = D // H

        def _trigram_dirs():
            t = np.array([[(i >> b & 1) * 2 - 1 for b in (2, 1, 0)] for i in range(8)], dtype=np.float32)
            return jnp.asarray(t / np.linalg.norm(t, axis=1, keepdims=True))
        key = jax.random.key(seed)
        k1, k2, k3, k4 = jax.random.split(key, 4)
        x = jax.random.normal(k1, (B, T, D), dtype=jnp.float32)
        Wqkv = jax.random.normal(k2, (D, 3 * D), dtype=jnp.float32) * 0.02
        Wout = jax.random.normal(k3, (D, D), dtype=jnp.float32) * 0.02
        head_scales = jax.random.normal(k4, (H,), dtype=jnp.float32) * 0.1
        head_dirs = _trigram_dirs()
        return {'x': x, 'Wqkv': Wqkv, 'Wout': Wout, 'head_scales': head_scales, 'head_dirs': head_dirs}
    _L1_attn_in = _L1_attn_setup()

    def _L1_ffn_setup():
        import jax, jax.numpy as jnp
        import numpy as np
        B, T, DIM = (2, 256, 128)
        H, DH, E, K = (16, 64, 8, 2)
        key = jax.random.key(seed)
        ks = jax.random.split(key, 7)
        s = 0.02
        return {'x': jax.random.normal(ks[0], (B, T, DIM), jnp.float32), 'Wq': jax.random.normal(ks[1], (H, DH, DIM), jnp.float32) * s, 'Wk': jax.random.normal(ks[2], (H, DH, DIM), jnp.float32) * s, 'Wv': jax.random.normal(ks[3], (E, DH, DIM), jnp.float32) * s, 'Ws': jax.random.normal(ks[4], (H, E, DIM), jnp.float32) * s, 'Wd': jax.random.normal(ks[5], (H, E, DIM), jnp.float32) * s, 'Wo': jax.random.normal(ks[6], (E, DIM, DH), jnp.float32) * s}
    _L1_ffn_in = _L1_ffn_setup()
    _L1_c = _w((lambda *s: np.random.randn(*s).astype(np.float32) * 0.05)(8, 128))
    _L1_wmod = _w((lambda *s: np.random.randn(*s).astype(np.float32) * 0.05)(128, 6 * 128) * 128 ** (-0.5))
    _d = {'L0_attn_x': _L0_attn_in['x'], 'L0_attn_norm1_g': _L0_attn_in['norm1_g'], 'L0_attn_norm1_b': _L0_attn_in['norm1_b'], 'L0_attn_qkv_w': _L0_attn_in['qkv_w'], 'L0_attn_proj_w': _L0_attn_in['proj_w'], 'L0_attn_proj_b': _L0_attn_in['proj_b'], 'L0_attn_norm2_g': _L0_attn_in['norm2_g'], 'L0_attn_norm2_b': _L0_attn_in['norm2_b'], 'L0_attn_fc1_w': _L0_attn_in['fc1_w'], 'L0_attn_fc1_b': _L0_attn_in['fc1_b'], 'L0_attn_fc2_w': _L0_attn_in['fc2_w'], 'L0_attn_fc2_b': _L0_attn_in['fc2_b'], 'L0_ffn_Wg': _L0_ffn_in['Wg'], 'L0_ffn_Wu': _L0_ffn_in['Wu'], 'L0_ffn_Wd': _L0_ffn_in['Wd'], 'L0_c': _L0_c, 'L0_wmod': _L0_wmod, 'L1_attn_Wqkv': _L1_attn_in['Wqkv'], 'L1_attn_Wout': _L1_attn_in['Wout'], 'L1_attn_head_scales': _L1_attn_in['head_scales'], 'L1_attn_head_dirs': _L1_attn_in['head_dirs'], 'L1_ffn_Wq': _L1_ffn_in['Wq'], 'L1_ffn_Wk': _L1_ffn_in['Wk'], 'L1_ffn_Wv': _L1_ffn_in['Wv'], 'L1_ffn_Ws': _L1_ffn_in['Ws'], 'L1_ffn_Wd': _L1_ffn_in['Wd'], 'L1_ffn_Wo': _L1_ffn_in['Wo'], 'L1_c': _L1_c, 'L1_wmod': _L1_wmod}
    _x0 = _d['L0_attn_x']
    _d['L0_attn_x'] = jax.random.normal(jax.random.fold_in(jax.random.key(seed), 1), (8, 512, 128), dtype=_x0.dtype)
    del _x0
    return _d

def reference(L0_attn_x, L0_attn_norm1_g, L0_attn_norm1_b, L0_attn_qkv_w, L0_attn_proj_w, L0_attn_proj_b, L0_attn_norm2_g, L0_attn_norm2_b, L0_attn_fc1_w, L0_attn_fc1_b, L0_attn_fc2_w, L0_attn_fc2_b, L0_ffn_Wg, L0_ffn_Wu, L0_ffn_Wd, L0_c, L0_wmod, L1_attn_Wqkv, L1_attn_Wout, L1_attn_head_scales, L1_attn_head_dirs, L1_ffn_Wq, L1_ffn_Wk, L1_ffn_Wv, L1_ffn_Ws, L1_ffn_Wd, L1_ffn_Wo, L1_c, L1_wmod):

    def _L0_attn_ref(x, norm1_g, norm1_b, qkv_w, proj_w, proj_b, norm2_g, norm2_b, fc1_w, fc1_b, fc2_w, fc2_b):
        import jax, jax.numpy as jnp
        import numpy as np
        DIM = 128
        HEADS = 16
        HIDDEN = 512
        EPS_ATTN = 1e-06
        EPS_LN = 1e-05

        def layer_norm(x, g, b):
            mu = jnp.mean(x, axis=-1, keepdims=True)
            var = jnp.var(x, axis=-1, keepdims=True)
            return (x - mu) * jax.lax.rsqrt(var + EPS_LN) * g + b
        B, N, C = x.shape
        H = HEADS
        d = C // H
        h = layer_norm(x, norm1_g, norm1_b)
        qkv = jnp.einsum('bnc,oc->bno', h, qkv_w)
        qkv = qkv.reshape(B, N, 3, H, d)
        q = jnp.transpose(qkv[:, :, 0], (0, 2, 1, 3))
        k = jnp.transpose(qkv[:, :, 1], (0, 2, 1, 3))
        v = jnp.transpose(qkv[:, :, 2], (0, 2, 1, 3))
        q = jax.nn.elu(q) + 1.0
        k = jax.nn.elu(k) + 1.0
        kv = jnp.einsum('bhnd,bhne->bhde', k, v)
        ksum = jnp.sum(k, axis=2)
        z = 1.0 / (jnp.einsum('bhnd,bhd->bhn', q, ksum) + EPS_ATTN)
        attn_out = jnp.einsum('bhnd,bhde->bhne', q, kv) * z[..., None]
        attn_out = jnp.transpose(attn_out, (0, 2, 1, 3)).reshape(B, N, C)
        attn_out = jnp.einsum('bnc,oc->bno', attn_out, proj_w) + proj_b
        x = x + attn_out
        h = layer_norm(x, norm2_g, norm2_b)
        h = jax.nn.gelu(jnp.einsum('bnc,hc->bnh', h, fc1_w) + fc1_b, approximate=False)
        h = jnp.einsum('bnh,ch->bnc', h, fc2_w) + fc2_b
        return x + h

    def _L0_ffn_ref(hidden_states, Wg, Wu, Wd):
        import jax, jax.numpy as jnp
        import numpy as np
        NUM_EXPERTS = 8
        HIDDEN = 128
        FFN = 512
        BATCH = 2
        SEQ = 256
        B, S, H = hidden_states.shape
        x = hidden_states.reshape(-1, H)

        def expert_step(acc, w):
            wg, wu, wd = w
            h = jax.nn.silu(x @ wg) * (x @ wu)
            return (acc + h @ wd, None)
        acc, _ = jax.lax.scan(expert_step, jnp.zeros_like(x), (Wg, Wu, Wd))
        return acc.reshape(B, S, H)

    def _L1_attn_ref(x, Wqkv, Wout, head_scales, head_dirs):
        import math
        import jax, jax.numpy as jnp
        import numpy as np
        B, T, D, H = (4, 128, 128, 8)
        HD = D // H

        def _trigram_dirs():
            t = np.array([[(i >> b & 1) * 2 - 1 for b in (2, 1, 0)] for i in range(8)], dtype=np.float32)
            return jnp.asarray(t / np.linalg.norm(t, axis=1, keepdims=True))
        b, t, d = x.shape
        scale = 1.0 / math.sqrt(HD)
        qkv = (x @ Wqkv).reshape(b, t, 3, H, HD)
        qkv = jnp.transpose(qkv, (2, 0, 3, 1, 4))
        q, k, v = (qkv[0], qkv[1], qkv[2])
        scores = jnp.einsum('bhqd,bhkd->bhqk', q, k) * scale
        q_proj = jnp.einsum('bhtd,hd->bht', q[..., :3], head_dirs)
        k_proj = jnp.einsum('bhtd,hd->bht', k[..., :3], head_dirs)
        geo_bias = q_proj[..., :, None] * k_proj[..., None, :]
        scores = scores + head_scales[None, :, None, None] * geo_bias
        causal = jnp.tril(jnp.ones((t, t), dtype=bool))
        scores = jnp.where(causal, scores, -jnp.inf)
        attn = jax.nn.softmax(scores, axis=-1)
        out = jnp.einsum('bhqk,bhkd->bhqd', attn, v)
        out = jnp.transpose(out, (0, 2, 1, 3)).reshape(b, t, d)
        return out @ Wout

    def _L1_ffn_ref(x, Wq, Wk, Wv, Ws, Wd, Wo):
        import jax, jax.numpy as jnp
        import numpy as np
        B, T, DIM = (2, 256, 128)
        H, DH, E, K = (16, 64, 8, 2)
        scale = DH ** (-0.5)
        q = jnp.einsum('btc,hdc->bhtd', x, Wq)
        k = jnp.einsum('btc,hdc->bhtd', x, Wk)
        gate_v = jnp.einsum('btc,hec->bthe', x, Ws)
        w, sel = jax.lax.top_k(gate_v, K)
        wsig = jax.nn.sigmoid(w)
        oh = jax.nn.one_hot(sel, E, dtype=x.dtype)
        mix_v = jnp.einsum('bthk,bthke->bthe', wsig, oh)
        proj_v = jnp.einsum('btc,edc->bted', x, Wv)
        v = jnp.einsum('bthe,bted->bhtd', mix_v, proj_v)
        scores = jnp.einsum('bhid,bhjd->bhij', q * scale, k)
        probs = jax.nn.softmax(scores, axis=-1)
        attn = jnp.einsum('bhij,bhjd->bihd', probs, v)
        gate_o = jnp.einsum('btc,hec->bthe', x, Wd)
        _, sel_o = jax.lax.top_k(gate_o, K)
        mask_o = jax.nn.one_hot(sel_o, E, dtype=x.dtype).sum(axis=3)
        res = jnp.einsum('bthe,bthd,efd->bthf', mask_o, attn, Wo)
        return res.sum(axis=2)
    x = L0_attn_x
    mod = (_silu(L0_c) @ L0_wmod).reshape(L0_c.shape[0], 6, 1, -1)
    sa, ca, ga, sb, cb, gb = (mod[:, 0], mod[:, 1], mod[:, 2], mod[:, 3], mod[:, 4], mod[:, 5])
    ga = (2 * (ga >= 0) - 1) * jnp.maximum(jnp.abs(ga), 0.25)
    gb = (2 * (gb >= 0) - 1) * jnp.maximum(jnp.abs(gb), 0.25)
    h = _layernorm(x, axis=-1) * (1 + ca) + sa
    x = x + ga * _L0_attn_ref(h, L0_attn_norm1_g, L0_attn_norm1_b, L0_attn_qkv_w, L0_attn_proj_w, L0_attn_proj_b, L0_attn_norm2_g, L0_attn_norm2_b, L0_attn_fc1_w, L0_attn_fc1_b, L0_attn_fc2_w, L0_attn_fc2_b)
    h = _layernorm(x, axis=-1) * (1 + cb) + sb
    x = x + gb * _L0_ffn_ref(h, L0_ffn_Wg, L0_ffn_Wu, L0_ffn_Wd)
    mod = (_silu(L1_c) @ L1_wmod).reshape(L1_c.shape[0], 6, 1, -1)
    sa, ca, ga, sb, cb, gb = (mod[:, 0], mod[:, 1], mod[:, 2], mod[:, 3], mod[:, 4], mod[:, 5])
    ga = (2 * (ga >= 0) - 1) * jnp.maximum(jnp.abs(ga), 0.25)
    gb = (2 * (gb >= 0) - 1) * jnp.maximum(jnp.abs(gb), 0.25)
    h = _layernorm(x, axis=-1) * (1 + ca) + sa
    x = x + ga * _L1_attn_ref(h, L1_attn_Wqkv, L1_attn_Wout, L1_attn_head_scales, L1_attn_head_dirs)
    h = _layernorm(x, axis=-1) * (1 + cb) + sb
    x = x + gb * _L1_ffn_ref(h, L1_ffn_Wq, L1_ffn_Wk, L1_ffn_Wv, L1_ffn_Ws, L1_ffn_Wd, L1_ffn_Wo)
    return x

_drawn_inputs = setup_inputs


def setup_inputs(seed=0):
    import zlib

    import numpy as np

    out = dict(_drawn_inputs(seed))
    spreads = {'L0_attn_norm1_g': (1.0, 0.6),
     'L0_attn_norm1_b': (0.0, 0.8),
     'L0_attn_proj_b': (0.0, 0.279),
     'L0_attn_norm2_g': (1.0, 0.6),
     'L0_attn_norm2_b': (0.0, 0.8),
     'L0_attn_fc1_b': (0.0, 0.8),
     'L0_attn_fc2_b': (0.0, 0.286)}
    factors = {'L0_attn_qkv_w': 8.0,
     'L0_attn_proj_w': 8.0,
     'L0_attn_fc1_w': 3.7,
     'L0_attn_fc2_w': 3.441,
     'L1_attn_Wqkv': 8.0,
     'L1_attn_Wout': 8.0,
     'L1_attn_head_scales': 8.0,
     'L1_attn_head_dirs': 8.0,
     'L1_ffn_Wq': 8.0,
     'L1_ffn_Wk': 8.0,
     'L1_ffn_Wv': 8.0,
     'L1_ffn_Ws': 8.0,
     'L1_ffn_Wd': 8.0,
     'L1_ffn_Wo': 8.0,
     'L1_c': 8.0,
     'L1_wmod': 8.0}
    for name, (base, spread) in spreads.items():
        noise = np.random.default_rng([zlib.crc32(name.encode()), seed]).standard_normal(out[name].shape)
        drawn = base * np.exp(spread * noise) if base else spread * noise
        out[name] = jnp.asarray(drawn.astype(out[name].dtype))
    for name, factor in factors.items():
        out[name] = (out[name] * factor).astype(out[name].dtype)
    return out
```

```python
from contextlib import ExitStack

import concourse.bass as bass
from concourse import mybir

F32 = mybir.dt.float32
BF16 = mybir.dt.bfloat16
ALU = mybir.AluOpType
ACT = mybir.ActivationFunctionType
X_AXIS = mybir.AxisListType.X

P = 128
NB = 8
T = 512
NT = T // P
H0, D0 = 16, 8
NJ = 4
NE = 8
H1, D1 = 8, 16
HS, DS = 16, 64
NP = HS // 2
VW = DS + 1
NQ = 8
GROUP = 4
NG = HS // GROUP
MIXED_AT = 10
EPS_LN, EPS_ATTN = 1e-5, 1e-6
BIG = 3.0e38
MASKED = -1.0e30
SA0, CA0, GA0, SB0, CB0, GB0, SA1, CA1, GA1, SB1, CB1, GB1 = range(12)
LNS = 6
PER = {}


def build(nc, a, row_table, out):
    ctx = ExitStack()
    with ctx:
        def sb(name, shape, dt=F32):
            return ctx.enter_context(nc.sbuf_tensor(name, shape, dt))

        def sem(name, per=0):
            s = ctx.enter_context(nc.semaphore(name))
            PER[name] = per
            return s, per

        ident = sb("ident", [P, P])
        ident_bf = sb("ident_bf", [P, P], BF16)
        causal_bf = sb("causal_bf", [P, P], BF16)
        block8 = sb("block8", [P, P])
        block16 = sb("block16", [P, P])
        head_of8 = sb("head_of8", [P, H0])
        head_of16 = sb("head_of16", [P, H1])
        ones_row = sb("ones_row", [1, P])
        first_wins = sb("first_wins", [P, NE])
        minus_half = sb("minus_half", [P, NT])
        qkvT = sb("qkvT", [P, 3 * P])
        projT = sb("projT", [P, P])
        fc1T = sb("fc1T", [P, T])
        fc2T = sb("fc2T", [P, NJ, P])
        proj_b_row = sb("proj_b_row", [1, NT, P])
        cols = sb("cols", [P, 9])
        Wg = sb("Wg", [P, NE, T])
        Wu = sb("Wu", [P, NE, T])
        Wd = sb("Wd", [P, NE, NJ, P])
        W1 = sb("W1", [P, 3 * P])
        Wout = sb("Wout", [P, P])
        WqT = sb("WqT", [P, HS * DS])
        WkT = sb("WkT", [P, HS * DS])
        WvT = sb("WvT", [P, NE * DS])
        gatesT = sb("gatesT", [P, 2 * P])
        WoT = sb("WoT", [P, NJ, P])
        mod = sb("mod", [P, NB, 12])
        rows0 = sb("rows0", [P, 3, P])
        rows1a = sb("rows1a", [P, P])
        rows1b = sb("rows1b", [P, P])

        HQ = HS // NQ

        xin = sb("xin", [P, NT, P])
        nrm = sb("nrm", [P, NT, P])
        stats = sb("stats", [P, NT, 6])
        mv = sb("mv", [P, NT, 2])
        pause = sb("pause", [P, 1])
        vareps = sb("vareps", [P, NT])
        rstd = sb("rstd", [P, NT])
        modA = sb("modA", [P, 12])
        modB = sb("modB", [P, 12])
        arena = sb("arena", [P, 6144])

        def part(at, shape):
            n = 1
            for x in shape:
                n *= x
            names = "abcd"[:len(shape)]
            v = arena[:, at:at + n]
            return v if len(shape) == 1 else v.rearrange(f"p ({' '.join(names)}) -> p {' '.join(names)}", **dict(zip(names, shape)))

        h0m = part(0, [NT, P])
        h0 = sb("h0", [P, NT, P])
        h1T = sb("h1T", [P, T])
        qmin = part(512, [T])
        qexp = part(1024, [T])
        qe = part(1536, [T])
        kmin = part(2048, [NT, P])
        kexp = part(2560, [NT, P])
        ke = part(3072, [NT, P])
        v0 = sb("v0", [P, NT, P + 1])
        kv = sb("kv", [P, P + H0])
        den0 = sb("den0", [P, NT, H0])
        rden0 = sb("rden0", [P, NT, H0])
        att = sb("att", [P, NT, P])
        attT = sb("attT", [P, T])
        x2 = h0
        x2g = h0m
        xg = xin
        hid = part(3584, [NJ, T])
        yS = nrm[:, :, :].rearrange("p i c -> p (i c)")
        x3 = sb("x3", [P, NT, P])
        silu = part(0, [2, T])
        act = part(1024, [2, T])
        x4 = x3
        q1T = attT
        k1T = att[:, :, :].rearrange("p i c -> p (i c)")
        k1z = part(0, [H1, T])
        v1 = sb("v1", [P, NT, H1, D1 + 1])
        nmax1 = sb("nmax1", [P, 2])
        p1 = part(4096, [2, T])
        p1T = part(5120, [2, T])
        o1 = sb("o1", [P, NT, H1, D1 + 1])
        rden1 = sb("rden1", [P, NT, H1])
        WoutG = sb("WoutG", [P, P])
        x5 = sb("x5", [P, NT, P])
        hdT = sb("hdT", [P, T])
        gate = part(0, [2, NT, HS, NE])
        eq = part(1024, [2 * NT * HS, NE])
        cand = part(2048, [2 * NT * HS, NE])
        oh1 = part(3072, [2 * NT * HS, NE])
        oh2 = part(4096, [2 * NT * HS, NE])
        top = sb("top", [P, 2, 2 * NT * HS])
        pick = sb("pick", [P, 2 * NT * HS])
        sigd = sb("sigd", [P, 2, NT * HS])
        sig = sb("sig", [P, 2, NT * HS])
        mixv = sb("mixv", [P, NT, HS, NE])
        masko = sb("masko", [P, NT, HS, NE])
        pv = sb("pv", [P, 2, NE * DS])
        prod = sb("prod", [P, 2, HS * NE * DS // NQ])
        vals = sb("vals", [P, NT, HS, VW])
        qsT = sb("qsT", [P, 2, NP, P])
        ksT = sb("ksT", [P, NP, T])
        nmax = sb("nmax", [P, 2])
        pr = sb("pr", [P, 2, T])
        prT = sb("prT", [P, 2, T])
        oa = sb("oa", [P, 2, HS, VW])
        rden = sb("rden", [P, 2, HS])
        coef = sb("coef", [P, 2, HS, NE])
        ym = sb("ym", [P, NE * DS])
        ymT = sb("ymT", [P, NJ, P])
        resg = sb("resg", [P, P])
        xout = x5

        bank = [ctx.enter_context(nc.psum_tensor(f"bank{i}", [P, T], F32)) for i in range(8)]
        F0, F1, F2, F3, S0, S1, TB, OB = bank

        def tiles(t):
            return t[:, :].rearrange("p (i c) -> p i c", i=NT)

        def wait(eng, s, b, k):
            if not (isinstance(b, int) and b * s[1] + k == 0):
                eng.wait_ge(s[0], b * s[1] + k)

        small_in = sem("small_in")
        raw_in = sem("raw_in")
        experts_in = sem("experts_in")
        const_g = sem("const_g")
        const_v = sem("const_v")
        setup_pe = sem("setup_pe")
        setup_v = sem("setup_v")
        setup_a = sem("setup_a")
        setup_done = sem("setup_done")

        x_in = sem("x_in", 32)
        rows1a_in = sem("rows1a_in", 16)
        rows1b_in = sem("rows1b_in", 16)
        table_out = sem("table_out")
        ln_stats = sem("ln_stats", LNS)
        ln_mv = sem("ln_mv", LNS)
        ln_eps = sem("ln_eps", LNS)
        ln_rstd = sem("ln_rstd", LNS)
        ln_n = sem("ln_n", LNS)
        ln_T = sem("ln_T", 5)
        ln_evac = sem("ln_evac", 5)
        modA_r = sem("modA_r", 1)
        modB_r = sem("modB_r", 1)
        h0m_r = sem("h0m_r", 1)
        h0_r = sem("h0_r", 1)
        qkv0_r = sem("qkv0_r", 3)
        emin_r = sem("emin_r", 3)
        eexp_r = sem("eexp_r", 3)
        elu_r = sem("elu_r", 3)
        v0_r = sem("v0_r", 2)
        kv_ps = sem("kv_ps", 1)
        kv_r = sem("kv_r", 1)
        num_ps = sem("num_ps", 2)
        den0_r = sem("den0_r", 1)
        rden0_r = sem("rden0_r", 1)
        att0_r = sem("att0_r", 1)
        att0_T = sem("att0_T", 1)
        attT0_r = sem("attT0_r", 1)
        proj_ps = sem("proj_ps", 1)
        x2_r = sem("x2_r", 1)
        fc1_ps = sem("fc1_ps", NJ)
        hid_r = sem("hid_r", NJ)
        fc2_ps = sem("fc2_ps", 1)
        y0_r = sem("y0_r", 1)
        y0_T = sem("y0_T", 1)
        x2g_r = sem("x2g_r", 1)
        xg_r = sem("xg_r", 1)
        x3_r = sem("x3_r", 1)
        gu_g = sem("gu_g", NE * NJ)
        gu_u = sem("gu_u", NE * NJ)
        silu_r = sem("silu_r", NE * NJ)
        act_r = sem("act_r", NE * NJ)
        down_ps = sem("down_ps", NE * NJ)
        y1_r = sem("y1_r", 1)
        y1_T = sem("y1_T", 1)
        x4_r = sem("x4_r", 1)
        qkv1_ps = sem("qkv1_ps", 3)
        q1_r = sem("q1_r", 1)
        k1_r = sem("k1_r", 1)
        v1_r = sem("v1_r", 1)
        k1z_r = sem("k1z_r", H1)
        N1 = NT * H1
        s1_ps = sem("s1_ps", N1)
        nmax1_r = sem("nmax1_r", N1)
        p1_r = sem("p1_r", N1)
        p1_T = sem("p1_T", N1)
        p1T_r = sem("p1T_r", N1)
        o1_ps = sem("o1_ps", NT)
        o1_r = sem("o1_r", NT)
        rden1_r = sem("rden1_r", 1)
        att1_r = sem("att1_r", 1)
        att1_T = sem("att1_T", 1)
        attT1_r = sem("attT1_r", 1)
        WoutG_r = sem("WoutG_r", 1)
        out1_ps = sem("out1_ps", 1)
        x5_r = sem("x5_r", 1)
        gate_ps = sem("gate_ps", 2)
        gate_r = sem("gate_r", 2)
        topk_v = sem("topk_v", 9)
        topk_g = sem("topk_g", 2)
        sig_e = sem("sig_e", 1)
        sig_v = sem("sig_v", 2)
        mix_g = sem("mix_g", 3)
        masko_r = sem("masko_r", 1)
        pv_ps = sem("pv_ps", NT)
        pv_r = sem("pv_r", NT)
        vprod_r = sem("vprod_r", NQ * NT)
        vals_r = sem("vals_r", NQ * NT)
        k_ps = sem("k_ps", NP)
        q_ps = sem("q_ps", 2 * NT)
        qs_r = sem("qs_r", 2 * NT)
        ks_r = sem("ks_r", NP)
        N2 = NT * HS
        s_ps = sem("s_ps", N2)
        nmax_r = sem("nmax_r", N2)
        p_r = sem("p_r", N2)
        p_T = sem("p_T", N2)
        pT_r = sem("pT_r", N2)
        o_ps = sem("o_ps", NT * NG)
        oa_r = sem("oa_r", NT * NG)
        rden_r = sem("rden_r", NT)
        coef_r = sem("coef_r", NT)
        oprod_r = sem("oprod_r", NQ * NT)
        ym_r = sem("ym_r", NQ * NT)
        ym_T = sem("ym_T", NT)
        ymT_r = sem("ymT_r", NT)
        res_ps = sem("res_ps", NT)
        resg_r = sem("resg_r", NT)
        xout_r = sem("xout_r", NT)
        stored = sem("stored", 16)

        block = ctx.enter_context(nc.Block())

        raw_qkv = part(0, [3, P])
        raw_proj = part(384, [P])
        raw_fc1 = part(512, [4, P])
        raw_fc2 = part(1024, [4, P])
        raw_wq = part(1536, [8, P])
        raw_wk = part(2560, [8, P])
        raw_wv = part(3584, [4, P])
        raw_wo = part(4096, [4, P])
        raw_gates = xin[:, 0:2, :]
        wmod = [ksT[:, 0:2, :].rearrange("p a c -> p (a c)")[:, 0:768],
                ksT[:, 2:4, :].rearrange("p a c -> p (a c)")[:, 0:768]]
        crow = [ksT[0:NB, 4, 0:P], ksT[0:NB, 5, 0:P]]
        cexp = [ksT[0:NB, 4, P:2 * P], ksT[0:NB, 5, P:2 * P]]
        crec = [ksT[0:NB, 4, 2 * P:3 * P], ksT[0:NB, 5, 2 * P:3 * P]]
        csil = [ksT[0:NB, 4, 3 * P:4 * P], ksT[0:NB, 5, 3 * P:4 * P]]
        cT = [ksT[:, 6, 0:NB], ksT[:, 6, NB:2 * NB]]
        col_rows = ksT[0:9, 6, P:2 * P]
        dirs = ksT[0:1, 7, 0:P]
        sdirs = ksT[0:1, 7, P:2 * P]
        scales = ksT[0:1, 7, 2 * P:2 * P + H1]
        wq1T = xin[:, 2, :]
        bias_m = xin[:, 3, :]
        sgn = nrm[:, 0, 0:NB]
        gab = nrm[:, 1, 0:NB]
        rtab = part(5120, [5, P])[0:NB]
        rsgn = part(5760, [P])[0:NB]
        rabs = part(5888, [P])[0:NB]
        wq1 = W1[:, 0:P]

        turns = ([(raw_qkv[:, i, :], qkvT[:, i * P:(i + 1) * P]) for i in range(3)]
                 + [(raw_proj, projT[:, :])]
                 + [(raw_fc1[:, i, :], fc1T[:, i * P:(i + 1) * P]) for i in range(4)]
                 + [(raw_fc2[:, i, :], fc2T[:, i, :]) for i in range(4)]
                 + [(raw_wq[:, i, :], WqT[:, i * P:(i + 1) * P]) for i in range(8)]
                 + [(raw_wk[:, i, :], WkT[:, i * P:(i + 1) * P]) for i in range(8)]
                 + [(raw_wv[:, i, :], WvT[:, i * P:(i + 1) * P]) for i in range(4)]
                 + [(raw_wo[:, i, :], WoT[:, i, :]) for i in range(4)]
                 + [(raw_gates[:, i, :], gatesT[:, i * P:(i + 1) * P]) for i in range(2)]
                 + [(wq1, wq1T)])
        NTURN = len(turns)

        def run(steps, b):
            for name in ORDER:
                if name in steps:
                    steps[name](b)

        ORDER = (["load", "attn0", "moe_in", "experts", "attn1", "gates", "values", "qk", "heads"])

        def loop(eng, steps):
            run(steps, 0)
            with eng.Fori(1, NB) as b:
                run(steps, b)

        @block.sync
        def _(sp):
            for row, src in ((0, a["L0_attn_norm1_g"]), (1, a["L0_attn_norm1_b"]), (2, a["L0_attn_norm2_g"]),
                             (3, a["L0_attn_norm2_b"]), (8, a["L0_attn_fc2_b"])):
                sp.dma_start(col_rows[row:row + 1, :], src.rearrange("(o p) -> o p", o=1)).then_inc(small_in[0], 16)
            sp.dma_start(col_rows[4:8, :], a["L0_attn_fc1_b"].rearrange("(j p) -> j p", p=P)).then_inc(small_in[0], 16)
            for i in range(NT):
                sp.dma_start(proj_b_row[:, i, :], a["L0_attn_proj_b"].rearrange("(o p) -> o p", o=1)).then_inc(small_in[0], 16)
            sp.dma_start(crow[0], a["L0_c"]).then_inc(small_in[0], 16)
            sp.dma_start(crow[1], a["L1_c"]).then_inc(small_in[0], 16)
            sp.dma_start(scales, a["L1_attn_head_scales"].rearrange("(o h) -> o h", o=1)).then_inc(small_in[0], 16)
            sp.wait_ge(const_g[0], 3)
            sp.dma_start(dirs.rearrange("o (h d) -> o h d", h=H1)[:, :, 0:3],
                         a["L1_attn_head_dirs"].rearrange("(o h) d -> o h d", o=1)).then_inc(small_in[0], 16)
            sp.dma_start(wmod[0], a["L0_wmod"]).then_inc(small_in[0], 16)
            sp.dma_start(wmod[1], a["L1_wmod"]).then_inc(small_in[0], 16)
            sp.dma_start(raw_qkv, a["L0_attn_qkv_w"].rearrange("(i p) c -> p i c", p=P)).then_inc(raw_in[0], 16)
            sp.dma_start(raw_proj, a["L0_attn_proj_w"]).then_inc(raw_in[0], 16)
            sp.dma_start(raw_fc1, a["L0_attn_fc1_w"].rearrange("(i p) c -> p i c", p=P)).then_inc(raw_in[0], 16)
            sp.dma_start(raw_fc2, a["L0_attn_fc2_w"].rearrange("p (i c) -> p i c", c=P)).then_inc(raw_in[0], 16)
            sp.dma_start(raw_wq, a["L1_ffn_Wq"].rearrange("(i a) d c -> (a d) i c", a=2)).then_inc(raw_in[0], 16)
            sp.dma_start(raw_wk, a["L1_ffn_Wk"].rearrange("(i a) d c -> (a d) i c", a=2)).then_inc(raw_in[0], 16)
            sp.dma_start(raw_wv, a["L1_ffn_Wv"].rearrange("(i a) d c -> (a d) i c", a=2)).then_inc(raw_in[0], 16)
            sp.dma_start(raw_wo.rearrange("p i (a d) -> p (i a) d", a=2), a["L1_ffn_Wo"].rearrange("e f d -> f e d")).then_inc(raw_in[0], 16)
            sp.dma_start(raw_gates[:, 0, :], a["L1_ffn_Ws"].rearrange("h e c -> (h e) c")).then_inc(raw_in[0], 16)
            sp.dma_start(raw_gates[:, 1, :], a["L1_ffn_Wd"].rearrange("h e c -> (h e) c")).then_inc(raw_in[0], 16)
            sp.dma_start(W1[:, :], a["L1_attn_Wqkv"]).then_inc(raw_in[0], 16)
            sp.dma_start(Wout[:, :], a["L1_attn_Wout"]).then_inc(raw_in[0], 16)
            sp.dma_start(Wg[:, :, :], a["L0_ffn_Wg"].rearrange("e c f -> c e f")).then_inc(experts_in[0], 16)
            sp.dma_start(Wu[:, :, :], a["L0_ffn_Wu"].rearrange("e c f -> c e f")).then_inc(experts_in[0], 16)
            sp.dma_start(Wd[:, :, :, :], a["L0_ffn_Wd"].rearrange("e (j p) c -> p e j c", p=P)).then_inc(experts_in[0], 16)
            sp.wait_ge(setup_done[0], 1)
            sp.dma_start(row_table, rtab.rearrange("b m c -> b (m c)")).then_inc(table_out[0], 16)
            sp.wait_ge(table_out[0], 16)

            def load(b):
                wait(sp, x3_r, b, 0)
                sp.dma_start(xin[:, :, :], a["L0_attn_x"][bass.ds(b, 1), :, :].rearrange("o (i p) c -> p (o i) c", p=P)).then_inc(x_in[0], 16)

                sp.dma_start(rows0[:, :, :].rearrange("p m c -> p (m c)"), row_table[bass.ds(b, 1), 0:3 * P].to_broadcast([P, 3 * P])).then_inc(x_in[0], 16)
                wait(sp, WoutG_r, b, 0)
                sp.dma_start(rows1a[:, :], row_table[bass.ds(b, 1), 3 * P:4 * P].to_broadcast([P, P])).then_inc(rows1a_in[0], 16)
                wait(sp, xout_r, b, 0)
                sp.dma_start(rows1b[:, :], row_table[bass.ds(b, 1), 4 * P:5 * P].to_broadcast([P, P])).then_inc(rows1b_in[0], 16)

            def heads(b):
                wait(sp, xout_r, b, NT)
                sp.dma_start(out[bass.ds(b, 1), :, :].rearrange("o (i p) c -> p (o i) c", p=P), xout[:, :, :]).then_inc(stored[0], 16)

            loop(sp, {"load": load, "heads": heads})
            sp.wait_ge(stored[0], 16 * NB)

        @block.gpsimd
        def _(g):
            g.memset(ident[:, :], 0.0)
            g.memset(dirs, 0.0)
            g.memset(block8[:, :], 1.0)
            g.memset(block16[:, :], 1.0)
            g.memset(head_of8[:, :], 1.0)
            g.memset(head_of16[:, :], 1.0)
            g.memset(causal_bf[:, :], 0.0)
            g.memset(ones_row[:, :], 1.0)
            g.memset(minus_half[:, :], -0.5)
            g.memset(v0[:, :, P:P + 1], 1.0)
            g.memset(v1[:, :, :, D1:D1 + 1], 1.0)
            g.memset(vals[:, :, :, DS:DS + 1], 1.0)
            for e in range(NE):
                g.memset(first_wins[:, e:e + 1], float(NE - e))
            g.memset(nmax[:, :], 0.0).then_inc(const_g[0], 3)
            g.wait_ge(const_g[0], 3)
            g.affine_select(out=ident[:, :], in_=ident[:, :], compare_op=ALU.not_equal, fill=1.0, base=0,
                            pattern=[[-1, P]], channel_multiplier=1)
            g.affine_select(out=causal_bf[:, :], in_=causal_bf[:, :], compare_op=ALU.is_ge, fill=MASKED, base=0,
                            pattern=[[-1, P]], channel_multiplier=1)

            def cut(tile, n, size, inner, k):
                view = tile[:, :].rearrange("p (n s) -> p n s", n=n)
                g.affine_select(out=view, in_=view, compare_op=ALU.is_ge, fill=0.0, base=0,
                                pattern=[[-size, n], [0, inner]], channel_multiplier=1).then_inc(const_g[0], 1)
                g.wait_ge(const_g[0], k)
                g.affine_select(out=view, in_=view, compare_op=ALU.is_ge, fill=0.0, base=size - 1,
                                pattern=[[size, n], [0, inner]], channel_multiplier=-1).then_inc(const_g[0], 1)

            cut(block8, H0, D0, D0, 4)
            cut(block16, H1, D1, D1, 6)
            cut(head_of8, H0, D0, 1, 8)
            cut(head_of16, H1, D1, 1, 10)
            g.wait_ge(const_g[0], 11)
            g.tensor_copy(ident_bf[:, :], ident[:, :]).then_inc(const_g[0], 1)
            g.wait_ge(setup_done[0], 1)

            def rstd_of(b, n):
                wait(g, ln_eps, b, n + 1)
                g.tensor_tensor(rstd[:, :], vareps[:, :], minus_half[:, :], ALU.pow).then_inc(ln_rstd[0], 1)

            def attn0(b):
                rstd_of(b, 0)
                rstd_of(b, 1)
                wait(g, x2_r, b, 1)
                g.tensor_tensor(x2g[:, :, :], x2[:, :, :], rows0[:, 2:3, :].to_broadcast([P, NT, P]), ALU.mult).then_inc(x2g_r[0], 1)
                wait(g, x2g_r, b, 1)
                wait(g, x_in, b, 32)
                g.tensor_tensor(xg[:, :, :], x2g[:, :, :], xin[:, :, :], ALU.add).then_inc(xg_r[0], 1)
                rstd_of(b, 2)

            def moe_in(b):
                rstd_of(b, 3)

            def attn1(b):
                rstd_of(b, 4)
                wait(g, k1_r, b, 1)
                wait(g, s1_ps, b, 0)
                wait(g, rows1a_in, b, 16)
                wait(g, out1_ps, b, 0)
                g.tensor_tensor(WoutG[:, :], Wout[:, :], rows1a[:, :], ALU.mult).then_inc(WoutG_r[0], 1)
                for h in range(H1):
                    g.tensor_scalar(k1z[:, h, :], k1T, head_of16[:, h:h + 1], None, ALU.mult).then_inc(k1z_r[0], 1)
                rstd_of(b, 5)

            def gates(b):
                for r in range(2):
                    wait(g, topk_v, b, 2 + 5 * r)
                    g.tensor_tensor(cand[:, :, :], eq[:, :, :], first_wins[:, :].unsqueeze(1).to_broadcast([P, 2 * NT * HS, NE]), ALU.mult).then_inc(topk_g[0], 1)
                wait(g, sig_v, b, 2)
                wait(g, topk_v, b, 9)
                half = NT * HS
                o1h = oh1[:, 0:half, :]
                o2h = oh2[:, 0:half, :]
                mixf = mixv[:, :, :, :].rearrange("p i h e -> p (i h) e")
                w1 = cand[:, 0:half, :]
                w2 = cand[:, half:2 * half, :]
                g.tensor_tensor(w1, o1h, sig[:, 0, :].unsqueeze(2).to_broadcast([P, half, NE]), ALU.mult).then_inc(mix_g[0], 1)
                g.tensor_tensor(w2, o2h, sig[:, 1, :].unsqueeze(2).to_broadcast([P, half, NE]), ALU.mult).then_inc(mix_g[0], 1)
                wait(g, mix_g, b, 2)
                g.tensor_tensor(mixf, w1, w2, ALU.add).then_inc(mix_g[0], 1)

            def values(b):
                wait(g, mix_g, b, 3)
                wait(g, ym_r, b, 0)
                for i in range(NT):
                    wait(g, pv_r, b, i + 1)
                    for q in range(NQ):
                        n = NQ * i + q
                        if n >= 2:
                            wait(g, vals_r, b, n - 1)
                        o = prod[:, n % 2, :].rearrange("p (h d e) -> p h d e", h=HS // NQ, e=NE)
                        x0 = pv[:, i % 2, :].rearrange("p (e d) -> p d e", e=NE).unsqueeze(1).to_broadcast([P, HS // NQ, DS, NE])
                        x1 = mixv[:, i, HQ * q:HQ * q + HQ, :].unsqueeze(2).to_broadcast([P, HQ, DS, NE])
                        g.tensor_tensor(o, x0, x1, ALU.mult).then_inc(vprod_r[0], 1)

            def heads(b):
                wait(g, vals_r, b, NQ * NT)
                wait(g, masko_r, b, 1)
                for i in range(NT):
                    wait(g, rden_r, b, i + 1)
                    g.tensor_tensor(coef[:, i % 2, :, :], masko[:, i, :, :], rden[:, i % 2, :].unsqueeze(2).to_broadcast([P, HS, NE]), ALU.mult).then_inc(coef_r[0], 1)
                    wait(g, coef_r, b, i + 1)
                    for q in range(NQ):
                        n = NQ * i + q
                        if n >= 2:
                            wait(g, ym_r, b, n - 1)
                        o = prod[:, n % 2, :].rearrange("p (d h) -> p d h", h=HS)
                        x0 = oa[:, i % 2, :, 0:DS].rearrange("p h d -> p d h")
                        x1 = coef[:, i % 2, :, q].unsqueeze(1).to_broadcast([P, DS, HS])
                        g.tensor_tensor(o, x0, x1, ALU.mult).then_inc(oprod_r[0], 1)

            loop(g, {"attn0": attn0, "moe_in": moe_in, "attn1": attn1, "gates": gates, "values": values, "heads": heads})

        @block.tensor
        def _(pe):
            def transposes(dst, src, src_tiles=NT):
                for i in range(src_tiles):
                    last = pe.transpose(dst[:, i * P:(i + 1) * P], src(i), ident[:, :])
                return last

            pe.wait_ge(const_g[0], 12)
            pe.wait_ge(raw_in[0], 16 * 12)
            for n in range((NTURN + 3) // 4):
                part = turns[4 * n:4 * n + 4]
                if n >= 2:
                    pe.wait_ge(setup_v[0], n - 1)
                for i, (src, _) in enumerate(part):
                    last = pe.transpose(bank[n % 2][:, i * P:(i + 1) * P], src, ident[:, :])
                last.then_inc(setup_pe[0], 1)
            n = (NTURN + 3) // 4
            pe.wait_ge(const_v[0], 9)
            pe.wait_ge(small_in[0], 16 * 16)
            for l in range(2):
                pe.transpose(bank[2][:, 8 * l:8 * l + 8], csil[l], ident[0:NB, 0:NB])
            pe.transpose(bank[2][:, 2 * NB:2 * NB + 9], col_rows, ident[0:9, 0:9])
            pe.matmul(bank[3][:, 0:P], sdirs, dirs, start=True, stop=True).then_inc(setup_pe[0], 1)
            pe.wait_ge(setup_v[0], n + 2)
            for l in range(2):
                for m in range(6):
                    last = pe.matmul(bank[4][:, 48 * l + 8 * m:48 * l + 8 * m + 8], wmod[l][:, m * P:(m + 1) * P], cT[l], start=True, stop=True)
            last.then_inc(setup_pe[0], 1)
            pe.matmul(bank[5][:, 0:P], wq1T, bias_m, start=True, stop=True).then_inc(setup_pe[0], 1)
            pe.matmul(bank[6][0:NB, 0:3 * P], cT[0], wmod[0][:, 0:3 * P], start=True, stop=True)
            pe.matmul(bank[7][0:NB, 0:P], cT[1], wmod[1][:, 2 * P:3 * P], start=True, stop=True)
            pe.matmul(bank[7][0:NB, P:2 * P], cT[1], wmod[1][:, 5 * P:6 * P], start=True, stop=True).then_inc(setup_pe[0], 1)
            pe.wait_ge(setup_done[0], 1)
            pe.wait_ge(experts_in[0], 48)

            def ln_turn(b, n, dst):
                wait(pe, ln_n, b, n + 1)
                transposes(dst, lambda i: nrm[:, i, :]).then_inc(ln_T[0], 1)

            def attn0(b):
                wait(pe, oa_r, b, 0)
                ln_turn(b, 1, F0)
                wait(pe, ln_evac, b, 1)
                pe.matmul(F1[:, :], qkvT[:, 0:P], h1T[:, :], start=True, stop=True).then_inc(qkv0_r[0], 1)
                for k, f in enumerate((F2, F3)):
                    for i in range(2):
                        t = 2 * k + i
                        last = pe.matmul(f[:, i * 256:(i + 1) * 256], h1T[:, t * P:(t + 1) * P], qkvT[:, P:3 * P], start=True, stop=True)
                    last.then_inc(qkv0_r[0], 1)
                wait(pe, elu_r, b, 3)
                wait(pe, v0_r, b, 2)
                for i in range(NT):
                    last = pe.matmul(F0[:, 0:P + 1], ke[:, i, :], v0[:, i, :], start=(i == 0), stop=(i == NT - 1))
                last.then_inc(kv_ps[0], 1)
                wait(pe, kv_r, b, 1)
                for k, f in enumerate((F2, F3)):
                    for i in range(2):
                        t = 2 * k + i
                        last = pe.matmul(f[:, i * 256:i * 256 + P + H0], qe[:, t * P:(t + 1) * P], kv[:, :], start=True, stop=True)
                    last.then_inc(num_ps[0], 1)
                wait(pe, att0_r, b, 1)
                transposes(F1, lambda i: att[:, i, :]).then_inc(att0_T[0], 1)
                pe.matmul(F0[:, :], ones_row[:, :], proj_b_row[:, :, :].rearrange("o i c -> o (i c)"), start=True, stop=False, skip_group_check=True)
                wait(pe, attT0_r, b, 1)
                for i in range(NT):
                    last = pe.matmul(F0[:, i * P:(i + 1) * P], attT[:, i * P:(i + 1) * P], projT[:, :], start=False, stop=(i == NT - 1), skip_group_check=True)
                last.then_inc(proj_ps[0], 1)
                ln_turn(b, 2, F1)
                wait(pe, ln_evac, b, 2)
                for j in range(NJ + 1):
                    if j < NJ:
                        if j >= 2:
                            wait(pe, hid_r, b, j - 1)
                        pe.matmul((F2, F3)[j % 2][:, :], fc1T[:, j * P:(j + 1) * P], h2T[:, :], start=True, stop=True).then_inc(fc1_ps[0], 1)
                    if j >= 1:
                        wait(pe, hid_r, b, j)
                        last = pe.matmul(F1[:, :], fc2T[:, j - 1, :], hid[:, j - 1, :], start=(j == 1), stop=(j == NJ))
                last.then_inc(fc2_ps[0], 1)
                wait(pe, y0_r, b, 1)
                transposes(F0, lambda i: yS[:, i * P:(i + 1) * P]).then_inc(y0_T[0], 1)

            h2T = h1T

            def moe_in(b):
                ln_turn(b, 3, F1)
                wait(pe, ln_evac, b, 3)

            def experts(b):
                hbT = h1T
                n_all = NE * NJ
                for n in range(n_all + 1):
                    if n < n_all:
                        e, j = n // NJ, n % NJ
                        if n == 0:
                            wait(pe, x3_r, b, 1)
                        if n >= 1:
                            wait(pe, silu_r, b, n)
                        pe.matmul(F0[:, :], Wg[:, e, j * P:(j + 1) * P], hbT[:, :], start=True, stop=True).then_inc(gu_g[0], 1)
                        if n >= 2:
                            wait(pe, act_r, b, n - 1)
                        pe.matmul((F2, F3)[n % 2][:, :], Wu[:, e, j * P:(j + 1) * P], hbT[:, :], start=True, stop=True).then_inc(gu_u[0], 1)
                    if n >= 1:
                        e, j = (n - 1) // NJ, (n - 1) % NJ
                        wait(pe, act_r, b, n)
                        pe.matmul(F1[:, :], Wd[:, e, j, :], act[:, (n - 1) % 2, :], start=(n == 1), stop=(n == n_all)).then_inc(down_ps[0], 1)
                wait(pe, y1_r, b, 1)
                transposes(F0, lambda i: yS[:, i * P:(i + 1) * P]).then_inc(y1_T[0], 1)

            def attn1(b):
                ln_turn(b, 4, F1)
                wait(pe, ln_evac, b, 4)
                wait(pe, x4_r, b, 1)
                hcT = h1T
                pe.matmul(F0[:, :], W1[:, 0:P], hcT[:, :], start=True, stop=True).then_inc(qkv1_ps[0], 1)
                pe.matmul(F2[:, :], W1[:, P:2 * P], hcT[:, :], start=True, stop=True).then_inc(qkv1_ps[0], 1)
                for i in range(NT):
                    last = pe.matmul(F3[:, i * P:(i + 1) * P], hcT[:, i * P:(i + 1) * P], W1[:, 2 * P:3 * P], start=True, stop=True)
                last.then_inc(qkv1_ps[0], 1)
                wait(pe, q1_r, b, 1)
                wait(pe, v1_r, b, 1)
                for n in range(N1 + 2):
                    if n < N1:
                        i, h = n // H1, n % H1
                        w = (i + 1) * P
                        f = (F0, F2)[n % 2]
                        if i == 0:
                            wait(pe, k1z_r, b, h + 1)
                        if n >= 2:
                            wait(pe, p1_r, b, n - 1)
                        pe.matmul(f[:, 0:w], q1T[:, i * P:(i + 1) * P], k1z[:, h, 0:w], start=True, stop=False, skip_group_check=True)
                        pe.matmul(f[:, w - P:w], ident_bf[:, :], causal_bf[:, :], start=False, stop=True, skip_group_check=True).then_inc(s1_ps[0], 1)
                    if 1 <= n <= N1:
                        m = n - 1
                        i = m // H1
                        wait(pe, p1_r, b, m + 1)
                        if m >= 1:
                            wait(pe, p1T_r, b, m)
                        transposes(F3, lambda j: p1[:, m % 2, j * P:(j + 1) * P], i + 1).then_inc(p1_T[0], 1)
                    if n >= 2:
                        m = n - 2
                        i, h = m // H1, m % H1
                        if h == 0 and i >= 1:
                            wait(pe, o1_r, b, i)
                        wait(pe, p1T_r, b, m + 1)
                        for j in range(i + 1):
                            last = pe.matmul(F1[:, h * (D1 + 1):(h + 1) * (D1 + 1)], p1T[:, m % 2, j * P:(j + 1) * P], v1[:, j, h, :], start=(j == 0), stop=(j == i))
                        if h == H1 - 1:
                            last.then_inc(o1_ps[0], 1)
                wait(pe, att1_r, b, 1)
                transposes(F0, lambda i: att[:, i, :]).then_inc(att1_T[0], 1)
                wait(pe, attT1_r, b, 1)
                wait(pe, WoutG_r, b, 1)
                for i in range(NT):
                    last = pe.matmul(F2[:, i * P:(i + 1) * P], attT[:, i * P:(i + 1) * P], WoutG[:, :], start=True, stop=True)
                last.then_inc(out1_ps[0], 1)
                ln_turn(b, 5, F1)
                wait(pe, ln_evac, b, 5)

            def gates(b):
                wait(pe, x5_r, b, 1)
                for k, f in enumerate((F0, F2)):
                    for i in range(2):
                        t = 2 * k + i
                        last = pe.matmul(f[:, i * 256:(i + 1) * 256], hdT[:, t * P:(t + 1) * P], gatesT[:, :], start=True, stop=True)
                    last.then_inc(gate_ps[0], 1)

            def values(b):
                for i in range(NT):
                    if i >= 2:
                        wait(pe, pv_r, b, i - 1)
                    pe.matmul((F1, F3)[i % 2][:, :], hdT[:, i * P:(i + 1) * P], WvT[:, :], start=True, stop=True).then_inc(pv_ps[0], 1)

            def qk(b):
                for p in range(NP):
                    if p >= 2:
                        wait(pe, ks_r, b, p - 1)
                    pe.matmul((S0, S1)[p % 2][:, :], WkT[:, p * P:(p + 1) * P], hdT[:, :], start=True, stop=True).then_inc(k_ps[0], 1)

            def heads(b):
                wait(pe, ks_r, b, NP)
                wait(pe, vals_r, b, NQ * NT)

                def queries(i, before):
                    for half in range(2):
                        if half:
                            wait(pe, qs_r, b, 2 * i + 1)
                        elif before is not None:
                            wait(pe, pT_r, b, before)
                        for p in range(4 * half, 4 * half + 4):
                            last = pe.matmul(TB[:, (p % 4) * P:(p % 4 + 1) * P], WqT[:, p * P:(p + 1) * P], hdT[:, i * P:(i + 1) * P], start=True, stop=True)
                        last.then_inc(q_ps[0], 1)
                    wait(pe, qs_r, b, 2 * i + 2)

                def mixed_out(i):
                    wait(pe, ym_r, b, NQ * (i + 1))
                    wait(pe, pT_r, b, min((i + 1) * HS + MIXED_AT, N2))
                    transposes(TB, lambda j: ym[:, j * P:(j + 1) * P]).then_inc(ym_T[0], 1)
                    wait(pe, ymT_r, b, i + 1)
                    for j in range(NJ):
                        last = pe.matmul(TB[:, 0:P], ymT[:, j, :], WoT[:, j, :], start=(j == 0), stop=(j == NJ - 1))
                    last.then_inc(res_ps[0], 1)
                    wait(pe, resg_r, b, i + 1)

                queries(0, None)
                for n in range(N2 + 2):
                    if n < N2:
                        i, h = n // HS, n % HS
                        r = 64 * (h % 2)
                        if h == 0:
                            wait(pe, qs_r, b, 2 * i + 2)
                        if n >= 2:
                            wait(pe, p_r, b, n - 1)
                        pe.matmul((S0, S1)[n % 2][:, :], qsT[r:r + DS, i % 2, h // 2, :], ksT[r:r + DS, h // 2, :], start=True, stop=True).then_inc(s_ps[0], 1)
                    if n % HS == HS - 4 and n < N2 - HS:
                        queries(n // HS + 1, n - 1)
                    if 1 <= n <= N2:
                        m = n - 1
                        wait(pe, p_r, b, m + 1)
                        if m >= 1:
                            wait(pe, pT_r, b, m)
                        transposes(TB, lambda j: pr[:, m % 2, j * P:(j + 1) * P]).then_inc(p_T[0], 1)
                    if n >= 2:
                        m = n - 2
                        i, h = m // HS, m % HS
                        if h % GROUP == 0 and m >= GROUP:
                            wait(pe, oa_r, b, m // GROUP)
                        wait(pe, pT_r, b, m + 1)
                        for j in range(NT):
                            last = pe.matmul(OB[:, (h % GROUP) * VW:(h % GROUP + 1) * VW], prT[:, m % 2, j * P:(j + 1) * P], vals[:, j, h, :], start=(j == 0), stop=(j == NT - 1))
                        if h % GROUP == GROUP - 1:
                            last.then_inc(o_ps[0], 1)
                    if n % HS == MIXED_AT and n > HS:
                        mixed_out(n // HS - 1)
                mixed_out(NT - 1)

            loop(pe, {"attn0": attn0, "moe_in": moe_in, "experts": experts, "attn1": attn1, "gates": gates,
                      "values": values, "qk": qk, "heads": heads})

        @block.scalar
        def _(s):
            s.wait_ge(small_in[0], 16 * 16)
            for l in range(2):
                s.activation(cexp[l], crow[l], ACT.Exp, scale=-1.0).then_inc(const_v[0], 1)
            s.wait_ge(setup_done[0], 1)

            def ln_out(b, n, dst, src, scale, bias, ready):
                wait(s, ln_T, b, n)
                if ready is not None:
                    wait(s, ready, b, 1)
                s.activation(dst, src, ACT.Identity, scale=scale, bias=bias).then_inc(ln_evac[0], 1)

            def attn0(b):
                ln_out(b, 1, h1T[:, :], F0[:, :], cols[:, 0:1], cols[:, 1:2], None)
                wait(s, emin_r, b, 1)
                s.activation(qexp, qmin, ACT.Exp).then_inc(eexp_r[0], 1)
                for k in range(2):
                    wait(s, emin_r, b, 2 + k)
                    s.activation(kexp[:, 2 * k:2 * k + 2, :], kmin[:, 2 * k:2 * k + 2, :], ACT.Exp).then_inc(eexp_r[0], 1)
                    s.activation(v0[:, 2 * k:2 * k + 2, 0:P], (F2, F3)[k][:, :].rearrange("p (i c) -> p i c", i=2)[:, :, P:2 * P], ACT.Copy).then_inc(v0_r[0], 1)
                wait(s, att0_T, b, 1)
                s.activation(attT[:, :], F1[:, :], ACT.Copy).then_inc(attT0_r[0], 1)
                ln_out(b, 2, h1T[:, :], F1[:, :], cols[:, 2:3], cols[:, 3:4], None)
                for j in range(NJ):
                    wait(s, fc1_ps, b, j + 1)
                    s.activation(hid[:, j, :], (F2, F3)[j % 2][:, :], ACT.Gelu, bias=cols[:, 4 + j:5 + j]).then_inc(hid_r[0], 1)

            def moe_in(b):
                ln_out(b, 3, h1T[:, :], F1[:, :], modB[:, CB0:CB0 + 1], modB[:, SB0:SB0 + 1], modB_r)

            def experts(b):
                for n in range(NE * NJ):
                    wait(s, gu_g, b, n + 1)
                    if n >= 2:
                        wait(s, act_r, b, n - 1)
                    s.activation(silu[:, n % 2, :], F0[:, :], ACT.Silu).then_inc(silu_r[0], 1)

            def attn1(b):
                ln_out(b, 4, h1T[:, :], F1[:, :], modB[:, CA1:CA1 + 1], modB[:, SA1:SA1 + 1], None)
                wait(s, qkv1_ps, b, 1)
                s.activation(q1T[:, :], F0[:, :], ACT.Copy).then_inc(q1_r[0], 1)
                wait(s, qkv1_ps, b, 3)
                s.activation(v1[:, :, :, 0:D1], F3[:, :].rearrange("p (i h d) -> p i h d", i=NT, h=H1), ACT.Copy).then_inc(v1_r[0], 1)
                for n in range(N1):
                    w = (n // H1 + 1) * P
                    wait(s, nmax1_r, b, n + 1)
                    if n >= 2:
                        wait(s, p1_T, b, n - 1)
                    s.activation(p1[:, n % 2, 0:w], (F0, F2)[n % 2][:, 0:w], ACT.Exp, bias=nmax1[:, n % 2:n % 2 + 1]).then_inc(p1_r[0], 1)
                wait(s, att1_T, b, 1)
                s.activation(attT[:, :], F0[:, :], ACT.Copy).then_inc(attT1_r[0], 1)
                wait(s, ks_r, b, 0)
                ln_out(b, 5, hdT[:, :], F1[:, :], modB[:, CB1:CB1 + 1], modB[:, SB1:SB1 + 1], None)

            def gates(b):
                for k, f in enumerate((F0, F2)):
                    wait(s, gate_ps, b, k + 1)
                    for i in range(2):
                        last = s.activation(gate[:, :, 2 * k + i, :, :].rearrange("p g h e -> p g (h e)"),
                                            f[:, i * 256:(i + 1) * 256].rearrange("p (g c) -> p g c", g=2), ACT.Copy)
                    last.then_inc(gate_r[0], 1)
                wait(s, topk_v, b, 6)
                s.activation(sigd[:, :, :], top[:, :, 0:NT * HS], ACT.Exp, scale=-1.0).then_inc(sig_e[0], 1)

            def values(b):
                for i in range(NT):
                    wait(s, pv_ps, b, i + 1)
                    if i >= 2:
                        wait(s, vprod_r, b, NQ * (i - 1))
                    s.activation(pv[:, i % 2, :], (F1, F3)[i % 2][:, :], ACT.Copy).then_inc(pv_r[0], 1)

            def qk(b):
                pass

            def heads(b):
                def queries(i):
                    for half in range(2):
                        wait(s, q_ps, b, 2 * i + half + 1)
                        s.activation(qsT[:, i % 2, 4 * half:4 * half + 4, :].rearrange("p a t -> p (a t)"), TB[:, :], ACT.Copy).then_inc(qs_r[0], 1)

                queries(0)
                for n in range(N2 + 1):
                    if n % HS == HS - 4 and n < N2 - HS:
                        queries(n // HS + 1)
                    if n < N2:
                        wait(s, nmax_r, b, n + 1)
                        if n >= 2:
                            wait(s, p_T, b, n - 1)
                        s.activation(pr[:, n % 2, :], (S0, S1)[n % 2][:, :], ACT.Exp, bias=nmax[:, n % 2:n % 2 + 1]).then_inc(p_r[0], 1)
                    if n % HS == MIXED_AT and n > HS or n == N2:
                        i = n // HS - 1
                        wait(s, ym_T, b, i + 1)
                        s.activation(ymT[:, :, :].rearrange("p j t -> p (j t)"), TB[:, :], ACT.Copy).then_inc(ymT_r[0], 1)

            loop(s, {"attn0": attn0, "moe_in": moe_in, "experts": experts, "attn1": attn1, "gates": gates,
                     "values": values, "qk": qk, "heads": heads})

        @block.vector
        def _(v):
            v.wait_ge(small_in[0], 16 * 16)
            v.wait_ge(const_v[0], 2)
            for l in range(2):
                v.tensor_scalar(cexp[l], cexp[l], 1.0, None, ALU.add)
            v.tensor_tensor(sdirs.rearrange("o (h d) -> o h d", h=H1), dirs.rearrange("o (h d) -> o h d", h=H1),
                            scales.unsqueeze(2).to_broadcast([1, H1, D1]), ALU.mult).then_inc(const_v[0], 3)
            v.wait_ge(const_v[0], 5)
            for l in range(2):
                last = v.reciprocal(crec[l], cexp[l])
            last.then_inc(const_v[0], 2)
            v.wait_ge(const_v[0], 7)
            for l in range(2):
                last = v.tensor_tensor(csil[l], crow[l], crec[l], ALU.mult)
            last.then_inc(const_v[0], 2)
            for n in range((NTURN + 3) // 4):
                part = turns[4 * n:4 * n + 4]
                v.wait_ge(setup_pe[0], n + 1)
                for i, (_, dst) in enumerate(part):
                    src = bank[n % 2][:, i * P:(i + 1) * P]
                    if 12 <= 4 * n + i < 20:
                        last = v.tensor_scalar(dst, src, DS ** -0.5, None, ALU.mult)
                    else:
                        last = v.tensor_copy(dst, src)
                last.then_inc(setup_v[0], 1)
            n = (NTURN + 3) // 4
            v.wait_ge(setup_pe[0], n + 1)
            v.tensor_copy(ksT[:, 6, 0:2 * NB], bank[2][:, 0:2 * NB])
            v.tensor_copy(cols[:, :], bank[2][:, 2 * NB:2 * NB + 9])
            v.wait_ge(const_g[0], 12)
            v.tensor_tensor(bias_m, bank[3][:, 0:P], block16[:, :], ALU.mult).then_inc(setup_v[0], 1)
            v.wait_ge(setup_v[0], n + 1)
            v.scalar_tensor_tensor(out=bias_m, in0=ident[:, :], scalar=D1 ** -0.5, in1=bias_m, op0=ALU.mult, op1=ALU.add).then_inc(setup_v[0], 1)
            v.wait_ge(setup_pe[0], n + 2)
            v.tensor_copy(mod[:, :, :].rearrange("p b m -> p m b"), bank[4][:, 0:96].rearrange("p (m b) -> p m b", m=12)).then_inc(setup_v[0], 1)
            v.wait_ge(setup_pe[0], n + 3)
            v.tensor_copy(W1[:, 0:P], bank[5][:, 0:P])

            def floor_gate(g, s, w, k):
                v.tensor_scalar(s, g, 0.0, 2.0, ALU.is_ge, ALU.mult).then_inc(setup_v[0], 1)
                v.wait_ge(setup_v[0], k + 1)
                v.tensor_scalar(s, s, -1.0, None, ALU.add).then_inc(setup_v[0], 1)
                v.wait_ge(setup_v[0], k + 2)
                v.tensor_tensor(w, g, s, ALU.mult).then_inc(setup_v[0], 1)
                v.wait_ge(setup_v[0], k + 3)
                v.tensor_scalar(w, w, 0.25, None, ALU.max).then_inc(setup_v[0], 1)
                v.wait_ge(setup_v[0], k + 4)
                v.tensor_tensor(g, w, s, ALU.mult).then_inc(setup_v[0], 1)
                v.wait_ge(setup_v[0], k + 5)

            v.wait_ge(setup_v[0], n + 3)
            k = n + 3
            for m in (CA0, CB0, CA1, CB1):
                v.tensor_scalar(mod[:, :, m], mod[:, :, m], 1.0, None, ALU.add)
            for m in (GA0, GB0, GA1, GB1):
                floor_gate(mod[:, :, m], sgn[:, 0:NB], gab[:, 0:NB], k)
                k += 5
            v.wait_ge(setup_pe[0], n + 4)
            v.tensor_copy(rtab[:, 0:3, :].rearrange("p m c -> p (m c)"), bank[6][0:NB, 0:3 * P])
            v.tensor_copy(rtab[:, 3:5, :].rearrange("p m c -> p (m c)"), bank[7][0:NB, 0:2 * P]).then_inc(setup_v[0], 1)
            k += 1
            v.wait_ge(setup_v[0], k)
            v.tensor_scalar(rtab[:, 1, :], rtab[:, 1, :], 1.0, None, ALU.add)
            for m in (2, 3, 4):
                floor_gate(rtab[:, m, :], rsgn, rabs, k)
                k += 5
            v.memset(nmax1[:, :], 0.0).then_inc(setup_done[0], 1)

            def stats_of(b, n, src):
                for i in range(NT):
                    last = v.bn_stats(stats[:, i, :], src[:, i, :])
                last.then_inc(ln_stats[0], 1)
                wait(v, ln_stats, b, n + 1)
                v.memset(pause[:, :], 0.0)
                for i in range(NT):
                    last = v.bn_aggr(mv[:, i, :], stats[:, i, :])
                last.then_inc(ln_mv[0], 1)
                wait(v, ln_mv, b, n + 1)
                v.tensor_scalar(vareps[:, :], mv[:, :, 1], EPS_LN, None, ALU.add).then_inc(ln_eps[0], 1)

            def norm_of(b, n, src):
                wait(v, ln_rstd, b, n + 1)
                for i in range(NT):
                    last = v.tensor_scalar(nrm[:, i, :], src[:, i, :], mv[:, i, 0:1], rstd[:, i:i + 1], ALU.subtract, ALU.mult)
                last.then_inc(ln_n[0], 1)

            def attn0(b):
                wait(v, x5_r, b, 0)
                v.tensor_scalar(modA[:, :], mod[:, bass.ds(b, 1), :].rearrange("p o m -> p (o m)"), 1.0, None, ALU.mult).then_inc(modA_r[0], 1)
                wait(v, x_in, b, 32)
                stats_of(b, 0, xin)
                norm_of(b, 0, xin)
                wait(v, ln_n, b, 1)
                v.tensor_tensor(h0m[:, :, :], nrm[:, :, :], rows0[:, 1:2, :].to_broadcast([P, NT, P]), ALU.mult).then_inc(h0m_r[0], 1)
                wait(v, h0m_r, b, 1)
                v.tensor_tensor(h0[:, :, :], h0m[:, :, :], rows0[:, 0:1, :].to_broadcast([P, NT, P]), ALU.add).then_inc(h0_r[0], 1)
                wait(v, h0_r, b, 1)
                stats_of(b, 1, h0)
                norm_of(b, 1, h0)
                kview = [f[:, :].rearrange("p (i c) -> p i c", i=2)[:, :, 0:P] for f in (F2, F3)]
                wait(v, qkv0_r, b, 1)
                v.tensor_scalar(qmin, F1[:, :], 0.0, None, ALU.min).then_inc(emin_r[0], 1)
                for k in range(2):
                    wait(v, qkv0_r, b, 2 + k)
                    v.tensor_scalar(kmin[:, 2 * k:2 * k + 2, :], kview[k], 0.0, None, ALU.min).then_inc(emin_r[0], 1)
                wait(v, eexp_r, b, 1)
                v.scalar_tensor_tensor(out=qe, in0=F1[:, :], scalar=0.0, in1=qexp, op0=ALU.max, op1=ALU.add).then_inc(elu_r[0], 1)
                for k in range(2):
                    wait(v, eexp_r, b, 2 + k)
                    wait(v, v0_r, b, 1 + k)
                    v.scalar_tensor_tensor(out=ke[:, 2 * k:2 * k + 2, :], in0=kview[k], scalar=0.0, in1=kexp[:, 2 * k:2 * k + 2, :], op0=ALU.max, op1=ALU.add).then_inc(elu_r[0], 1)
                wait(v, kv_ps, b, 1)
                v.tensor_tensor(kv[:, 0:P], F0[:, 0:P], block8[:, :], ALU.mult)
                v.tensor_scalar(kv[:, P:P + H0], head_of8[:, :], F0[:, P:P + 1], None, ALU.mult).then_inc(kv_r[0], 1)
                nview = [f[:, :].rearrange("p (i c) -> p i c", i=2) for f in (F2, F3)]
                wait(v, num_ps, b, 2)
                for k in range(2):
                    last = v.tensor_scalar(den0[:, 2 * k:2 * k + 2, :], nview[k][:, :, P:P + H0], EPS_ATTN, None, ALU.add)
                last.then_inc(den0_r[0], 1)
                wait(v, den0_r, b, 1)
                v.reciprocal(rden0[:, :, :], den0[:, :, :]).then_inc(rden0_r[0], 1)
                wait(v, rden0_r, b, 1)
                for t in range(NT):
                    last = v.tensor_tensor(att[:, t, :].rearrange("p (h d) -> p h d", h=H0),
                                           nview[t // 2][:, t % 2, 0:P].rearrange("p (h d) -> p h d", h=H0),
                                           rden0[:, t, :].unsqueeze(2).to_broadcast([P, H0, D0]), ALU.mult)
                last.then_inc(att0_r[0], 1)
                wait(v, proj_ps, b, 1)
                wait(v, xg_r, b, 0)
                v.tensor_tensor(x2[:, :, :], tiles(F0), h0[:, :, :], ALU.add).then_inc(x2_r[0], 1)
                wait(v, x2_r, b, 1)
                stats_of(b, 2, x2)
                norm_of(b, 2, x2)
                wait(v, fc2_ps, b, 1)
                v.tensor_scalar(yS, F1[:, :], cols[:, 8:9], modA[:, GA0:GA0 + 1], ALU.add, ALU.mult).then_inc(y0_r[0], 1)
                wait(v, y0_T, b, 1)
                wait(v, xg_r, b, 1)
                v.tensor_tensor(x3[:, :, :], tiles(F0), xg[:, :, :], ALU.add).then_inc(x3_r[0], 1)

            def moe_in(b):
                wait(v, ln_evac, b, 0)
                v.tensor_scalar(modB[:, :], mod[:, bass.ds(b, 1), :].rearrange("p o m -> p (o m)"), 1.0, None, ALU.mult).then_inc(modB_r[0], 1)
                wait(v, x3_r, b, 1)
                stats_of(b, 3, x3)
                norm_of(b, 3, x3)

            def experts(b):
                for n in range(NE * NJ):
                    wait(v, silu_r, b, n + 1)
                    wait(v, gu_u, b, n + 1)
                    if n >= 2:
                        wait(v, down_ps, b, n - 1)
                    v.tensor_tensor(act[:, n % 2, :], (F2, F3)[n % 2][:, :], silu[:, n % 2, :], ALU.mult).then_inc(act_r[0], 1)
                wait(v, down_ps, b, NE * NJ)
                v.tensor_scalar(yS, F1[:, :], modB[:, GB0:GB0 + 1], None, ALU.mult).then_inc(y1_r[0], 1)
                wait(v, y1_T, b, 1)
                v.tensor_tensor(x4[:, :, :], tiles(F0), x3[:, :, :], ALU.add).then_inc(x4_r[0], 1)

            def attn1(b):
                wait(v, x4_r, b, 1)
                stats_of(b, 4, x4)
                norm_of(b, 4, x4)
                wait(v, qkv1_ps, b, 2)
                v.tensor_copy(k1T, F2[:, :]).then_inc(k1_r[0], 1)
                for n in range(N1 + 1):
                    if n < N1:
                        w = (n // H1 + 1) * P
                        wait(v, s1_ps, b, n + 1)
                        if n >= 2:
                            wait(v, p1_r, b, n - 1)
                        v.tensor_reduce(nmax1[:, n % 2:n % 2 + 1], (F0, F2)[n % 2][:, 0:w], X_AXIS, ALU.max, negate=True).then_inc(nmax1_r[0], 1)
                    if n >= 1:
                        m = n - 1
                        w = (m // H1 + 1) * P
                        wait(v, p1_T, b, m + 1)
                        v.tensor_copy(p1T[:, m % 2, 0:w], F3[:, 0:w]).then_inc(p1T_r[0], 1)
                    if n >= 2 and (n - 2) % H1 == H1 - 1 or n == N1:
                        i = (n - 2) // H1 if n < N1 else NT - 1
                        wait(v, o1_ps, b, i + 1)
                        v.tensor_copy(o1[:, i, :, :].rearrange("p h d -> p (h d)"), F1[:, 0:H1 * (D1 + 1)]).then_inc(o1_r[0], 1)
                wait(v, o1_r, b, NT)
                v.reciprocal(rden1[:, :, :], o1[:, :, :, D1]).then_inc(rden1_r[0], 1)
                wait(v, rden1_r, b, 1)
                v.tensor_tensor(att[:, :, :].rearrange("p i (h d) -> p i h d", h=H1), o1[:, :, :, 0:D1],
                                rden1[:, :, :].unsqueeze(3).to_broadcast([P, NT, H1, D1]), ALU.mult).then_inc(att1_r[0], 1)
                wait(v, out1_ps, b, 1)
                wait(v, stored, b, 0)
                v.tensor_tensor(x5[:, :, :], tiles(F2), x4[:, :, :], ALU.add).then_inc(x5_r[0], 1)
                wait(v, x5_r, b, 1)
                stats_of(b, 5, x5)
                norm_of(b, 5, x5)

            def gates(b):
                g = gate[:, :, :, :, :].rearrange("p g i h e -> p (g i h) e")
                n = 2 * NT * HS
                half = NT * HS

                def wide(t):
                    return t.unsqueeze(2).to_broadcast([P, n, NE])

                wait(v, gate_r, b, 2)
                v.tensor_reduce(top[:, 0, :], g, X_AXIS, ALU.max).then_inc(topk_v[0], 1)
                for r in range(2):
                    one = (oh1, oh2)[r]
                    k = 5 * r
                    wait(v, topk_v, b, k + 1)
                    v.tensor_tensor(eq[:, :, :], g, wide(top[:, r, :]), ALU.is_ge).then_inc(topk_v[0], 1)
                    wait(v, topk_g, b, r + 1)
                    v.tensor_reduce(pick[:, :], cand[:, :, :], X_AXIS, ALU.max).then_inc(topk_v[0], 1)
                    wait(v, topk_v, b, k + 3)
                    v.tensor_tensor(one[:, :, :], cand[:, :, :], wide(pick[:, :]), ALU.is_equal).then_inc(topk_v[0], 1)
                    if r == 0:
                        wait(v, topk_v, b, 4)
                        v.scalar_tensor_tensor(out=g, in0=oh1[:, :, :], scalar=-BIG, in1=g, op0=ALU.mult, op1=ALU.add).then_inc(topk_v[0], 1)
                        wait(v, topk_v, b, 5)
                        v.tensor_reduce(top[:, 1, :], g, X_AXIS, ALU.max).then_inc(topk_v[0], 1)
                wait(v, sig_e, b, 1)
                v.tensor_scalar(sigd[:, :, :], sigd[:, :, :], 1.0, None, ALU.add).then_inc(sig_v[0], 1)
                wait(v, sig_v, b, 1)
                v.reciprocal(sig[:, :, :], sigd[:, :, :]).then_inc(sig_v[0], 1)
                wait(v, topk_v, b, 9)
                v.tensor_tensor(masko[:, :, :, :].rearrange("p i h e -> p (i h) e"), oh1[:, half:n, :], oh2[:, half:n, :], ALU.add).then_inc(masko_r[0], 1)

            def values(b):
                for n in range(NQ * NT):
                    i, q = n // NQ, n % NQ
                    wait(v, vprod_r, b, n + 1)
                    v.tensor_reduce(vals[:, i, HQ * q:HQ * q + HQ, 0:DS], prod[:, n % 2, :].rearrange("p (h d e) -> p h d e", h=HQ, e=NE), X_AXIS, ALU.add).then_inc(vals_r[0], 1)

            def qk(b):
                for p in range(NP):
                    wait(v, k_ps, b, p + 1)
                    v.tensor_copy(ksT[:, p, :], (S0, S1)[p % 2][:, :]).then_inc(ks_r[0], 1)

            def heads(b):
                wait(v, rows1b_in, b, 16)

                def mixed(i):
                    for q in range(NQ):
                        n = NQ * i + q
                        wait(v, oprod_r, b, n + 1)
                        v.tensor_reduce(ym[:, q * DS:(q + 1) * DS], prod[:, n % 2, :].rearrange("p (d h) -> p d h", h=HS), X_AXIS, ALU.add).then_inc(ym_r[0], 1)

                def out_tile(i):
                    wait(v, res_ps, b, i + 1)
                    v.tensor_tensor(resg[:, :], TB[:, 0:P], rows1b[:, :], ALU.mult).then_inc(resg_r[0], 1)
                    wait(v, resg_r, b, i + 1)
                    v.tensor_tensor(xout[:, i, :], resg[:, :], x5[:, i, :], ALU.add).then_inc(xout_r[0], 1)

                def collect(c):
                    wait(v, o_ps, b, c + 1)
                    i = c // NG
                    v.tensor_copy(oa[:, i % 2, GROUP * (c % NG):GROUP * (c % NG + 1), :].rearrange("p h d -> p (h d)"), OB[:, 0:GROUP * VW]).then_inc(oa_r[0], 1)
                    if c % NG == NG - 1:
                        wait(v, oa_r, b, c + 1)
                        v.reciprocal(rden[:, i % 2, :], oa[:, i % 2, :, DS]).then_inc(rden_r[0], 1)

                for n in range(N2 + 1):
                    if n < N2:
                        wait(v, s_ps, b, n + 1)
                        if n >= 2:
                            wait(v, p_r, b, n - 1)
                        v.tensor_reduce(nmax[:, n % 2:n % 2 + 1], (S0, S1)[n % 2][:, :], X_AXIS, ALU.max, negate=True).then_inc(nmax_r[0], 1)
                    if n >= 1:
                        m = n - 1
                        wait(v, p_T, b, m + 1)
                        v.tensor_copy(prT[:, m % 2, :], TB[:, :]).then_inc(pT_r[0], 1)
                    if n > GROUP and n % GROUP == 1:
                        collect(n // GROUP - 1)
                    if n > HS and n % HS == 7:
                        mixed(n // HS - 1)
                    if n > HS and n % HS == MIXED_AT:
                        out_tile(n // HS - 1)
                collect(NT * NG - 1)
                mixed(NT - 1)
                out_tile(NT - 1)

            loop(v, {"attn0": attn0, "moe_in": moe_in, "experts": experts, "attn1": attn1, "gates": gates,
                     "values": values, "qk": qk, "heads": heads})


NAMES = ['L0_attn_x', 'L0_attn_norm1_g', 'L0_attn_norm1_b', 'L0_attn_qkv_w', 'L0_attn_proj_w', 'L0_attn_proj_b',
         'L0_attn_norm2_g', 'L0_attn_norm2_b', 'L0_attn_fc1_w', 'L0_attn_fc1_b', 'L0_attn_fc2_w', 'L0_attn_fc2_b',
         'L0_ffn_Wg', 'L0_ffn_Wu', 'L0_ffn_Wd', 'L0_c', 'L0_wmod', 'L1_attn_Wqkv', 'L1_attn_Wout',
         'L1_attn_head_scales', 'L1_attn_head_dirs', 'L1_ffn_Wq', 'L1_ffn_Wk', 'L1_ffn_Wv', 'L1_ffn_Ws', 'L1_ffn_Wd',
         'L1_ffn_Wo', 'L1_c', 'L1_wmod']


def kernel(**inputs):
    import numpy as _np
    import concourse.bacc as _bacc
    from concourse import mybir as _mybir
    from concourse.bass_utils import run_bass_kernel_spmd as _run

    nc = _bacc.Bacc("TRN2", target_bir_lowering=False, num_devices=1)
    arrays, aps = {}, {}
    for name in NAMES:
        x = _np.ascontiguousarray(inputs[name])
        arrays[f"in_{name}"] = x
        aps[name] = nc.dram_tensor(f"in_{name}", x.shape, _mybir.dt.from_np(x.dtype), kind="ExternalInput").ap()
    out = nc.dram_tensor("out_0", (NB, T, P), F32, kind="ExternalOutput").ap()
    row_table = nc.dram_tensor("row_table", (NB, 5 * P), F32, kind="Internal").ap()
    build(nc, aps, row_table, out)
    r = _run(nc, [arrays], core_ids=[0])
    return r.results[0]["out_0"]
```

```python
from contextlib import ExitStack

import concourse.bass as bass
from concourse import mybir

F32 = mybir.dt.float32
BF16 = mybir.dt.bfloat16
ALU = mybir.AluOpType
ACT = mybir.ActivationFunctionType
X_AXIS = mybir.AxisListType.X

P = 128
NB = 8
T = 512
NT = T // P
H0, D0 = 16, 8
NJ = 4
NE = 8
H1, D1 = 8, 16
HS, DS = 16, 64
NP = HS // 2
VW = DS + 1
NQ = 8
GROUP = 4
NG = HS // GROUP
QUERIES_AT = 10
PIECES_AT = 4
MIXED_AT = 13
EPS_LN, EPS_ATTN = 1e-5, 1e-6
BIG = 3.0e38
MASKED = -1.0e30
SA0, CA0, GA0, SB0, CB0, GB0, SA1, CA1, GA1, SB1, CB1, GB1 = range(12)
LNS = 6
N1, N2 = NT * H1, NT * HS
A1 = 5
MARKS = {"load": 1, "attn0": 24, "moe_in": 3, "experts": NE * NJ + 2, "attn1": A1 + N1 + 2 + 6, "gates": 5,
         "values": NQ * NT, "heads": N2 + 2 + NQ + 2}
PER = {}


def build(nc, a, row_table, out):
    ctx = ExitStack()
    with ctx:
        def sb(name, shape, dt=F32):
            return ctx.enter_context(nc.sbuf_tensor(name, shape, dt))

        def sem(name, per=0):
            s = ctx.enter_context(nc.semaphore(name))
            PER[name] = per
            return s, per

        ident = sb("ident", [P, P])
        ident_bf = sb("ident_bf", [P, P], BF16)
        causal_bf = sb("causal_bf", [P, P], BF16)
        block8 = sb("block8", [P, P])
        head_of8 = sb("head_of8", [P, H0])
        head_of16 = sb("head_of16", [P, H1])
        ones_row = sb("ones_row", [1, P])
        first_wins = sb("first_wins", [P, NE])
        minus_half = sb("minus_half", [P, NT])
        qkvT = sb("qkvT", [P, 3 * P])
        projT = sb("projT", [P, P])
        fc1T = sb("fc1T", [P, T])
        fc2T = sb("fc2T", [P, NJ, P])
        proj_b_row = sb("proj_b_row", [1, NT, P])
        cols = sb("cols", [P, 9])
        Wg = sb("Wg", [P, NE, T])
        Wu = sb("Wu", [P, NE, T])
        Wd = sb("Wd", [P, NE, NJ, P])
        W1 = sb("W1", [P, 3 * P])
        Wout = sb("Wout", [P, P])
        WqT = sb("WqT", [P, HS * DS])
        WkT = sb("WkT", [P, HS * DS])
        WvT = sb("WvT", [P, NE * DS])
        gatesT = sb("gatesT", [P, 2 * P])
        WoT = sb("WoT", [P, NJ, P])
        mod = sb("mod", [P, NB, 12])
        rows0 = sb("rows0", [P, 3, P])
        rows1a = sb("rows1a", [P, P])
        rows1b = sb("rows1b", [P, P])

        HQ = HS // NQ

        xin = sb("xin", [P, NT, P])
        nrm_o1 = sb("nrm_o1", [P, NT * H1 * (D1 + 1)])
        nrm = nrm_o1[:, 0:NT * P].rearrange("p (i c) -> p i c", i=NT)
        o1 = nrm_o1[:, :].rearrange("p (i h d) -> p i h d", i=NT, h=H1)
        stats = sb("stats", [P, NT, 6])
        mv = sb("mv", [P, NT, 2])
        pause = sb("pause", [P, 1])
        vareps = sb("vareps", [P, NT])
        rstd = sb("rstd", [P, NT])
        modA = sb("modA", [P, 12])
        modB = sb("modB", [P, 12])
        arena = sb("arena", [P, 6144])

        def part(at, shape):
            n = 1
            for x in shape:
                n *= x
            names = "abcd"[:len(shape)]
            v = arena[:, at:at + n]
            return v if len(shape) == 1 else v.rearrange(f"p ({' '.join(names)}) -> p {' '.join(names)}", **dict(zip(names, shape)))

        h0m = part(0, [NT, P])
        h0 = sb("h0", [P, NT, P])
        h1T = sb("h1T", [P, T])
        qmin = part(512, [T])
        qexp = part(1024, [T])
        qe = part(1536, [T])
        kmin = part(2048, [NT, P])
        kexp = part(2560, [NT, P])
        ke = part(3072, [NT, P])
        v0 = part(3584, [NT, P + 1])
        kv = sb("kv", [P, P + H0])
        den0 = sb("den0", [P, NT, H0])
        rden0 = sb("rden0", [P, NT, H0])
        att = sb("att", [P, NT, P])
        attT = sb("attT", [P, T])
        x2 = h0
        x2g = h0m
        xg = xin
        hid = part(3584, [NJ, T])
        yS = nrm.rearrange("p i c -> p (i c)")
        x3 = h0
        silu = part(0, [2, T])
        act = part(1024, [2, T])
        x4 = x3
        q1T = attT
        k1T = att[:, :, :].rearrange("p i c -> p (i c)")
        k1z = part(0, [H1, T])
        v1 = sb("v1", [P, NT, H1, D1 + 1])
        nmax1 = sb("nmax1", [P, 2])
        p1 = part(4096, [2, T])
        p1T = part(5120, [2, T])
        rden1 = sb("rden1", [P, NT, H1])
        WoutG = sb("WoutG", [P, P])
        x5 = sb("x5", [P, NT, P])
        hdT = sb("hdT", [P, T])
        hdB = sb("hdB", [P, T])
        gate = part(0, [2, NT, HS, NE])
        eq = part(1024, [2 * NT * HS, NE])
        cand = part(2048, [2 * NT * HS, NE])
        oh1 = part(3072, [2 * NT * HS, NE])
        oh2 = part(4096, [2 * NT * HS, NE])
        top = sb("top", [P, 2, 2 * NT * HS])
        pick = sb("pick", [P, 2 * NT * HS])
        sigd = sb("sigd", [P, 2, NT * HS])
        sig = sb("sig", [P, 2, NT * HS])
        mixv = sb("mixv", [P, NT, HS, NE])
        masko = sb("masko", [P, NT, HS, NE])
        maskB = sb("maskB", [P, NT, HS, NE])
        pv = sb("pv", [P, 2, NE * DS])
        prod = sb("prod", [P, 2, HS * NE * DS // NQ])
        vals = sb("vals", [P, NT, HS, VW])
        qsT = sb("qsT", [P, 2, NP, P])
        ksT = sb("ksT", [P, NP, T])
        nmax = sb("nmax", [P, 2])
        pr = sb("pr", [P, 2, T])
        prT = sb("prT", [P, 2, T])
        oa = sb("oa", [P, 2, HS, VW])
        rden = sb("rden", [P, 2, HS])
        coef = sb("coef", [P, 2, HS, NE])
        ym = sb("ym", [P, NE * DS])
        ymT = sb("ymT", [P, NJ, P])
        resg = sb("resg", [P, P])
        xout = sb("xout", [P, NT, P])

        bank = [ctx.enter_context(nc.psum_tensor(f"bank{i}", [P, T], F32)) for i in range(8)]
        F0, F1, F2, F3, S0, S1, TB, OB = bank

        def tiles(t):
            return t[:, :].rearrange("p (i c) -> p i c", i=NT)

        def wait(eng, s, b, k):
            number, offset = b
            k += offset * s[1]
            if not (isinstance(number, int) and number * s[1] + k == 0):
                eng.wait_ge(s[0], number * s[1] + k)

        small_in = sem("small_in")
        raw_in = sem("raw_in")
        experts_in = sem("experts_in")
        const_g = sem("const_g")
        const_v = sem("const_v")
        setup_pe = sem("setup_pe")
        setup_v = sem("setup_v")
        setup_a = sem("setup_a")
        setup_done = sem("setup_done")

        x_in = sem("x_in", 32)
        rows1a_in = sem("rows1a_in", 16)
        rows1b_in = sem("rows1b_in", 16)
        table_out = sem("table_out")
        ln_stats = sem("ln_stats", LNS)
        ln_mv = sem("ln_mv", LNS)
        ln_eps = sem("ln_eps", LNS)
        ln_rstd = sem("ln_rstd", LNS)
        ln_n = sem("ln_n", LNS)
        ln_T = sem("ln_T", 5)
        ln_evac = sem("ln_evac", 5)
        modA_r = sem("modA_r", 1)
        modB_r = sem("modB_r", 1)
        h0m_r = sem("h0m_r", 1)
        h0_r = sem("h0_r", 1)
        qkv0_r = sem("qkv0_r", 3)
        emin_r = sem("emin_r", 3)
        eexp_r = sem("eexp_r", 3)
        elu_r = sem("elu_r", 3)
        v0_r = sem("v0_r", 2)
        kv_ps = sem("kv_ps", 1)
        kv_r = sem("kv_r", 1)
        num_ps = sem("num_ps", 2)
        den0_r = sem("den0_r", 1)
        rden0_r = sem("rden0_r", 1)
        att0_r = sem("att0_r", 1)
        att0_T = sem("att0_T", 1)
        attT0_r = sem("attT0_r", 1)
        proj_ps = sem("proj_ps", 1)
        x2_r = sem("x2_r", 1)
        fc1_ps = sem("fc1_ps", NJ)
        hid_r = sem("hid_r", NJ)
        fc2_ps = sem("fc2_ps", 1)
        y0_r = sem("y0_r", 1)
        y0_T = sem("y0_T", 1)
        x2g_r = sem("x2g_r", 1)
        xg_r = sem("xg_r", 1)
        x3_r = sem("x3_r", 1)
        gu_g = sem("gu_g", NE * NJ)
        gu_u = sem("gu_u", NE * NJ)
        silu_r = sem("silu_r", NE * NJ)
        act_r = sem("act_r", NE * NJ)
        down_ps = sem("down_ps", NE * NJ)
        y1_r = sem("y1_r", 1)
        y1_T = sem("y1_T", 1)
        x4_r = sem("x4_r", 1)
        qkv1_ps = sem("qkv1_ps", 3)
        q1_r = sem("q1_r", 1)
        k1_r = sem("k1_r", 1)
        v1_r = sem("v1_r", 1)
        k1z_r = sem("k1z_r", H1)
        s1_ps = sem("s1_ps", N1)
        nmax1_r = sem("nmax1_r", N1)
        p1_r = sem("p1_r", N1)
        p1_T = sem("p1_T", N1)
        p1T_r = sem("p1T_r", N1)
        o1_ps = sem("o1_ps", NT)
        o1_r = sem("o1_r", NT)
        rden1_r = sem("rden1_r", 1)
        att1_r = sem("att1_r", 1)
        att1_T = sem("att1_T", 1)
        attT1_r = sem("attT1_r", 1)
        WoutG_r = sem("WoutG_r", 1)
        out1_ps = sem("out1_ps", 1)
        x5_r = sem("x5_r", 1)
        gate_ps = sem("gate_ps", 2)
        gate_r = sem("gate_r", 2)
        topk_v = sem("topk_v", 9)
        topk_g = sem("topk_g", 2)
        sig_e = sem("sig_e", 1)
        sig_v = sem("sig_v", 2)
        mix_g = sem("mix_g", 3)
        masko_r = sem("masko_r", 1)
        pv_ps = sem("pv_ps", NT)
        pv_r = sem("pv_r", NT)
        vprod_r = sem("vprod_r", NQ * NT)
        vals_r = sem("vals_r", NQ * NT)
        k_ps = sem("k_ps", NP)
        q_ps = sem("q_ps", 2 * NT)
        qs_r = sem("qs_r", 2 * NT)
        ks_r = sem("ks_r", NP)
        s_ps = sem("s_ps", N2)
        nmax_r = sem("nmax_r", N2)
        p_r = sem("p_r", N2)
        p_T = sem("p_T", N2)
        pT_r = [sem("pT_even", N2 // 2), sem("pT_odd", N2 // 2)]
        hdB_r = sem("hdB_r", 1)
        maskB_r = sem("maskB_r", 1)
        xcopy_r = sem("xcopy_r", 1)
        o_ps = sem("o_ps", NT * NG)
        oa_r = sem("oa_r", NT * NG)
        rden_r = sem("rden_r", NT)
        coef_r = sem("coef_r", NT)
        oprod_r = sem("oprod_r", NQ * NT)
        ym_r = sem("ym_r", NQ * NT)
        ym_T = sem("ym_T", NT)
        ymT_r = sem("ymT_r", NT)
        res_ps = sem("res_ps", NT)
        resg_r = sem("resg_r", NT)
        xout_r = sem("xout_r", NT)
        stored = sem("stored", 16)

        block = ctx.enter_context(nc.Block())

        raw_qkv = part(0, [3, P])
        raw_proj = part(384, [P])
        raw_fc1 = part(512, [4, P])
        raw_fc2 = part(1024, [4, P])
        raw_wq = part(1536, [8, P])
        raw_wk = part(2560, [8, P])
        raw_wv = part(3584, [4, P])
        raw_wo = part(4096, [4, P])
        raw_gates = xin[:, 0:2, :]
        wmod = [ksT[:, 0:2, :].rearrange("p a c -> p (a c)")[:, 0:768],
                ksT[:, 2:4, :].rearrange("p a c -> p (a c)")[:, 0:768]]
        crow = [ksT[0:NB, 4, 0:P], ksT[0:NB, 5, 0:P]]
        cexp = [ksT[0:NB, 4, P:2 * P], ksT[0:NB, 5, P:2 * P]]
        crec = [ksT[0:NB, 4, 2 * P:3 * P], ksT[0:NB, 5, 2 * P:3 * P]]
        csil = [ksT[0:NB, 4, 3 * P:4 * P], ksT[0:NB, 5, 3 * P:4 * P]]
        cT = [ksT[:, 6, 0:NB], ksT[:, 6, NB:2 * NB]]
        col_rows = ksT[0:9, 6, P:2 * P]
        dirs = ksT[0:1, 7, 0:P]
        sdirs = ksT[0:1, 7, P:2 * P]
        scales = ksT[0:1, 7, 2 * P:2 * P + H1]
        wq1T = xin[:, 2, :]
        bias_m = xin[:, 3, :]
        block16 = part(4608, [P])
        sgn = nrm[:, 0, 0:NB]
        gab = nrm[:, 1, 0:NB]
        rtab = part(5120, [5, P])[0:NB]
        rsgn = part(5760, [P])[0:NB]
        rabs = part(5888, [P])[0:NB]
        wq1 = W1[:, 0:P]

        turns = ([(raw_qkv[:, i, :], qkvT[:, i * P:(i + 1) * P]) for i in range(3)]
                 + [(raw_proj, projT[:, :])]
                 + [(raw_fc1[:, i, :], fc1T[:, i * P:(i + 1) * P]) for i in range(4)]
                 + [(raw_fc2[:, i, :], fc2T[:, i, :]) for i in range(4)]
                 + [(raw_wq[:, i, :], WqT[:, i * P:(i + 1) * P]) for i in range(8)]
                 + [(raw_wk[:, i, :], WkT[:, i * P:(i + 1) * P]) for i in range(8)]
                 + [(raw_wv[:, i, :], WvT[:, i * P:(i + 1) * P]) for i in range(4)]
                 + [(raw_wo[:, i, :], WoT[:, i, :]) for i in range(4)]
                 + [(raw_gates[:, i, :], gatesT[:, i * P:(i + 1) * P]) for i in range(2)]
                 + [(wq1, wq1T)])
        NTURN = len(turns)

        def schedule(stages, work):
            for main, beside in work:
                total = sum(MARKS[name] for name, _ in main)
                marks = [(name, b, m) for name, b in beside for m in range(1, MARKS[name] + 1)]
                running = {}
                done = 0

                def advance(gen, m):
                    while gen[1] < m:
                        gen[1] = next(gen[0], 10 ** 6)

                n = 0
                for name, b in main:
                    gen = [stages[name](b), 0] if name in stages else None
                    for m in range(1, MARKS[name] + 1):
                        if gen:
                            advance(gen, m)
                        n += 1
                        while done * total < n * len(marks):
                            oname, ob, om = marks[done]
                            if oname in stages:
                                if om == 1:
                                    running[oname] = [stages[oname](ob), 0]
                                advance(running[oname], om)
                            done += 1

        FRONT_A = ("load", "attn0", "moe_in")
        FRONT_B = ("attn1", "gates")

        def program(eng, stages):
            def of(names, b, offset=0):
                return [(name, (b, offset)) for name in names]

            schedule(stages, [(of(FRONT_A, 0), []), (of(("experts",), 0), []),
                              (of(FRONT_B, 0) + of(FRONT_A, 1), [])])
            second = eng.alloc_register("second")
            with eng.Fori(1, NB - 1) as b:
                schedule(stages, [(of(("experts",), b), of(("values",), b, -1))])
                eng.reg_mov(second, b)
                c = eng.snap(second, min_val=1, max_val=NB - 2)
                schedule(stages, [(of(("heads",), c, -1), of(FRONT_B, c) + of(FRONT_A, c, 1))])
            last = NB - 1
            schedule(stages, [(of(("experts",), last), of(("values",), last - 1)),
                              (of(("heads",), last - 1), of(FRONT_B, last)),
                              (of(("values",), last), []), (of(("heads",), last), [])])

        @block.sync
        def _(sp):
            for row, src in ((0, a["L0_attn_norm1_g"]), (1, a["L0_attn_norm1_b"]), (2, a["L0_attn_norm2_g"]),
                             (3, a["L0_attn_norm2_b"]), (8, a["L0_attn_fc2_b"])):
                sp.dma_start(col_rows[row:row + 1, :], src.rearrange("(o p) -> o p", o=1)).then_inc(small_in[0], 16)
            sp.dma_start(col_rows[4:8, :], a["L0_attn_fc1_b"].rearrange("(j p) -> j p", p=P)).then_inc(small_in[0], 16)
            for i in range(NT):
                sp.dma_start(proj_b_row[:, i, :], a["L0_attn_proj_b"].rearrange("(o p) -> o p", o=1)).then_inc(small_in[0], 16)
            sp.dma_start(crow[0], a["L0_c"]).then_inc(small_in[0], 16)
            sp.dma_start(crow[1], a["L1_c"]).then_inc(small_in[0], 16)
            sp.dma_start(scales, a["L1_attn_head_scales"].rearrange("(o h) -> o h", o=1)).then_inc(small_in[0], 16)
            sp.wait_ge(const_g[0], 3)
            sp.dma_start(dirs.rearrange("o (h d) -> o h d", h=H1)[:, :, 0:3],
                         a["L1_attn_head_dirs"].rearrange("(o h) d -> o h d", o=1)).then_inc(small_in[0], 16)
            sp.dma_start(wmod[0], a["L0_wmod"]).then_inc(small_in[0], 16)
            sp.dma_start(wmod[1], a["L1_wmod"]).then_inc(small_in[0], 16)
            sp.dma_start(raw_qkv, a["L0_attn_qkv_w"].rearrange("(i p) c -> p i c", p=P)).then_inc(raw_in[0], 16)
            sp.dma_start(raw_proj, a["L0_attn_proj_w"]).then_inc(raw_in[0], 16)
            sp.dma_start(raw_fc1, a["L0_attn_fc1_w"].rearrange("(i p) c -> p i c", p=P)).then_inc(raw_in[0], 16)
            sp.dma_start(raw_fc2, a["L0_attn_fc2_w"].rearrange("p (i c) -> p i c", c=P)).then_inc(raw_in[0], 16)
            sp.dma_start(raw_wq, a["L1_ffn_Wq"].rearrange("(i a) d c -> (a d) i c", a=2)).then_inc(raw_in[0], 16)
            sp.dma_start(raw_wk, a["L1_ffn_Wk"].rearrange("(i a) d c -> (a d) i c", a=2)).then_inc(raw_in[0], 16)
            sp.dma_start(raw_wv, a["L1_ffn_Wv"].rearrange("(i a) d c -> (a d) i c", a=2)).then_inc(raw_in[0], 16)
            sp.dma_start(raw_wo.rearrange("p i (a d) -> p (i a) d", a=2), a["L1_ffn_Wo"].rearrange("e f d -> f e d")).then_inc(raw_in[0], 16)
            sp.dma_start(raw_gates[:, 0, :], a["L1_ffn_Ws"].rearrange("h e c -> (h e) c")).then_inc(raw_in[0], 16)
            sp.dma_start(raw_gates[:, 1, :], a["L1_ffn_Wd"].rearrange("h e c -> (h e) c")).then_inc(raw_in[0], 16)
            sp.dma_start(W1[:, :], a["L1_attn_Wqkv"]).then_inc(raw_in[0], 16)
            sp.dma_start(Wout[:, :], a["L1_attn_Wout"]).then_inc(raw_in[0], 16)
            sp.dma_start(Wg[:, :, :], a["L0_ffn_Wg"].rearrange("e c f -> c e f")).then_inc(experts_in[0], 16)
            sp.dma_start(Wu[:, :, :], a["L0_ffn_Wu"].rearrange("e c f -> c e f")).then_inc(experts_in[0], 16)
            sp.dma_start(Wd[:, :, :, :], a["L0_ffn_Wd"].rearrange("e (j p) c -> p e j c", p=P)).then_inc(experts_in[0], 16)
            sp.wait_ge(setup_done[0], 1)
            sp.dma_start(row_table, rtab.rearrange("b m c -> b (m c)")).then_inc(table_out[0], 16)
            sp.wait_ge(table_out[0], 16)

            def load(b):
                wait(sp, x3_r, b, 0)
                sp.dma_start(xin[:, :, :], a["L0_attn_x"][bass.ds(b[0] + b[1], 1), :, :].rearrange("o (i p) c -> p (o i) c", p=P)).then_inc(x_in[0], 16)

                sp.dma_start(rows0[:, :, :].rearrange("p m c -> p (m c)"), row_table[bass.ds(b[0] + b[1], 1), 0:3 * P].to_broadcast([P, 3 * P])).then_inc(x_in[0], 16)
                wait(sp, WoutG_r, b, 0)
                sp.dma_start(rows1a[:, :], row_table[bass.ds(b[0] + b[1], 1), 3 * P:4 * P].to_broadcast([P, P])).then_inc(rows1a_in[0], 16)
                yield 1

            def values(b):
                wait(sp, xout_r, b, 0)
                sp.dma_start(rows1b[:, :], row_table[bass.ds(b[0] + b[1], 1), 4 * P:5 * P].to_broadcast([P, P])).then_inc(rows1b_in[0], 16)
                yield MARKS["values"]

            def heads(b):
                yield MARKS["heads"] - 1
                wait(sp, xout_r, b, NT)
                sp.dma_start(out[bass.ds(b[0] + b[1], 1), :, :].rearrange("o (i p) c -> p (o i) c", p=P), xout[:, :, :]).then_inc(stored[0], 16)
                yield MARKS["heads"]

            program(sp, {"load": load, "values": values, "heads": heads})
            sp.wait_ge(stored[0], 16 * NB)

        @block.gpsimd
        def _(g):
            g.memset(ident[:, :], 0.0)
            g.memset(dirs, 0.0)
            g.memset(block8[:, :], 1.0)
            g.memset(block16, 1.0)
            g.memset(head_of8[:, :], 1.0)
            g.memset(head_of16[:, :], 1.0)
            g.memset(causal_bf[:, :], 0.0)
            g.memset(ones_row[:, :], 1.0)
            g.memset(minus_half[:, :], -0.5)
            g.memset(v1[:, :, :, D1:D1 + 1], 1.0)
            g.memset(vals[:, :, :, DS:DS + 1], 1.0)
            for e in range(NE):
                g.memset(first_wins[:, e:e + 1], float(NE - e))
            g.memset(nmax[:, :], 0.0).then_inc(const_g[0], 3)
            g.wait_ge(const_g[0], 3)
            g.affine_select(out=ident[:, :], in_=ident[:, :], compare_op=ALU.not_equal, fill=1.0, base=0,
                            pattern=[[-1, P]], channel_multiplier=1)
            g.affine_select(out=causal_bf[:, :], in_=causal_bf[:, :], compare_op=ALU.is_ge, fill=MASKED, base=0,
                            pattern=[[-1, P]], channel_multiplier=1)

            def cut(tile, n, size, inner, k):
                view = tile.rearrange("p (n s) -> p n s", n=n)
                g.affine_select(out=view, in_=view, compare_op=ALU.is_ge, fill=0.0, base=0,
                                pattern=[[-size, n], [0, inner]], channel_multiplier=1).then_inc(const_g[0], 1)
                g.wait_ge(const_g[0], k)
                g.affine_select(out=view, in_=view, compare_op=ALU.is_ge, fill=0.0, base=size - 1,
                                pattern=[[size, n], [0, inner]], channel_multiplier=-1).then_inc(const_g[0], 1)

            cut(block8[:, :], H0, D0, D0, 4)
            cut(block16, H1, D1, D1, 6)
            cut(head_of8[:, :], H0, D0, 1, 8)
            cut(head_of16[:, :], H1, D1, 1, 10)
            g.wait_ge(const_g[0], 11)
            g.tensor_copy(ident_bf[:, :], ident[:, :]).then_inc(const_g[0], 1)
            g.wait_ge(setup_done[0], 1)

            def rstd_of(b, n):
                wait(g, ln_eps, b, n + 1)
                g.tensor_tensor(rstd[:, :], vareps[:, :], minus_half[:, :], ALU.pow).then_inc(ln_rstd[0], 1)

            def attn0(b):
                rstd_of(b, 0)
                yield 1
                rstd_of(b, 1)
                yield 14
                rstd_of(b, 2)
                wait(g, x2_r, b, 1)
                g.tensor_tensor(x2g, x2[:, :, :], rows0[:, 2:3, :].to_broadcast([P, NT, P]), ALU.mult).then_inc(x2g_r[0], 1)
                wait(g, x2g_r, b, 1)
                wait(g, x_in, b, 32)
                g.tensor_tensor(xg[:, :, :], x2g, xin[:, :, :], ALU.add).then_inc(xg_r[0], 1)
                yield 24

            def moe_in(b):
                rstd_of(b, 3)
                yield 3

            def attn1(b):
                rstd_of(b, 4)
                yield 4
                wait(g, rows1a_in, b, 16)
                wait(g, out1_ps, b, 0)
                g.tensor_tensor(WoutG[:, :], Wout[:, :], rows1a[:, :], ALU.mult).then_inc(WoutG_r[0], 1)
                yield A1 + N1 + 4
                rstd_of(b, 5)
                yield MARKS["attn1"]

            def gates(b):
                yield 1
                for r in range(2):
                    wait(g, topk_v, b, 2 + 5 * r)
                    g.tensor_tensor(cand, eq, first_wins[:, :].unsqueeze(1).to_broadcast([P, 2 * NT * HS, NE]), ALU.mult).then_inc(topk_g[0], 1)
                    yield (2, 4)[r]
                wait(g, sig_v, b, 2)
                wait(g, topk_v, b, 9)
                half = NT * HS
                o1h = oh1[:, 0:half, :]
                o2h = oh2[:, 0:half, :]
                mixf = mixv[:, :, :, :].rearrange("p i h e -> p (i h) e")
                w1 = cand[:, 0:half, :]
                w2 = cand[:, half:2 * half, :]
                g.tensor_tensor(w1, o1h, sig[:, 0, :].unsqueeze(2).to_broadcast([P, half, NE]), ALU.mult).then_inc(mix_g[0], 1)
                g.tensor_tensor(w2, o2h, sig[:, 1, :].unsqueeze(2).to_broadcast([P, half, NE]), ALU.mult).then_inc(mix_g[0], 1)
                wait(g, mix_g, b, 2)
                g.tensor_tensor(mixf, w1, w2, ALU.add).then_inc(mix_g[0], 1)
                yield 5

            def values(b):
                wait(g, mix_g, b, 3)
                wait(g, ym_r, b, 0)
                for n in range(NQ * NT):
                    i, q = n // NQ, n % NQ
                    wait(g, pv_r, b, i + 1)
                    if n >= 2:
                        wait(g, vals_r, b, n - 1)
                    o = prod[:, n % 2, :].rearrange("p (h d e) -> p h d e", h=HQ, e=NE)
                    x0 = pv[:, i % 2, :].rearrange("p (e d) -> p d e", e=NE).unsqueeze(1).to_broadcast([P, HQ, DS, NE])
                    x1 = mixv[:, i, HQ * q:HQ * q + HQ, :].unsqueeze(2).to_broadcast([P, HQ, DS, NE])
                    g.tensor_tensor(o, x0, x1, ALU.mult).then_inc(vprod_r[0], 1)
                    yield n + 1

            def heads(b):
                wait(g, vals_r, b, NQ * NT)
                wait(g, maskB_r, b, 1)
                for i in range(NT):
                    start = (i + 1) * HS + PIECES_AT if i < NT - 1 else N2 + 2
                    yield start - 1
                    wait(g, rden_r, b, i + 1)
                    g.tensor_tensor(coef[:, i % 2, :, :], maskB[:, i, :, :], rden[:, i % 2, :].unsqueeze(2).to_broadcast([P, HS, NE]), ALU.mult).then_inc(coef_r[0], 1)
                    wait(g, coef_r, b, i + 1)
                    for q in range(NQ):
                        n = NQ * i + q
                        if n >= 2:
                            wait(g, ym_r, b, n - 1)
                        o = prod[:, n % 2, :].rearrange("p (d h) -> p d h", h=HS)
                        x0 = oa[:, i % 2, :, 0:DS].rearrange("p h d -> p d h")
                        x1 = coef[:, i % 2, :, q].unsqueeze(1).to_broadcast([P, DS, HS])
                        g.tensor_tensor(o, x0, x1, ALU.mult).then_inc(oprod_r[0], 1)
                        yield start + q

            program(g, {"attn0": attn0, "moe_in": moe_in, "attn1": attn1, "gates": gates, "values": values, "heads": heads})

        @block.tensor
        def _(pe):
            def transposes(dst, src, src_tiles=NT):
                for i in range(src_tiles):
                    last = pe.transpose(dst[:, i * P:(i + 1) * P], src(i), ident[:, :])
                return last

            pe.wait_ge(const_g[0], 12)
            pe.wait_ge(raw_in[0], 16 * 12)
            for n in range((NTURN + 3) // 4):
                part = turns[4 * n:4 * n + 4]
                if n >= 2:
                    pe.wait_ge(setup_v[0], n - 1)
                for i, (src, _) in enumerate(part):
                    last = pe.transpose(bank[n % 2][:, i * P:(i + 1) * P], src, ident[:, :])
                last.then_inc(setup_pe[0], 1)
            n = (NTURN + 3) // 4
            pe.wait_ge(const_v[0], 9)
            pe.wait_ge(small_in[0], 16 * 16)
            for l in range(2):
                pe.transpose(bank[2][:, 8 * l:8 * l + 8], csil[l], ident[0:NB, 0:NB])
            pe.transpose(bank[2][:, 2 * NB:2 * NB + 9], col_rows, ident[0:9, 0:9])
            pe.matmul(bank[3][:, 0:P], sdirs, dirs, start=True, stop=True).then_inc(setup_pe[0], 1)
            pe.wait_ge(setup_v[0], n + 2)
            for l in range(2):
                for m in range(6):
                    last = pe.matmul(bank[4][:, 48 * l + 8 * m:48 * l + 8 * m + 8], wmod[l][:, m * P:(m + 1) * P], cT[l], start=True, stop=True)
            last.then_inc(setup_pe[0], 1)
            pe.matmul(bank[5][:, 0:P], wq1T, bias_m, start=True, stop=True).then_inc(setup_pe[0], 1)
            pe.matmul(bank[6][0:NB, 0:3 * P], cT[0], wmod[0][:, 0:3 * P], start=True, stop=True)
            pe.matmul(bank[7][0:NB, 0:P], cT[1], wmod[1][:, 2 * P:3 * P], start=True, stop=True)
            pe.matmul(bank[7][0:NB, P:2 * P], cT[1], wmod[1][:, 5 * P:6 * P], start=True, stop=True).then_inc(setup_pe[0], 1)
            pe.wait_ge(setup_done[0], 1)
            pe.wait_ge(experts_in[0], 48)

            def ln_turn(b, n, dst):
                wait(pe, ln_n, b, n + 1)
                transposes(dst, lambda i: nrm[:, i, :]).then_inc(ln_T[0], 1)

            def attn0(b):
                yield 3
                ln_turn(b, 1, F0)
                yield 4
                wait(pe, ln_evac, b, 1)
                pe.matmul(F1[:, :], qkvT[:, 0:P], h1T[:, :], start=True, stop=True).then_inc(qkv0_r[0], 1)
                for k, f in enumerate((F2, F3)):
                    for i in range(2):
                        t = 2 * k + i
                        last = pe.matmul(f[:, i * 256:(i + 1) * 256], h1T[:, t * P:(t + 1) * P], qkvT[:, P:3 * P], start=True, stop=True)
                    last.then_inc(qkv0_r[0], 1)
                yield 7
                wait(pe, elu_r, b, 3)
                wait(pe, v0_r, b, 2)
                for i in range(NT):
                    last = pe.matmul(F0[:, 0:P + 1], ke[:, i, :], v0[:, i, :], start=(i == 0), stop=(i == NT - 1))
                last.then_inc(kv_ps[0], 1)
                yield 9
                wait(pe, kv_r, b, 1)
                for k, f in enumerate((F2, F3)):
                    for i in range(2):
                        t = 2 * k + i
                        last = pe.matmul(f[:, i * 256:i * 256 + P + H0], qe[:, t * P:(t + 1) * P], kv[:, :], start=True, stop=True)
                    last.then_inc(num_ps[0], 1)
                yield 11
                wait(pe, att0_r, b, 1)
                transposes(F1, lambda i: att[:, i, :]).then_inc(att0_T[0], 1)
                pe.matmul(F0[:, :], ones_row[:, :], proj_b_row[:, :, :].rearrange("o i c -> o (i c)"), start=True, stop=False, skip_group_check=True)
                yield 12
                wait(pe, attT0_r, b, 1)
                for i in range(NT):
                    last = pe.matmul(F0[:, i * P:(i + 1) * P], attT[:, i * P:(i + 1) * P], projT[:, :], start=False, stop=(i == NT - 1), skip_group_check=True)
                last.then_inc(proj_ps[0], 1)
                yield 15
                ln_turn(b, 2, F1)
                yield 16
                wait(pe, ln_evac, b, 2)
                for j in range(NJ + 1):
                    if j < NJ:
                        if j >= 2:
                            wait(pe, hid_r, b, j - 1)
                        pe.matmul((F2, F3)[j % 2][:, :], fc1T[:, j * P:(j + 1) * P], h2T[:, :], start=True, stop=True).then_inc(fc1_ps[0], 1)
                    if j >= 1:
                        wait(pe, hid_r, b, j)
                        last = pe.matmul(F1[:, :], fc2T[:, j - 1, :], hid[:, j - 1, :], start=(j == 1), stop=(j == NJ))
                    if j < NJ:
                        yield 17 + j
                last.then_inc(fc2_ps[0], 1)
                yield 22
                wait(pe, y0_r, b, 1)
                transposes(F0, lambda i: yS[:, i * P:(i + 1) * P]).then_inc(y0_T[0], 1)
                yield 24

            h2T = h1T

            def moe_in(b):
                yield 2
                ln_turn(b, 3, F1)
                yield 3

            def experts(b):
                hbT = h1T
                n_all = NE * NJ
                wait(pe, ln_evac, b, 3)
                wait(pe, x3_r, b, 1)
                for n in range(n_all + 1):
                    if n < n_all:
                        e, j = n // NJ, n % NJ
                        if n >= 1:
                            wait(pe, silu_r, b, n)
                        pe.matmul(F0[:, :], Wg[:, e, j * P:(j + 1) * P], hbT[:, :], start=True, stop=True).then_inc(gu_g[0], 1)
                        if n >= 2:
                            wait(pe, act_r, b, n - 1)
                        pe.matmul((F2, F3)[n % 2][:, :], Wu[:, e, j * P:(j + 1) * P], hbT[:, :], start=True, stop=True).then_inc(gu_u[0], 1)
                    if n >= 1:
                        e, j = (n - 1) // NJ, (n - 1) % NJ
                        wait(pe, act_r, b, n)
                        pe.matmul(F1[:, :], Wd[:, e, j, :], act[:, (n - 1) % 2, :], start=(n == 1), stop=(n == n_all)).then_inc(down_ps[0], 1)
                    yield n + 1
                wait(pe, y1_r, b, 1)
                transposes(F0, lambda i: yS[:, i * P:(i + 1) * P]).then_inc(y1_T[0], 1)
                yield MARKS["experts"]

            def attn1(b):
                yield 2
                ln_turn(b, 4, F1)
                yield 3
                wait(pe, ln_evac, b, 4)
                wait(pe, x4_r, b, 1)
                hcT = h1T
                pe.matmul(F0[:, :], W1[:, 0:P], hcT[:, :], start=True, stop=True).then_inc(qkv1_ps[0], 1)
                pe.matmul(F2[:, :], W1[:, P:2 * P], hcT[:, :], start=True, stop=True).then_inc(qkv1_ps[0], 1)
                for i in range(NT):
                    last = pe.matmul(F3[:, i * P:(i + 1) * P], hcT[:, i * P:(i + 1) * P], W1[:, 2 * P:3 * P], start=True, stop=True)
                last.then_inc(qkv1_ps[0], 1)
                yield A1
                wait(pe, q1_r, b, 1)
                wait(pe, v1_r, b, 1)
                for n in range(N1 + 2):
                    if n < N1:
                        i, h = n // H1, n % H1
                        w = (i + 1) * P
                        f = (F0, F2)[n % 2]
                        if i == 0:
                            wait(pe, k1z_r, b, h + 1)
                        if n >= 2:
                            wait(pe, p1_r, b, n - 1)
                        pe.matmul(f[:, 0:w], q1T[:, i * P:(i + 1) * P], k1z[:, h, 0:w], start=True, stop=False, skip_group_check=True)
                        pe.matmul(f[:, w - P:w], ident_bf[:, :], causal_bf[:, :], start=False, stop=True, skip_group_check=True).then_inc(s1_ps[0], 1)
                    if 1 <= n <= N1:
                        m = n - 1
                        i = m // H1
                        wait(pe, p1_r, b, m + 1)
                        if m >= 1:
                            wait(pe, p1T_r, b, m)
                        transposes(F3, lambda j: p1[:, m % 2, j * P:(j + 1) * P], i + 1).then_inc(p1_T[0], 1)
                    if n >= 2:
                        m = n - 2
                        i, h = m // H1, m % H1
                        if h == 0 and i >= 1:
                            wait(pe, o1_r, b, i)
                        wait(pe, p1T_r, b, m + 1)
                        for j in range(i + 1):
                            last = pe.matmul(F1[:, h * (D1 + 1):(h + 1) * (D1 + 1)], p1T[:, m % 2, j * P:(j + 1) * P], v1[:, j, h, :], start=(j == 0), stop=(j == i))
                        if h == H1 - 1:
                            last.then_inc(o1_ps[0], 1)
                    yield A1 + 1 + n
                yield A1 + N1 + 3
                wait(pe, att1_r, b, 1)
                transposes(F0, lambda i: att[:, i, :]).then_inc(att1_T[0], 1)
                yield A1 + N1 + 4
                wait(pe, attT1_r, b, 1)
                wait(pe, WoutG_r, b, 1)
                for i in range(NT):
                    last = pe.matmul(F2[:, i * P:(i + 1) * P], attT[:, i * P:(i + 1) * P], WoutG[:, :], start=True, stop=True)
                last.then_inc(out1_ps[0], 1)
                yield A1 + N1 + 7
                ln_turn(b, 5, F1)
                yield MARKS["attn1"]

            def gates(b):
                wait(pe, ln_evac, b, 5)
                wait(pe, x5_r, b, 1)
                for k, f in enumerate((F0, F2)):
                    for i in range(2):
                        t = 2 * k + i
                        last = pe.matmul(f[:, i * 256:(i + 1) * 256], hdT[:, t * P:(t + 1) * P], gatesT[:, :], start=True, stop=True)
                    last.then_inc(gate_ps[0], 1)
                yield 5

            def values(b):
                wait(pe, p_r, b, 0)
                for n in range(NQ * NT):
                    if n == 0:
                        for i in range(2):
                            pe.matmul((S0, S1)[i][:, :], hdT[:, i * P:(i + 1) * P], WvT[:, :], start=True, stop=True).then_inc(pv_ps[0], 1)
                    if n % NQ == 0 and n // NQ in (1, 2):
                        i = n // NQ + 1
                        wait(pe, pv_r, b, i - 1)
                        pe.matmul((S0, S1)[i % 2][:, :], hdT[:, i * P:(i + 1) * P], WvT[:, :], start=True, stop=True).then_inc(pv_ps[0], 1)
                    if n % 4 == 2:
                        p = n // 4
                        if p == 0:
                            wait(pe, hdB_r, b, 1)
                            wait(pe, resg_r, b, 0)
                            wait(pe, oa_r, b, 0)
                        if p >= 2:
                            wait(pe, ks_r, b, p - 1)
                        pe.matmul((TB, OB)[p % 2][:, :], WkT[:, p * P:(p + 1) * P], hdB[:, :], start=True, stop=True).then_inc(k_ps[0], 1)
                    yield n + 1

            def heads(b):
                wait(pe, ks_r, b, NP)
                wait(pe, pv_r, b, NT)

                def queries(i, before):
                    for half in range(2):
                        if half:
                            wait(pe, qs_r, b, 2 * i + 1)
                        elif before is not None:
                            wait(pe, pT_r[before % 2], b, before // 2 + 1)
                        for p in range(4 * half, 4 * half + 4):
                            last = pe.matmul(TB[:, (p % 4) * P:(p % 4 + 1) * P], WqT[:, p * P:(p + 1) * P], hdB[:, i * P:(i + 1) * P], start=True, stop=True)
                        last.then_inc(q_ps[0], 1)
                    wait(pe, qs_r, b, 2 * i + 2)

                def mixed_out(i, before):
                    wait(pe, ym_r, b, NQ * (i + 1))
                    wait(pe, pT_r[before % 2], b, before // 2 + 1)
                    transposes(TB, lambda j: ym[:, j * P:(j + 1) * P]).then_inc(ym_T[0], 1)
                    wait(pe, ymT_r, b, i + 1)
                    for j in range(NJ):
                        last = pe.matmul(TB[:, 0:P], ymT[:, j, :], WoT[:, j, :], start=(j == 0), stop=(j == NJ - 1))
                    last.then_inc(res_ps[0], 1)
                    wait(pe, resg_r, b, i + 1)

                queries(0, None)
                for n in range(N2 + 2):
                    if n % HS == MIXED_AT and n > HS:
                        mixed_out(n // HS - 1, n - 2)
                    if n < N2:
                        i, h = n // HS, n % HS
                        r = 64 * (h % 2)
                        if n >= 2:
                            wait(pe, p_r, b, n - 1)
                        pe.matmul((S0, S1)[n % 2][:, :], qsT[r:r + DS, i % 2, h // 2, :], ksT[r:r + DS, h // 2, :], start=True, stop=True).then_inc(s_ps[0], 1)
                    if n % HS == QUERIES_AT and n < N2 - HS:
                        queries(n // HS + 1, n - 2)
                    if 1 <= n <= N2:
                        m = n - 1
                        wait(pe, p_r, b, m + 1)
                        if m >= 1:
                            wait(pe, pT_r[(m - 1) % 2], b, (m - 1) // 2 + 1)
                        transposes(TB, lambda j: pr[:, m % 2, j * P:(j + 1) * P]).then_inc(p_T[0], 1)
                    if n == 2:
                        wait(pe, vals_r, b, NQ * NT)
                    if n >= 2:
                        m = n - 2
                        i, h = m // HS, m % HS
                        if h % GROUP == 0 and m >= GROUP:
                            wait(pe, oa_r, b, m // GROUP)
                        wait(pe, pT_r[m % 2], b, m // 2 + 1)
                        for j in range(NT):
                            last = pe.matmul(OB[:, (h % GROUP) * VW:(h % GROUP + 1) * VW], prT[:, m % 2, j * P:(j + 1) * P], vals[:, j, h, :], start=(j == 0), stop=(j == NT - 1))
                        if h % GROUP == GROUP - 1:
                            last.then_inc(o_ps[0], 1)
                    yield n + 1
                yield N2 + 2 + NQ
                mixed_out(NT - 1, N2 - 1)
                yield MARKS["heads"]

            program(pe, {"attn0": attn0, "moe_in": moe_in, "experts": experts, "attn1": attn1, "gates": gates,
                      "values": values, "heads": heads})

        @block.scalar
        def _(s):
            s.wait_ge(small_in[0], 16 * 16)
            for l in range(2):
                s.activation(cexp[l], crow[l], ACT.Exp, scale=-1.0).then_inc(const_v[0], 1)
            s.wait_ge(setup_done[0], 1)

            def ln_out(b, n, dst, src, scale, bias):
                wait(s, ln_T, b, n)
                s.activation(dst, src, ACT.Identity, scale=scale, bias=bias).then_inc(ln_evac[0], 1)

            def attn0(b):
                yield 3
                ln_out(b, 1, h1T[:, :], F0[:, :], cols[:, 0:1], cols[:, 1:2])
                yield 5
                wait(s, emin_r, b, 1)
                s.activation(qexp, qmin, ACT.Exp).then_inc(eexp_r[0], 1)
                for k in range(2):
                    wait(s, emin_r, b, 2 + k)
                    s.activation(kexp[:, 2 * k:2 * k + 2, :], kmin[:, 2 * k:2 * k + 2, :], ACT.Exp).then_inc(eexp_r[0], 1)
                    s.activation(v0[:, 2 * k:2 * k + 2, 0:P], (F2, F3)[k][:, :].rearrange("p (i c) -> p i c", i=2)[:, :, P:2 * P], ACT.Copy).then_inc(v0_r[0], 1)
                yield 11
                wait(s, att0_T, b, 1)
                s.activation(attT[:, :], F1[:, :], ACT.Copy).then_inc(attT0_r[0], 1)
                yield 15
                ln_out(b, 2, h1T[:, :], F1[:, :], cols[:, 2:3], cols[:, 3:4])
                yield 16
                for j in range(NJ):
                    wait(s, fc1_ps, b, j + 1)
                    s.activation(hid[:, j, :], (F2, F3)[j % 2][:, :], ACT.Gelu, bias=cols[:, 4 + j:5 + j]).then_inc(hid_r[0], 1)
                    yield 17 + j
                yield 24

            def moe_in(b):
                yield 2
                wait(s, modB_r, b, 1)
                ln_out(b, 3, h1T[:, :], F1[:, :], modB[:, CB0:CB0 + 1], modB[:, SB0:SB0 + 1])
                yield 3

            def experts(b):
                for n in range(NE * NJ):
                    wait(s, gu_g, b, n + 1)
                    if n >= 2:
                        wait(s, act_r, b, n - 1)
                    s.activation(silu[:, n % 2, :], F0[:, :], ACT.Silu).then_inc(silu_r[0], 1)
                    yield n + 1
                yield MARKS["experts"]

            def attn1(b):
                yield 2
                ln_out(b, 4, h1T[:, :], F1[:, :], modB[:, CA1:CA1 + 1], modB[:, SA1:SA1 + 1])
                yield 3
                wait(s, qkv1_ps, b, 1)
                s.activation(q1T[:, :], F0[:, :], ACT.Copy).then_inc(q1_r[0], 1)
                wait(s, qkv1_ps, b, 3)
                s.activation(v1[:, :, :, 0:D1], F3[:, :].rearrange("p (i h d) -> p i h d", i=NT, h=H1), ACT.Copy).then_inc(v1_r[0], 1)
                wait(s, k1_r, b, 1)
                for h in range(H1):
                    s.activation(k1z[:, h, :], k1T, ACT.Copy, scale=head_of16[:, h:h + 1]).then_inc(k1z_r[0], 1)
                    yield 4 if h < 4 else A1
                for n in range(N1 + 1):
                    if n < N1:
                        w = (n // H1 + 1) * P
                        wait(s, nmax1_r, b, n + 1)
                        if n >= 2:
                            wait(s, p1_T, b, n - 1)
                        s.activation(p1[:, n % 2, 0:w], (F0, F2)[n % 2][:, 0:w], ACT.Exp, bias=nmax1[:, n % 2:n % 2 + 1]).then_inc(p1_r[0], 1)
                    if n >= 1:
                        m = n - 1
                        w = (m // H1 + 1) * P
                        wait(s, p1_T, b, m + 1)
                        s.activation(p1T[:, m % 2, 0:w], F3[:, 0:w], ACT.Copy).then_inc(p1T_r[0], 1)
                    yield A1 + 1 + n
                yield A1 + N1 + 3
                wait(s, att1_T, b, 1)
                s.activation(attT[:, :], F0[:, :], ACT.Copy).then_inc(attT1_r[0], 1)
                yield A1 + N1 + 7
                wait(s, pv_ps, b, 0)
                ln_out(b, 5, hdT[:, :], F1[:, :], modB[:, CB1:CB1 + 1], modB[:, SB1:SB1 + 1])
                yield MARKS["attn1"]

            def gates(b):
                for k, f in enumerate((F0, F2)):
                    wait(s, gate_ps, b, k + 1)
                    for i in range(2):
                        last = s.activation(gate[:, :, 2 * k + i, :, :].rearrange("p g h e -> p g (h e)"),
                                            f[:, i * 256:(i + 1) * 256].rearrange("p (g c) -> p g c", g=2), ACT.Copy)
                    last.then_inc(gate_r[0], 1)
                yield 3
                wait(s, topk_v, b, 6)
                s.activation(sigd[:, :, :], top[:, :, 0:NT * HS], ACT.Exp, scale=-1.0).then_inc(sig_e[0], 1)
                yield 5

            def values(b):
                wait(s, vprod_r, b, 0)
                for n in range(NQ * NT):
                    if n % NQ == 0:
                        for i in (0, 1) if n == 0 else (n // NQ + 1,) if n // NQ < NT - 1 else ():
                            wait(s, pv_ps, b, i + 1)
                            if i >= 2:
                                wait(s, vprod_r, b, NQ * (i - 1))
                            s.activation(pv[:, i % 2, :], (S0, S1)[i % 2][:, :], ACT.Copy).then_inc(pv_r[0], 1)
                    if n == 0:
                        wait(s, q_ps, b, 0)
                        s.activation(hdB[:, :], hdT[:, :], ACT.Copy).then_inc(hdB_r[0], 1)
                        wait(s, coef_r, b, 0)
                        wait(s, masko_r, b, 1)
                        s.activation(maskB[:, :, :, :].rearrange("p i h e -> p (i h e)"), masko[:, :, :, :].rearrange("p i h e -> p (i h e)"), ACT.Copy).then_inc(maskB_r[0], 1)
                    if n == NQ * NT // 2:
                        wait(s, stored, b, 0)
                        s.activation(xout[:, :, :], x5[:, :, :], ACT.Copy).then_inc(xcopy_r[0], 1)
                    yield n + 1

            def heads(b):
                def queries(i):
                    for half in range(2):
                        wait(s, q_ps, b, 2 * i + half + 1)
                        s.activation(qsT[:, i % 2, 4 * half:4 * half + 4, :].rearrange("p a t -> p (a t)"), TB[:, :], ACT.Copy).then_inc(qs_r[0], 1)

                def mixed(i):
                    wait(s, ym_T, b, i + 1)
                    s.activation(ymT[:, :, :].rearrange("p j t -> p (j t)"), TB[:, :], ACT.Copy).then_inc(ymT_r[0], 1)

                queries(0)
                for n in range(N2 + 2):
                    if n % HS == MIXED_AT and n > HS:
                        mixed(n // HS - 1)
                    if n % HS == QUERIES_AT and n < N2 - HS:
                        queries(n // HS + 1)
                    if n < N2:
                        wait(s, nmax_r, b, n + 1)
                        if n >= 2:
                            wait(s, p_T, b, n - 1)
                        s.activation(pr[:, n % 2, :], (S0, S1)[n % 2][:, :], ACT.Exp, bias=nmax[:, n % 2:n % 2 + 1]).then_inc(p_r[0], 1)
                    if 1 <= n <= N2 and (n - 1) % 2:
                        wait(s, p_T, b, n)
                        s.activation(prT[:, 1, :], TB[:, :], ACT.Copy).then_inc(pT_r[1][0], 1)
                    yield n + 1
                yield N2 + 2 + NQ
                mixed(NT - 1)
                yield MARKS["heads"]

            program(s, {"attn0": attn0, "moe_in": moe_in, "experts": experts, "attn1": attn1, "gates": gates,
                     "values": values, "heads": heads})

        @block.vector
        def _(v):
            v.wait_ge(small_in[0], 16 * 16)
            v.wait_ge(const_v[0], 2)
            for l in range(2):
                v.tensor_scalar(cexp[l], cexp[l], 1.0, None, ALU.add)
            v.tensor_tensor(sdirs.rearrange("o (h d) -> o h d", h=H1), dirs.rearrange("o (h d) -> o h d", h=H1),
                            scales.unsqueeze(2).to_broadcast([1, H1, D1]), ALU.mult).then_inc(const_v[0], 3)
            v.wait_ge(const_v[0], 5)
            for l in range(2):
                last = v.reciprocal(crec[l], cexp[l])
            last.then_inc(const_v[0], 2)
            v.wait_ge(const_v[0], 7)
            for l in range(2):
                last = v.tensor_tensor(csil[l], crow[l], crec[l], ALU.mult)
            last.then_inc(const_v[0], 2)
            for n in range((NTURN + 3) // 4):
                part = turns[4 * n:4 * n + 4]
                v.wait_ge(setup_pe[0], n + 1)
                for i, (_, dst) in enumerate(part):
                    src = bank[n % 2][:, i * P:(i + 1) * P]
                    if 12 <= 4 * n + i < 20:
                        last = v.tensor_scalar(dst, src, DS ** -0.5, None, ALU.mult)
                    else:
                        last = v.tensor_copy(dst, src)
                last.then_inc(setup_v[0], 1)
            n = (NTURN + 3) // 4
            v.wait_ge(setup_pe[0], n + 1)
            v.tensor_copy(ksT[:, 6, 0:2 * NB], bank[2][:, 0:2 * NB])
            v.tensor_copy(cols[:, :], bank[2][:, 2 * NB:2 * NB + 9])
            v.wait_ge(const_g[0], 12)
            v.tensor_tensor(bias_m, bank[3][:, 0:P], block16, ALU.mult).then_inc(setup_v[0], 1)
            v.wait_ge(setup_v[0], n + 1)
            v.scalar_tensor_tensor(out=bias_m, in0=ident[:, :], scalar=D1 ** -0.5, in1=bias_m, op0=ALU.mult, op1=ALU.add).then_inc(setup_v[0], 1)
            v.wait_ge(setup_pe[0], n + 2)
            v.tensor_copy(mod[:, :, :].rearrange("p b m -> p m b"), bank[4][:, 0:96].rearrange("p (m b) -> p m b", m=12)).then_inc(setup_v[0], 1)
            v.wait_ge(setup_pe[0], n + 3)
            v.tensor_copy(W1[:, 0:P], bank[5][:, 0:P])

            def floor_gate(g, s, w, k):
                v.tensor_scalar(s, g, 0.0, 2.0, ALU.is_ge, ALU.mult).then_inc(setup_v[0], 1)
                v.wait_ge(setup_v[0], k + 1)
                v.tensor_scalar(s, s, -1.0, None, ALU.add).then_inc(setup_v[0], 1)
                v.wait_ge(setup_v[0], k + 2)
                v.tensor_tensor(w, g, s, ALU.mult).then_inc(setup_v[0], 1)
                v.wait_ge(setup_v[0], k + 3)
                v.tensor_scalar(w, w, 0.25, None, ALU.max).then_inc(setup_v[0], 1)
                v.wait_ge(setup_v[0], k + 4)
                v.tensor_tensor(g, w, s, ALU.mult).then_inc(setup_v[0], 1)
                v.wait_ge(setup_v[0], k + 5)

            v.wait_ge(setup_v[0], n + 3)
            k = n + 3
            for m in (CA0, CB0, CA1, CB1):
                v.tensor_scalar(mod[:, :, m], mod[:, :, m], 1.0, None, ALU.add)
            for m in (GA0, GB0, GA1, GB1):
                floor_gate(mod[:, :, m], sgn[:, 0:NB], gab[:, 0:NB], k)
                k += 5
            v.wait_ge(setup_pe[0], n + 4)
            v.tensor_copy(rtab[:, 0:3, :].rearrange("p m c -> p (m c)"), bank[6][0:NB, 0:3 * P])
            v.tensor_copy(rtab[:, 3:5, :].rearrange("p m c -> p (m c)"), bank[7][0:NB, 0:2 * P]).then_inc(setup_v[0], 1)
            k += 1
            v.wait_ge(setup_v[0], k)
            v.tensor_scalar(rtab[:, 1, :], rtab[:, 1, :], 1.0, None, ALU.add)
            for m in (2, 3, 4):
                floor_gate(rtab[:, m, :], rsgn, rabs, k)
                k += 5
            v.memset(nmax1[:, :], 0.0).then_inc(setup_done[0], 1)

            def stats_of(b, n, src):
                for i in range(NT):
                    last = v.bn_stats(stats[:, i, :], src[:, i, :])
                last.then_inc(ln_stats[0], 1)
                wait(v, ln_stats, b, n + 1)
                v.memset(pause[:, :], 0.0)
                for i in range(NT):
                    last = v.bn_aggr(mv[:, i, :], stats[:, i, :])
                last.then_inc(ln_mv[0], 1)
                wait(v, ln_mv, b, n + 1)
                v.tensor_scalar(vareps[:, :], mv[:, :, 1], EPS_LN, None, ALU.add).then_inc(ln_eps[0], 1)

            def norm_of(b, n, src):
                wait(v, ln_rstd, b, n + 1)
                for i in range(NT):
                    last = v.tensor_scalar(nrm[:, i, :], src[:, i, :], mv[:, i, 0:1], rstd[:, i:i + 1], ALU.subtract, ALU.mult)
                last.then_inc(ln_n[0], 1)

            def attn0(b):
                wait(v, x5_r, b, 0)
                v.tensor_scalar(modA[:, :], mod[:, bass.ds(b[0] + b[1], 1), :].rearrange("p o m -> p (o m)"), 1.0, None, ALU.mult).then_inc(modA_r[0], 1)
                wait(v, x_in, b, 32)
                stats_of(b, 0, xin)
                yield 1
                norm_of(b, 0, xin)
                wait(v, ln_n, b, 1)
                wait(v, mix_g, b, 0)
                v.tensor_tensor(h0m, nrm[:, :, :], rows0[:, 1:2, :].to_broadcast([P, NT, P]), ALU.mult).then_inc(h0m_r[0], 1)
                wait(v, h0m_r, b, 1)
                v.tensor_tensor(h0[:, :, :], h0m, rows0[:, 0:1, :].to_broadcast([P, NT, P]), ALU.add).then_inc(h0_r[0], 1)
                wait(v, h0_r, b, 1)
                stats_of(b, 1, h0)
                yield 2
                norm_of(b, 1, h0)
                yield 5
                kview = [f[:, :].rearrange("p (i c) -> p i c", i=2)[:, :, 0:P] for f in (F2, F3)]
                wait(v, qkv0_r, b, 1)
                v.tensor_scalar(qmin, F1[:, :], 0.0, None, ALU.min).then_inc(emin_r[0], 1)
                for k in range(2):
                    wait(v, qkv0_r, b, 2 + k)
                    v.tensor_scalar(kmin[:, 2 * k:2 * k + 2, :], kview[k], 0.0, None, ALU.min).then_inc(emin_r[0], 1)
                yield 6
                v.memset(v0[:, :, P:P + 1], 1.0)
                wait(v, eexp_r, b, 1)
                v.scalar_tensor_tensor(out=qe, in0=F1[:, :], scalar=0.0, in1=qexp, op0=ALU.max, op1=ALU.add).then_inc(elu_r[0], 1)
                for k in range(2):
                    wait(v, eexp_r, b, 2 + k)
                    wait(v, v0_r, b, 1 + k)
                    v.scalar_tensor_tensor(out=ke[:, 2 * k:2 * k + 2, :], in0=kview[k], scalar=0.0, in1=kexp[:, 2 * k:2 * k + 2, :], op0=ALU.max, op1=ALU.add).then_inc(elu_r[0], 1)
                yield 8
                wait(v, kv_ps, b, 1)
                v.tensor_tensor(kv[:, 0:P], F0[:, 0:P], block8[:, :], ALU.mult)
                v.tensor_scalar(kv[:, P:P + H0], head_of8[:, :], F0[:, P:P + 1], None, ALU.mult).then_inc(kv_r[0], 1)
                yield 10
                nview = [f[:, :].rearrange("p (i c) -> p i c", i=2) for f in (F2, F3)]
                wait(v, num_ps, b, 2)
                for k in range(2):
                    last = v.tensor_scalar(den0[:, 2 * k:2 * k + 2, :], nview[k][:, :, P:P + H0], EPS_ATTN, None, ALU.add)
                last.then_inc(den0_r[0], 1)
                wait(v, den0_r, b, 1)
                v.reciprocal(rden0[:, :, :], den0[:, :, :]).then_inc(rden0_r[0], 1)
                wait(v, rden0_r, b, 1)
                for t in range(NT):
                    last = v.tensor_tensor(att[:, t, :].rearrange("p (h d) -> p h d", h=H0),
                                           nview[t // 2][:, t % 2, 0:P].rearrange("p (h d) -> p h d", h=H0),
                                           rden0[:, t, :].unsqueeze(2).to_broadcast([P, H0, D0]), ALU.mult)
                last.then_inc(att0_r[0], 1)
                yield 13
                wait(v, proj_ps, b, 1)
                v.tensor_tensor(x2[:, :, :], tiles(F0), h0[:, :, :], ALU.add).then_inc(x2_r[0], 1)
                wait(v, x2_r, b, 1)
                stats_of(b, 2, x2)
                yield 14
                norm_of(b, 2, x2)
                yield 21
                wait(v, fc2_ps, b, 1)
                v.tensor_scalar(yS, F1[:, :], cols[:, 8:9], modA[:, GA0:GA0 + 1], ALU.add, ALU.mult).then_inc(y0_r[0], 1)
                yield 23
                wait(v, y0_T, b, 1)
                wait(v, xg_r, b, 1)
                v.tensor_tensor(x3[:, :, :], tiles(F0), xg[:, :, :], ALU.add).then_inc(x3_r[0], 1)
                yield 24

            def moe_in(b):
                wait(v, ln_evac, b, 0)
                v.tensor_scalar(modB[:, :], mod[:, bass.ds(b[0] + b[1], 1), :].rearrange("p o m -> p (o m)"), 1.0, None, ALU.mult).then_inc(modB_r[0], 1)
                wait(v, x3_r, b, 1)
                stats_of(b, 3, x3)
                yield 1
                norm_of(b, 3, x3)
                yield 3

            def experts(b):
                for n in range(NE * NJ):
                    wait(v, silu_r, b, n + 1)
                    wait(v, gu_u, b, n + 1)
                    if n >= 2:
                        wait(v, down_ps, b, n - 1)
                    v.tensor_tensor(act[:, n % 2, :], (F2, F3)[n % 2][:, :], silu[:, n % 2, :], ALU.mult).then_inc(act_r[0], 1)
                    yield n + 1
                wait(v, down_ps, b, NE * NJ)
                v.tensor_scalar(yS, F1[:, :], modB[:, GB0:GB0 + 1], None, ALU.mult).then_inc(y1_r[0], 1)
                yield NE * NJ + 1
                wait(v, y1_T, b, 1)
                v.tensor_tensor(x4[:, :, :], tiles(F0), x3[:, :, :], ALU.add).then_inc(x4_r[0], 1)
                yield MARKS["experts"]

            def attn1(b):
                wait(v, x4_r, b, 1)
                stats_of(b, 4, x4)
                yield 1
                norm_of(b, 4, x4)
                yield 3
                wait(v, qkv1_ps, b, 2)
                v.tensor_copy(k1T, F2[:, :]).then_inc(k1_r[0], 1)
                yield A1
                for n in range(N1 + 2):
                    if n >= H1 + 2 and n % H1 == 2:
                        i = n // H1 - 1
                        wait(v, o1_ps, b, i + 1)
                        v.tensor_copy(o1[:, i, :, :].rearrange("p h d -> p (h d)"), F1[:, 0:H1 * (D1 + 1)]).then_inc(o1_r[0], 1)
                    if n < N1:
                        w = (n // H1 + 1) * P
                        wait(v, s1_ps, b, n + 1)
                        if n >= 2:
                            wait(v, p1_r, b, n - 1)
                        v.tensor_reduce(nmax1[:, n % 2:n % 2 + 1], (F0, F2)[n % 2][:, 0:w], X_AXIS, ALU.max, negate=True).then_inc(nmax1_r[0], 1)
                    yield A1 + 1 + n
                wait(v, o1_ps, b, NT)
                v.tensor_copy(o1[:, NT - 1, :, :].rearrange("p h d -> p (h d)"), F1[:, 0:H1 * (D1 + 1)]).then_inc(o1_r[0], 1)
                wait(v, o1_r, b, NT)
                v.reciprocal(rden1[:, :, :], o1[:, :, :, D1]).then_inc(rden1_r[0], 1)
                wait(v, rden1_r, b, 1)
                v.tensor_tensor(att[:, :, :].rearrange("p i (h d) -> p i h d", h=H1), o1[:, :, :, 0:D1],
                                rden1[:, :, :].unsqueeze(3).to_broadcast([P, NT, H1, D1]), ALU.mult).then_inc(att1_r[0], 1)
                yield A1 + N1 + 5
                wait(v, out1_ps, b, 1)
                wait(v, xcopy_r, b, 0)
                v.tensor_tensor(x5[:, :, :], tiles(F2), x4[:, :, :], ALU.add).then_inc(x5_r[0], 1)
                wait(v, x5_r, b, 1)
                stats_of(b, 5, x5)
                yield A1 + N1 + 6
                norm_of(b, 5, x5)
                yield MARKS["attn1"]

            def gates(b):
                g = gate.rearrange("p g i h e -> p (g i h) e")
                n = 2 * NT * HS
                half = NT * HS

                def wide(t):
                    return t.unsqueeze(2).to_broadcast([P, n, NE])

                yield 1
                wait(v, gate_r, b, 2)
                v.tensor_reduce(top[:, 0, :], g, X_AXIS, ALU.max).then_inc(topk_v[0], 1)
                for r in range(2):
                    one = (oh1, oh2)[r]
                    k = 5 * r
                    wait(v, topk_v, b, k + 1)
                    v.tensor_tensor(eq, g, wide(top[:, r, :]), ALU.is_ge).then_inc(topk_v[0], 1)
                    yield 2 + 2 * r
                    wait(v, topk_g, b, r + 1)
                    v.tensor_reduce(pick[:, :], cand, X_AXIS, ALU.max).then_inc(topk_v[0], 1)
                    wait(v, topk_v, b, k + 3)
                    v.tensor_tensor(one, cand, wide(pick[:, :]), ALU.is_equal).then_inc(topk_v[0], 1)
                    if r == 0:
                        wait(v, topk_v, b, 4)
                        v.scalar_tensor_tensor(out=g, in0=oh1, scalar=-BIG, in1=g, op0=ALU.mult, op1=ALU.add).then_inc(topk_v[0], 1)
                        wait(v, topk_v, b, 5)
                        v.tensor_reduce(top[:, 1, :], g, X_AXIS, ALU.max).then_inc(topk_v[0], 1)
                        yield 3
                wait(v, sig_e, b, 1)
                v.tensor_scalar(sigd[:, :, :], sigd[:, :, :], 1.0, None, ALU.add).then_inc(sig_v[0], 1)
                wait(v, sig_v, b, 1)
                v.reciprocal(sig[:, :, :], sigd[:, :, :]).then_inc(sig_v[0], 1)
                wait(v, topk_v, b, 9)
                wait(v, maskB_r, b, 0)
                v.tensor_tensor(masko[:, :, :, :].rearrange("p i h e -> p (i h) e"), oh1[:, half:n, :], oh2[:, half:n, :], ALU.add).then_inc(masko_r[0], 1)
                yield 5

            def values(b):
                for n in range(NQ * NT):
                    i, q = n // NQ, n % NQ
                    wait(v, vprod_r, b, n + 1)
                    v.tensor_reduce(vals[:, i, HQ * q:HQ * q + HQ, 0:DS], prod[:, n % 2, :].rearrange("p (h d e) -> p h d e", h=HQ, e=NE), X_AXIS, ALU.add).then_inc(vals_r[0], 1)
                    if n % 4 == 3:
                        p = n // 4
                        wait(v, k_ps, b, p + 1)
                        v.tensor_copy(ksT[:, p, :], (TB, OB)[p % 2][:, :]).then_inc(ks_r[0], 1)
                    yield n + 1

            def heads(b):
                def piece(n):
                    wait(v, oprod_r, b, n + 1)
                    if n % NQ == 0:
                        wait(v, ym_T, b, n // NQ)
                    v.tensor_reduce(ym[:, (n % NQ) * DS:(n % NQ + 1) * DS], prod[:, n % 2, :].rearrange("p (d h) -> p d h", h=HS), X_AXIS, ALU.add).then_inc(ym_r[0], 1)

                def out_tile(i):
                    wait(v, res_ps, b, i + 1)
                    v.tensor_tensor(resg[:, :], TB[:, 0:P], rows1b[:, :], ALU.mult).then_inc(resg_r[0], 1)
                    wait(v, resg_r, b, i + 1)
                    v.tensor_tensor(xout[:, i, :], resg[:, :], xout[:, i, :], ALU.add).then_inc(xout_r[0], 1)

                def collect(c):
                    wait(v, o_ps, b, c + 1)
                    i = c // NG
                    if c % NG == 0 and i >= 2:
                        wait(v, oprod_r, b, NQ * (i - 1))
                    v.tensor_copy(oa[:, i % 2, GROUP * (c % NG):GROUP * (c % NG + 1), :].rearrange("p h d -> p (h d)"), OB[:, 0:GROUP * VW]).then_inc(oa_r[0], 1)
                    if c % NG == NG - 1:
                        wait(v, oa_r, b, c + 1)
                        v.reciprocal(rden[:, i % 2, :], oa[:, i % 2, :, DS]).then_inc(rden_r[0], 1)

                wait(v, rows1b_in, b, 16)
                wait(v, xcopy_r, b, 1)
                for n in range(N2 + 2):
                    if n > GROUP and n % GROUP == 2:
                        collect(n // GROUP - 1)
                    if n % HS == MIXED_AT and n > HS:
                        out_tile(n // HS - 1)
                    if n < N2:
                        wait(v, s_ps, b, n + 1)
                        if n >= 2:
                            wait(v, p_r, b, n - 1)
                        v.tensor_reduce(nmax[:, n % 2:n % 2 + 1], (S0, S1)[n % 2][:, :], X_AXIS, ALU.max, negate=True).then_inc(nmax_r[0], 1)
                    if 1 <= n <= N2 and (n - 1) % 2 == 0:
                        wait(v, p_T, b, n)
                        v.tensor_copy(prT[:, 0, :], TB[:, :]).then_inc(pT_r[0][0], 1)
                    if n > HS and PIECES_AT < n % HS + 1 <= PIECES_AT + NQ:
                        piece(NQ * (n // HS - 1) + n % HS - PIECES_AT)
                    if n == N2 + 1:
                        collect(NT * NG - 1)
                    yield n + 1
                for q in range(NQ):
                    piece(NQ * (NT - 1) + q)
                    yield N2 + 3 + q
                out_tile(NT - 1)
                yield MARKS["heads"]

            program(v, {"attn0": attn0, "moe_in": moe_in, "experts": experts, "attn1": attn1, "gates": gates,
                     "values": values, "heads": heads})


NAMES = ['L0_attn_x', 'L0_attn_norm1_g', 'L0_attn_norm1_b', 'L0_attn_qkv_w', 'L0_attn_proj_w', 'L0_attn_proj_b',
         'L0_attn_norm2_g', 'L0_attn_norm2_b', 'L0_attn_fc1_w', 'L0_attn_fc1_b', 'L0_attn_fc2_w', 'L0_attn_fc2_b',
         'L0_ffn_Wg', 'L0_ffn_Wu', 'L0_ffn_Wd', 'L0_c', 'L0_wmod', 'L1_attn_Wqkv', 'L1_attn_Wout',
         'L1_attn_head_scales', 'L1_attn_head_dirs', 'L1_ffn_Wq', 'L1_ffn_Wk', 'L1_ffn_Wv', 'L1_ffn_Ws', 'L1_ffn_Wd',
         'L1_ffn_Wo', 'L1_c', 'L1_wmod']


def kernel(**inputs):
    import numpy as _np
    import concourse.bacc as _bacc
    from concourse import mybir as _mybir
    from concourse.bass_utils import run_bass_kernel_spmd as _run

    nc = _bacc.Bacc("TRN2", target_bir_lowering=False, num_devices=1)
    arrays, aps = {}, {}
    for name in NAMES:
        x = _np.ascontiguousarray(inputs[name])
        arrays[f"in_{name}"] = x
        aps[name] = nc.dram_tensor(f"in_{name}", x.shape, _mybir.dt.from_np(x.dtype), kind="ExternalInput").ap()
    out = nc.dram_tensor("out_0", (NB, T, P), F32, kind="ExternalOutput").ap()
    row_table = nc.dram_tensor("row_table", (NB, 5 * P), F32, kind="Internal").ap()
    build(nc, aps, row_table, out)
    r = _run(nc, [arrays], core_ids=[0])
    return r.results[0]["out_0"]
```

```python
from contextlib import ExitStack

import concourse.bass as bass
from concourse import mybir

F32 = mybir.dt.float32
F32R = mybir.dt.float32r
BF16 = mybir.dt.bfloat16
ALU = mybir.AluOpType
ACT = mybir.ActivationFunctionType
X_AXIS = mybir.AxisListType.X

P = 128
NB = 8
T = 512
NT = T // P
H0, D0 = 16, 8
NJ = 4
NE = 8
H1, D1 = 8, 16
HS, DS = 16, 64
NP = HS // 2
VW = DS + 1
NQ = 8
GROUP = 4
NG = HS // GROUP
QUERIES_AT = (8, 11)
PIECES_AT = 5
PIECES_BY = 2
MIXED_AT = 20
HEAD1_SHARE, FINISH_SHARE = 0.35, 1.6
NPROD = 3
EPS_LN, EPS_ATTN = 1e-5, 1e-6
BIG = 3.0e38
MASKED = -1.0e30
SA0, CA0, GA0, SB0, CB0, GB0, SA1, CA1, GA1, SB1, CB1, GB1 = range(12)
LNS = 6
N1, N2 = NT * H1, NT * HS
A1 = 7
E1 = A1 + N1 + 3
MARKS = {"load": 1, "attn0": 24, "moe_in": 3, "experts": NE * NJ, "attn1": E1 + 6, "gates": 13,
         "values": NQ * NT + 1}


VALUES_V = [n for n in range(NQ * NT) if n % 4 == 3]
LAST_VALUES_V = [n for n in range(NQ * NT) if n % 2]
OUTPUTS_V = [n for n in range(NQ * NT) if n // NQ == NT - 1 and n % 2]


def values_v(b):
    return LAST_VALUES_V if isinstance(b[0], int) and sum(b) == NB - 1 else VALUES_V


def by_pool(n, by_v):
    return n - by_vector(n, by_v)


def by_vector(n, by_v):
    return sum(m < n for m in by_v)


def head_steps():
    steps = [("queries", 0), ("queries", 1)]
    for m in range(N2):
        i, h = m // HS, m % HS
        if i < NT - 1 and h in QUERIES_AT:
            steps.append(("queries", 2 * (i + 1) + QUERIES_AT.index(h)))
        if m >= HS + MIXED_AT and (m - MIXED_AT) % HS == 0:
            steps.append(("mixed", (m - MIXED_AT) // HS - 1))
        if m >= HS + MIXED_AT + 2 and (m - MIXED_AT - 2) % HS == 0:
            steps.append(("result", (m - MIXED_AT - 2) // HS - 1))
        steps.append(("head", m))
    last = len(steps) - 1
    steps += [("rest", 0)] * 4 + [("mixed", NT - 2), ("rest", 0), ("result", NT - 2)] + [("rest", 0)] * 6
    steps += [("mixed", NT - 1), ("rest", 0), ("result", NT - 1)]
    at = {step: k for k, step in enumerate(steps)}
    pieces = {}
    for n in range(NQ * NT):
        i, q = n // NQ, n % NQ
        m = (i + 1) * HS + PIECES_AT + PIECES_BY * q
        if i == NT - 1:
            k = last + 6 + q
        else:
            k = at["head", m] if m < N2 else last + m - N2 + 1
        pieces[k] = n
    return steps, pieces, last + 1


HEAD_STEPS, PIECE_AT, FINISH_AT = head_steps()
PIECE_STEP = {n: k for k, n in PIECE_AT.items()}
TURN = [sum(kind != "rest" for kind, _ in HEAD_STEPS[:k + 1]) for k in range(len(HEAD_STEPS))]
NTURNS = TURN[-1]
MARKS["begin"] = BEGIN = 2
MARKS["heads"] = FINISH_AT - BEGIN
CLOSE_AT = HEAD_STEPS.index(("mixed", NT - 1))
MARKS["finish"] = (CLOSE_AT - FINISH_AT + 1) // 2
MARKS["close"] = len(HEAD_STEPS) + 1 - CLOSE_AT
CLOSE_BEHIND, BEGIN_BEHIND = 4, 28


def weight(name, m):
    return HEAD1_SHARE if name == "attn1" and A1 < m <= E1 else FINISH_SHARE if name == "finish" else 1


def mark_of(k):
    return k + 1 if k < BEGIN else k + 1 - BEGIN if k < FINISH_AT else (k - FINISH_AT) // 2 + 1 if k < CLOSE_AT else k + 1 - CLOSE_AT


def step_of(k):
    return (*HEAD_STEPS[k], TURN[k]) if 0 <= k < len(HEAD_STEPS) else ("rest", 0, 0)


def build(nc, a, row_table, out):
    ctx = ExitStack()
    with ctx:
        def sb(name, shape, dt=F32):
            return ctx.enter_context(nc.sbuf_tensor(name, shape, dt))

        def sem(name, per=0):
            s = ctx.enter_context(nc.semaphore(name))
            return s, per

        ident = sb("ident", [P, P])
        ident_bf = sb("ident_bf", [P, P], BF16)
        causal_bf = sb("causal_bf", [P, P], BF16)
        block8 = sb("block8", [P, P])
        head_of8 = sb("head_of8", [P, H0])
        head_of16 = sb("head_of16", [P, H1])
        ones_row = sb("ones_row", [1, P])
        first_wins = sb("first_wins", [P, NE])
        minus_half = sb("minus_half", [P, NT])
        qkvT = sb("qkvT", [P, 3 * P])
        projT = sb("projT", [P, P])
        fc1T = sb("fc1T", [P, T])
        fc2T = sb("fc2T", [P, NJ, P])
        proj_b_row = sb("proj_b_row", [1, NT, P])
        cols = sb("cols", [P, 9])
        Wg = sb("Wg", [P, 2, T])
        Wu = sb("Wu", [P, 2, T])
        Wd = sb("Wd", [P, 2, NJ, P])
        W1 = sb("W1", [P, 3 * P])
        Wout = sb("Wout", [P, P])
        WqT = sb("WqT", [P, HS * DS])
        WkT = sb("WkT", [P, HS * DS])
        WvT = sb("WvT", [P, NE * DS])
        gatesT = sb("gatesT", [P, 2 * P])
        WoT = sb("WoT", [P, NJ, P])
        mod = sb("mod", [P, NB, 12])
        rows0 = sb("rows0", [P, 3, P])
        rows1a = sb("rows1a", [P, P])
        rows1b = sb("rows1b", [P, P])

        HQ = HS // NQ

        xin = sb("xin", [P, NT, P])
        nrm_o1 = sb("nrm_o1", [P, NT * H1 * (D1 + 1)])
        nrm = nrm_o1[:, 0:NT * P].rearrange("p (i c) -> p i c", i=NT)
        o1 = nrm_o1[:, :].rearrange("p (i h d) -> p i h d", i=NT, h=H1)
        stats = sb("stats", [P, NT, 6])
        mv = sb("mv", [P, NT, 2])
        pause = sb("pause", [P, 1])
        vareps = sb("vareps", [P, NT])
        rstd = sb("rstd", [P, NT])
        modA = sb("modA", [P, 12])
        modB = sb("modB", [P, 12])
        arena = sb("arena", [P, 6144])

        def part(at, shape):
            n = 1
            for x in shape:
                n *= x
            names = "abcd"[:len(shape)]
            v = arena[:, at:at + n]
            return v if len(shape) == 1 else v.rearrange(f"p ({' '.join(names)}) -> p {' '.join(names)}", **dict(zip(names, shape)))

        h0m = part(0, [NT, P])
        h0 = sb("h0", [P, NT, P])
        h1T = sb("h1T", [P, T])
        qmin = part(512, [T])
        qexp = part(1024, [T])
        qe = part(1536, [T])
        kmin = part(2048, [NT, P])
        kexp = part(2560, [NT, P])
        ke = part(3072, [NT, P])
        v0 = part(3584, [NT, P + 1])
        kv = sb("kv", [P, P + H0])
        den0 = sb("den0", [P, NT, H0])
        rden0 = sb("rden0", [P, NT, H0])
        att = sb("att", [P, NT, P])
        attT = sb("attT", [P, T])
        x2 = h0
        x2g = h0m
        xg = xin
        hid = part(3584, [NJ, T])
        yS = nrm.rearrange("p i c -> p (i c)")
        x3 = h0
        silu = part(0, [2, T])
        act = part(1024, [3, T])
        x4 = x3
        q1T = attT
        k1T = att[:, :, :].rearrange("p i c -> p (i c)")
        k1z = part(0, [H1, T])
        v1 = sb("v1", [P, NT, H1, D1 + 1])
        nmax1 = sb("nmax1", [P, 2])
        p1 = part(4096, [2, T])
        p1T = part(5120, [2, T])
        rden1 = sb("rden1", [P, NT, H1])
        WoutG = sb("WoutG", [P, P])
        x5 = sb("x5", [P, NT, P])
        hdT = sb("hdT", [P, T])
        hdB = sb("hdB", [P, T])
        gate = part(0, [2, NT, HS, NE])
        eq = part(1024, [2 * NT * HS, NE])
        cand = part(2048, [2 * NT * HS, NE])
        oh1 = part(3072, [2 * NT * HS, NE])
        oh2 = part(4096, [2 * NT * HS, NE])
        top = sb("top", [P, 2, 2 * NT * HS])
        pick = sb("pick", [P, 2 * NT * HS])
        sigd = sb("sigd", [P, 2, NT * HS])
        sig = sb("sig", [P, 2, NT * HS])
        mixv = sb("mixv", [P, NT, HS, NE])
        masko = sb("masko", [P, NT, HS, NE])
        maskB = sb("maskB", [P, NT, HS, NE])
        pv = sb("pv", [P, 2, NE * DS])
        prod = sb("prod", [P, NPROD, HS * NE * DS // NQ])
        vals = sb("vals", [P, NT, HS, VW])
        keys = sb("keys", [P, HS, T], F32R)
        q_high = sb("q_high", [P, 3, HS // 2, P], F32R)
        q_low = sb("q_low", [P, 3, HS // 2, P], F32R)
        nmax = sb("nmax", [P, 2])
        pr = sb("pr", [P, 2, T])
        prT = sb("prT", [P, 2, T])
        oa = sb("oa", [P, 2, HS, VW])
        rden = sb("rden", [P, 2, HS])
        coef = sb("coef", [P, 2, HS, NE])
        ym = sb("ym", [P, NE * DS])
        ymT = sb("ymT", [P, NJ, P])
        resc = sb("resc", [P, P])
        resg = sb("resg", [P, P])
        xout = sb("xout", [P, NT, P])

        bank = [ctx.enter_context(nc.psum_tensor(f"bank{i}", [P, T], F32)) for i in range(8)]
        F0, F1, F2, F3, S0, S1, TB, OB = bank

        def tiles(t):
            return t[:, :].rearrange("p (i c) -> p i c", i=NT)

        def wait(eng, s, b, k):
            number, offset = b
            k += offset * s[1]
            if not (isinstance(number, int) and number * s[1] + k <= 0):
                eng.wait_ge(s[0], number * s[1] + k)

        small_in = sem("small_in")
        raw_in = sem("raw_in")
        const_g = sem("const_g")
        const_v = sem("const_v")
        setup_pe = sem("setup_pe")
        setup_v = sem("setup_v")
        setup_done = sem("setup_done")

        x_in = sem("x_in", 32)
        rows1a_in = sem("rows1a_in", 16)
        rows1b_in = sem("rows1b_in", 16)
        table_out = sem("table_out")
        experts_in = [sem("experts_even", 48 * NE // 2), sem("experts_odd", 48 * NE // 2)]
        ln_stats = sem("ln_stats", LNS)
        ln_mv = sem("ln_mv", LNS)
        ln_eps = sem("ln_eps", LNS)
        ln_rstd = sem("ln_rstd", LNS)
        ln_n = sem("ln_n", LNS)
        ln_T = sem("ln_T", 5)
        ln_evac = sem("ln_evac", 5)
        modA_r = sem("modA_r", 1)
        modB_r = sem("modB_r", 1)
        h0m_r = sem("h0m_r", 1)
        h0_r = sem("h0_r", 1)
        qkv0_r = sem("qkv0_r", 3)
        emin_r = sem("emin_r", 3)
        eexp_r = sem("eexp_r", 3)
        elu_r = sem("elu_r", 3)
        v0_r = sem("v0_r", 2)
        kv_ps = sem("kv_ps", 1)
        kv_r = sem("kv_r", 1)
        num_ps = sem("num_ps", 2)
        den0_r = sem("den0_r", 1)
        rden0_r = sem("rden0_r", 1)
        att0_r = sem("att0_r", 1)
        att0_T = sem("att0_T", 1)
        attT0_r = sem("attT0_r", 1)
        proj_ps = sem("proj_ps", 1)
        x2_r = sem("x2_r", 1)
        fc1_ps = sem("fc1_ps", NJ)
        hid_r = sem("hid_r", NJ)
        fc2_ps = sem("fc2_ps", 1)
        y0_r = sem("y0_r", 1)
        y0_T = sem("y0_T", 1)
        x2g_r = sem("x2g_r", 1)
        xg_r = sem("xg_r", 1)
        x3_r = sem("x3_r", 1)
        gu_g = sem("gu_g", NE * NJ)
        gu_u = sem("gu_u", NE * NJ)
        silu_r = sem("silu_r", NE * NJ)
        act_r = sem("act_r", NE * NJ)
        down_ps = sem("down_ps", NE * NJ)
        y1_r = sem("y1_r", 1)
        y1_T = sem("y1_T", 1)
        x4_r = sem("x4_r", 1)
        qkv1_ps = sem("qkv1_ps", 3)
        q1_r = sem("q1_r", 1)
        k1_r = sem("k1_r", 1)
        v1_r = sem("v1_r", 1)
        k1z_r = [sem("k1z_first", H1 // 2), sem("k1z_second", H1 // 2)]
        s1_ps = sem("s1_ps", N1)
        nmax1_r = sem("nmax1_r", N1)
        p1_r = sem("p1_r", N1)
        p1_T = sem("p1_T", N1)
        p1T_r = sem("p1T_r", N1)
        o1_ps = sem("o1_ps", NT)
        o1_r = sem("o1_r", NT)
        rden1_r = sem("rden1_r", 1)
        att1_r = sem("att1_r", 1)
        att1_T = sem("att1_T", 1)
        attT1_r = sem("attT1_r", 1)
        WoutG_r = sem("WoutG_r", 1)
        out1_ps = sem("out1_ps", 1)
        x5_r = sem("x5_r", 1)
        gate_ps = sem("gate_ps", 2)
        gate_r = sem("gate_r", 2)
        topk_v = sem("topk_v", 9)
        topk_g = sem("topk_g", 2)
        sig_e = sem("sig_e", 1)
        sig_v = sem("sig_v", 2)
        mix_g = sem("mix_g", 3)
        masko_r = sem("masko_r", 1)
        pv_ps = sem("pv_ps", NT)
        pv_r = sem("pv_r", NT)
        vprod_r = sem("vprod_r", by_pool(NQ * NT, VALUES_V))
        vprod_v = sem("vprod_v", len(VALUES_V))
        vals_r = sem("vals_r", NQ * NT)
        k_ps = sem("k_ps", NP)
        kh_r = sem("kh_r", HS)
        ks_r = sem("ks_r", NP)
        ql_r = sem("ql_r", 2 * NT)
        q_both = sem("q_both", 2 * NT)
        s_ps = sem("s_ps", NTURNS)
        s_out = sem("s_out", NTURNS)
        nmax_r = sem("nmax_r", N2)
        p_T = sem("p_T", N2)
        pT_r = sem("pT_r", N2)
        hdB_r = sem("hdB_r", 1)
        maskB_r = sem("maskB_r", 1)
        xcopy_r = sem("xcopy_r", 1)
        o_ps = sem("o_ps", NT * NG)
        oa_r = sem("oa_r", NT * NG)
        rden_r = sem("rden_r", NT)
        coef_r = sem("coef_r", NT)
        oprod_r = sem("oprod_r", by_pool(NQ * NT, OUTPUTS_V))
        oprod_v = sem("oprod_v", len(OUTPUTS_V))
        ym_r = sem("ym_r", NQ * NT)
        resg_r = sem("resg_r", NT)
        xout_r = sem("xout_r", NT)
        stored = sem("stored", 16)

        block = ctx.enter_context(nc.Block())

        raw_qkv = part(0, [3, P])
        raw_proj = part(384, [P])
        raw_fc1 = part(512, [4, P])
        raw_fc2 = part(1024, [4, P])
        raw_wq = part(1536, [8, P])
        raw_wk = part(2560, [8, P])
        raw_wv = part(3584, [4, P])
        raw_wo = part(4096, [4, P])
        raw_gates = xin[:, 0:2, :]
        stage = vals[:, :, :, :].rearrange("p i h d -> p (i h d)")[:, 0:8 * T].rearrange("p (a t) -> p a t", a=8)
        wmod = [stage[:, 0:2, :].rearrange("p a c -> p (a c)")[:, 0:768],
                stage[:, 2:4, :].rearrange("p a c -> p (a c)")[:, 0:768]]
        crow = [stage[0:NB, 4, 0:P], stage[0:NB, 5, 0:P]]
        cexp = [stage[0:NB, 4, P:2 * P], stage[0:NB, 5, P:2 * P]]
        crec = [stage[0:NB, 4, 2 * P:3 * P], stage[0:NB, 5, 2 * P:3 * P]]
        csil = [stage[0:NB, 4, 3 * P:4 * P], stage[0:NB, 5, 3 * P:4 * P]]
        cT = [stage[:, 6, 0:NB], stage[:, 6, NB:2 * NB]]
        col_rows = stage[0:9, 6, P:2 * P]
        dirs = stage[0:1, 7, 0:P]
        sdirs = stage[0:1, 7, P:2 * P]
        scales = stage[0:1, 7, 2 * P:2 * P + H1]
        wq1T = xin[:, 2, :]
        bias_m = xin[:, 3, :]
        block16 = part(4608, [P])
        sgn = nrm[:, 0, 0:4 * NB].rearrange("p (b m) -> p b m", b=NB)
        gab = nrm[:, 1, 0:4 * NB].rearrange("p (b m) -> p b m", b=NB)
        rtab = part(5120, [5, P])[0:NB]
        rsgn = part(4736, [3, P])[0:NB]
        rabs = part(5760, [3, P])[0:NB]
        wq1 = W1[:, 0:P]

        turns = ([(raw_qkv[:, i, :], qkvT[:, i * P:(i + 1) * P]) for i in range(3)]
                 + [(raw_proj, projT[:, :])]
                 + [(raw_fc1[:, i, :], fc1T[:, i * P:(i + 1) * P]) for i in range(4)]
                 + [(raw_fc2[:, i, :], fc2T[:, i, :]) for i in range(4)]
                 + [(raw_wq[:, i, :], WqT[:, i * P:(i + 1) * P]) for i in range(8)]
                 + [(raw_wk[:, i, :], WkT[:, i * P:(i + 1) * P]) for i in range(8)]
                 + [(raw_wv[:, i, :], WvT[:, i * P:(i + 1) * P]) for i in range(4)]
                 + [(raw_wo[:, i, :], WoT[:, i, :]) for i in range(4)]
                 + [(raw_gates[:, i, :], gatesT[:, i * P:(i + 1) * P]) for i in range(2)]
                 + [(wq1, wq1T)])
        NTURN = len(turns)

        def schedule(stages, work):
            running = {}

            def marks_of(parts):
                return [(name, b, m) for name, b, *some in parts for m in (some[0] if some else range(1, MARKS[name] + 1))]

            def run(name, b, m):
                if name in stages:
                    if m == 1:
                        running[name] = [stages[name](b), 0]
                    stage = running[name]
                    while stage[1] < m:
                        stage[1] = next(stage[0], 10 ** 6)

            for main, beside in work:
                main, beside = marks_of(main), marks_of(beside)
                total = sum(weight(name, m) for name, _, m in beside)
                done = before = 0
                for n, mark in enumerate(main, 1):
                    run(*mark)
                    while done < len(beside) and (before * len(main) < n * total or n == len(main)):
                        before += weight(beside[done][0], beside[done][2])
                        run(*beside[done])
                        done += 1

        FRONT_A = ("load", "attn0", "moe_in")
        FRONT_B = ("attn1", "gates")

        def program(eng, stages):
            def of(names, b, offset=0):
                return [(name, (b, offset)) for name in names]

            def after_heads(b, offset=0):
                return [("finish", (b, offset)), ("values", (b, offset + 1), range(1, CLOSE_BEHIND + 1)), ("close", (b, offset)),
                        ("values", (b, offset + 1), range(CLOSE_BEHIND + 1, BEGIN_BEHIND + 1)), ("begin", (b, offset + 1)),
                        ("values", (b, offset + 1), range(BEGIN_BEHIND + 1, MARKS["values"] + 1))]

            schedule(stages, [(of(FRONT_A, 0), []), (of(("experts",), 0), []),
                              (of(FRONT_B, 0), []), (of(FRONT_A, 1) + of(("experts",), 1), of(("values", "begin"), 0))])
            second = eng.alloc_register("second")
            with eng.Fori(1, NB - 1) as b:
                schedule(stages, [(of(("heads",), b, -1), of(FRONT_B, b) + of(FRONT_A, b, 1))])
                eng.reg_mov(second, b)
                c = eng.snap(second, min_val=1, max_val=NB - 2)
                schedule(stages, [(of(("experts",), c, 1), after_heads(c, -1))])
            last = NB - 1
            schedule(stages, [(of(("heads",), last - 1), of(FRONT_B, last)),
                              (after_heads(last, -1), []), (of(("heads", "finish", "close"), last), [])])

        def queries_of(bank_k, odd):
            return bank_k[DS * odd:DS * odd + DS, :].rearrange("p (a t) -> p a t", a=4)

        def own_half(part, j, odd):
            return part[DS * odd:DS * odd + DS, j % 3, :, :].rearrange("p (a o) t -> p a o t", o=2)[:, :, odd, :]

        def other_half(part, j, odd):
            return part[DS - DS * odd:2 * DS - DS * odd, j % 3, :, :].rearrange("p (a o) t -> p a o t", o=2)[:, :, odd, :]

        def value_piece(n):
            i, q = n // NQ, n % NQ
            return (prod[:, n % NPROD, :].rearrange("p (h d e) -> p h d e", h=HQ, e=NE),
                    pv[:, i % 2, :].rearrange("p (e d) -> p d e", e=NE).unsqueeze(1).to_broadcast([P, HQ, DS, NE]),
                    mixv[:, i, HQ * q:HQ * q + HQ, :].unsqueeze(2).to_broadcast([P, HQ, DS, NE]))

        def output_piece(n):
            i, q = n // NQ, n % NQ
            return (prod[:, n % NPROD, :].rearrange("p (d h) -> p d h", h=HS),
                    oa[:, i % 2, :, 0:DS].rearrange("p h d -> p d h"),
                    coef[:, i % 2, :, q].unsqueeze(1).to_broadcast([P, DS, HS]))

        @block.sync
        def _(sp):
            for row, src in ((0, a["L0_attn_norm1_g"]), (1, a["L0_attn_norm1_b"]), (2, a["L0_attn_norm2_g"]),
                             (3, a["L0_attn_norm2_b"]), (8, a["L0_attn_fc2_b"])):
                sp.dma_start(col_rows[row:row + 1, :], src.rearrange("(o p) -> o p", o=1)).then_inc(small_in[0], 16)
            sp.dma_start(col_rows[4:8, :], a["L0_attn_fc1_b"].rearrange("(j p) -> j p", p=P)).then_inc(small_in[0], 16)
            for i in range(NT):
                sp.dma_start(proj_b_row[:, i, :], a["L0_attn_proj_b"].rearrange("(o p) -> o p", o=1)).then_inc(small_in[0], 16)
            sp.dma_start(crow[0], a["L0_c"]).then_inc(small_in[0], 16)
            sp.dma_start(crow[1], a["L1_c"]).then_inc(small_in[0], 16)
            sp.dma_start(scales, a["L1_attn_head_scales"].rearrange("(o h) -> o h", o=1)).then_inc(small_in[0], 16)
            sp.wait_ge(const_g[0], 3)
            sp.dma_start(dirs.rearrange("o (h d) -> o h d", h=H1)[:, :, 0:3],
                         a["L1_attn_head_dirs"].rearrange("(o h) d -> o h d", o=1)).then_inc(small_in[0], 16)
            sp.dma_start(wmod[0], a["L0_wmod"]).then_inc(small_in[0], 16)
            sp.dma_start(wmod[1], a["L1_wmod"]).then_inc(small_in[0], 16)
            sp.wait_ge(setup_done[0], 1)
            sp.dma_start(row_table, rtab.rearrange("b m c -> b (m c)")).then_inc(table_out[0], 16)

            def expert(b, e):
                wait(sp, down_ps, b, NJ * (e - 1) if e >= 2 else 0)
                sp.dma_start(Wg[:, e % 2, :], a["L0_ffn_Wg"][e, :, :]).then_inc(experts_in[e % 2][0], 16)
                sp.dma_start(Wu[:, e % 2, :], a["L0_ffn_Wu"][e, :, :]).then_inc(experts_in[e % 2][0], 16)
                sp.dma_start(Wd[:, e % 2, :, :], a["L0_ffn_Wd"][e, :, :].rearrange("(j p) c -> p j c", p=P)).then_inc(experts_in[e % 2][0], 16)

            def experts(b):
                for e in range(2, NE):
                    yield NJ * (e - 1) + 2
                    expert(b, e)
                yield MARKS["experts"]

            def load(b):
                wait(sp, x3_r, b, 0)
                sp.dma_start(xin[:, :, :], a["L0_attn_x"][bass.ds(b[0] + b[1], 1), :, :].rearrange("o (i p) c -> p (o i) c", p=P)).then_inc(x_in[0], 16)
                if isinstance(b[0], int) and sum(b) == 0:
                    sp.wait_ge(table_out[0], 16)
                sp.dma_start(rows0[:, :, :].rearrange("p m c -> p (m c)"), row_table[bass.ds(b[0] + b[1], 1), 0:3 * P].to_broadcast([P, 3 * P])).then_inc(x_in[0], 16)
                wait(sp, WoutG_r, b, 0)
                sp.dma_start(rows1a[:, :], row_table[bass.ds(b[0] + b[1], 1), 3 * P:4 * P].to_broadcast([P, P])).then_inc(rows1a_in[0], 16)
                expert(b, 0)
                expert(b, 1)
                yield 1

            def values(b):
                yield NQ * NT // 2
                wait(sp, xout_r, b, 0)
                sp.dma_start(rows1b[:, :], row_table[bass.ds(b[0] + b[1], 1), 4 * P:5 * P].to_broadcast([P, P])).then_inc(rows1b_in[0], 16)
                yield MARKS["values"]

            def close(b):
                yield MARKS["close"] - 1
                wait(sp, xout_r, b, NT)
                sp.dma_start(out[bass.ds(b[0] + b[1], 1), :, :].rearrange("o (i p) c -> p (o i) c", p=P), xout[:, :, :]).then_inc(stored[0], 16)
                yield MARKS["close"]

            program(sp, {"load": load, "experts": experts, "values": values, "close": close})
            sp.wait_ge(stored[0], 16 * NB)

        @block.gpsimd
        def _(g):
            g.memset(ident[:, :], 0.0)
            g.memset(dirs, 0.0)
            g.memset(block8[:, :], 1.0)
            g.memset(block16, 1.0)
            g.memset(head_of8[:, :], 1.0)
            g.memset(head_of16[:, :], 1.0)
            g.memset(causal_bf[:, :], 0.0)
            g.memset(ones_row[:, :], 1.0)
            g.memset(minus_half[:, :], -0.5)
            g.memset(v1[:, :, :, D1:D1 + 1], 1.0)
            for e in range(NE):
                g.memset(first_wins[:, e:e + 1], float(NE - e))
            g.memset(nmax[:, :], 0.0).then_inc(const_g[0], 3)
            g.wait_ge(const_g[0], 3)
            g.affine_select(out=ident[:, :], in_=ident[:, :], compare_op=ALU.not_equal, fill=1.0, base=0,
                            pattern=[[-1, P]], channel_multiplier=1)
            g.affine_select(out=causal_bf[:, :], in_=causal_bf[:, :], compare_op=ALU.is_ge, fill=MASKED, base=0,
                            pattern=[[-1, P]], channel_multiplier=1)

            def cut(tile, n, size, inner, k):
                view = tile.rearrange("p (n s) -> p n s", n=n)
                g.affine_select(out=view, in_=view, compare_op=ALU.is_ge, fill=0.0, base=0,
                                pattern=[[-size, n], [0, inner]], channel_multiplier=1).then_inc(const_g[0], 1)
                g.wait_ge(const_g[0], k)
                g.affine_select(out=view, in_=view, compare_op=ALU.is_ge, fill=0.0, base=size - 1,
                                pattern=[[size, n], [0, inner]], channel_multiplier=-1).then_inc(const_g[0], 1)

            cut(block8[:, :], H0, D0, D0, 4)
            cut(block16, H1, D1, D1, 6)
            cut(head_of8[:, :], H0, D0, 1, 8)
            cut(head_of16[:, :], H1, D1, 1, 10)
            g.wait_ge(const_g[0], 11)
            g.tensor_copy(ident_bf[:, :], ident[:, :]).then_inc(const_g[0], 1)
            g.wait_ge(setup_done[0], 1)

            def rstd_of(b, n):
                wait(g, ln_eps, b, n + 1)
                g.tensor_tensor(rstd[:, :], vareps[:, :], minus_half[:, :], ALU.pow).then_inc(ln_rstd[0], 1)

            def attn0(b):
                rstd_of(b, 0)
                yield 1
                rstd_of(b, 1)
                yield 14
                rstd_of(b, 2)
                wait(g, x2_r, b, 1)
                g.tensor_tensor(x2g, x2[:, :, :], rows0[:, 2:3, :].to_broadcast([P, NT, P]), ALU.mult).then_inc(x2g_r[0], 1)
                wait(g, x2g_r, b, 1)
                wait(g, x_in, b, 32)
                g.tensor_tensor(xg[:, :, :], x2g, xin[:, :, :], ALU.add).then_inc(xg_r[0], 1)
                yield 24

            def moe_in(b):
                rstd_of(b, 3)
                yield 3

            def attn1(b):
                yield 2
                rstd_of(b, 4)
                yield 5
                wait(g, k1_r, b, 1)
                for h in range(H1 // 2, H1):
                    g.tensor_tensor(k1z[:, h, :], k1T, head_of16[:, h:h + 1].to_broadcast([P, T]), ALU.mult).then_inc(k1z_r[1][0], 1)
                wait(g, rows1a_in, b, 16)
                wait(g, out1_ps, b, 0)
                g.tensor_tensor(WoutG[:, :], Wout[:, :], rows1a[:, :], ALU.mult).then_inc(WoutG_r[0], 1)
                yield E1 + 2
                rstd_of(b, 5)
                yield MARKS["attn1"]

            def gates(b):
                yield 2
                for r in range(2):
                    wait(g, topk_v, b, 2 + 5 * r)
                    g.tensor_tensor(cand, eq, first_wins[:, :].unsqueeze(1).to_broadcast([P, 2 * NT * HS, NE]), ALU.mult).then_inc(topk_g[0], 1)
                    yield (8, 11)[r]
                wait(g, sig_v, b, 2)
                wait(g, topk_v, b, 9)
                half = NT * HS
                o1h = oh1[:, 0:half, :]
                o2h = oh2[:, 0:half, :]
                mixf = mixv[:, :, :, :].rearrange("p i h e -> p (i h) e")
                w1 = cand[:, 0:half, :]
                w2 = cand[:, half:2 * half, :]
                g.tensor_tensor(w1, o1h, sig[:, 0, :].unsqueeze(2).to_broadcast([P, half, NE]), ALU.mult).then_inc(mix_g[0], 1)
                g.tensor_tensor(w2, o2h, sig[:, 1, :].unsqueeze(2).to_broadcast([P, half, NE]), ALU.mult).then_inc(mix_g[0], 1)
                wait(g, mix_g, b, 2)
                g.tensor_tensor(mixf, w1, w2, ALU.add).then_inc(mix_g[0], 1)
                yield MARKS["gates"]

            def values(b):
                wait(g, mix_g, b, 3)
                wait(g, ym_r, b, 0)
                for n in range(NQ * NT):
                    if n not in values_v(b):
                        wait(g, pv_r, b, n // NQ + 1)
                        if n >= NPROD:
                            wait(g, vals_r, b, n - NPROD + 1)
                        g.tensor_tensor(*value_piece(n), ALU.mult).then_inc(vprod_r[0], 1)
                    yield n + 1

            def heads(b):
                wait(g, vals_r, b, NQ * NT)
                wait(g, maskB_r, b, 1)
                yield from mixing(b, BEGIN, FINISH_AT)

            def finish(b):
                yield from mixing(b, FINISH_AT, CLOSE_AT)

            def mixing(b, first, end):
                for i in range(NT):
                    if not first <= PIECE_STEP[NQ * (i + 1) - 1]:
                        continue
                    if first <= PIECE_STEP[NQ * i] < end:
                        yield mark_of(PIECE_STEP[NQ * i] - 3)
                        wait(g, rden_r, b, i + 1)
                        g.tensor_tensor(coef[:, i % 2, :, :], maskB[:, i, :, :], rden[:, i % 2, :].unsqueeze(2).to_broadcast([P, HS, NE]), ALU.mult).then_inc(coef_r[0], 1)
                        wait(g, coef_r, b, i + 1)
                    for q in range(NQ):
                        n = NQ * i + q
                        if first <= PIECE_STEP[n] < end:
                            if n not in OUTPUTS_V:
                                if n >= NPROD:
                                    wait(g, ym_r, b, n - NPROD + 1)
                                g.tensor_tensor(*output_piece(n), ALU.mult).then_inc(oprod_r[0], 1)
                            yield mark_of(max(PIECE_STEP[n] - 2, first))

            program(g, {"attn0": attn0, "moe_in": moe_in, "attn1": attn1, "gates": gates, "values": values,
                        "heads": heads, "finish": finish})

        @block.tensor
        def _(pe):
            def transposes(dst, src, src_tiles=NT):
                for i in range(src_tiles):
                    last = pe.transpose(dst[:, i * P:(i + 1) * P], src(i), ident[:, :])
                return last

            pe.wait_ge(const_g[0], 12)
            pe.wait_ge(raw_in[0], 16 * 12)
            for n in range((NTURN + 3) // 4):
                part = turns[4 * n:4 * n + 4]
                if n >= 2:
                    pe.wait_ge(setup_v[0], n - 1)
                for i, (src, _) in enumerate(part):
                    last = pe.transpose(bank[n % 2][:, i * P:(i + 1) * P], src, ident[:, :])
                last.then_inc(setup_pe[0], 1)
            n = (NTURN + 3) // 4
            pe.wait_ge(const_v[0], 9)
            pe.wait_ge(small_in[0], 16 * 16)
            for l in range(2):
                pe.transpose(bank[2][:, 8 * l:8 * l + 8], csil[l], ident[0:NB, 0:NB])
            pe.transpose(bank[2][:, 2 * NB:2 * NB + 9], col_rows, ident[0:9, 0:9])
            pe.matmul(bank[3][:, 0:P], sdirs, dirs, start=True, stop=True).then_inc(setup_pe[0], 1)
            pe.wait_ge(setup_v[0], n + 2)
            for l in range(2):
                for m in range(6):
                    last = pe.matmul(bank[4][:, 48 * l + 8 * m:48 * l + 8 * m + 8], wmod[l][:, m * P:(m + 1) * P], cT[l], start=True, stop=True)
            last.then_inc(setup_pe[0], 1)
            pe.matmul(bank[5][:, 0:P], wq1T, bias_m, start=True, stop=True).then_inc(setup_pe[0], 1)
            pe.matmul(bank[6][0:NB, 0:3 * P], cT[0], wmod[0][:, 0:3 * P], start=True, stop=True)
            pe.matmul(bank[7][0:NB, 0:P], cT[1], wmod[1][:, 2 * P:3 * P], start=True, stop=True)
            pe.matmul(bank[7][0:NB, P:2 * P], cT[1], wmod[1][:, 5 * P:6 * P], start=True, stop=True).then_inc(setup_pe[0], 1)
            pe.wait_ge(setup_done[0], 1)

            def ln_turn(b, n, dst):
                wait(pe, ln_n, b, n + 1)
                transposes(dst, lambda i: nrm[:, i, :]).then_inc(ln_T[0], 1)

            def attn0(b):
                yield 3
                ln_turn(b, 1, F0)
                yield 4
                wait(pe, ln_evac, b, 1)
                pe.matmul(F1[:, :], qkvT[:, 0:P], h1T[:, :], start=True, stop=True).then_inc(qkv0_r[0], 1)
                for k, f in enumerate((F2, F3)):
                    for i in range(2):
                        t = 2 * k + i
                        last = pe.matmul(f[:, i * 256:(i + 1) * 256], h1T[:, t * P:(t + 1) * P], qkvT[:, P:3 * P], start=True, stop=True)
                    last.then_inc(qkv0_r[0], 1)
                yield 7
                wait(pe, elu_r, b, 3)
                wait(pe, v0_r, b, 2)
                for i in range(NT):
                    last = pe.matmul(F0[:, 0:P + 1], ke[:, i, :], v0[:, i, :], start=(i == 0), stop=(i == NT - 1))
                last.then_inc(kv_ps[0], 1)
                yield 9
                wait(pe, kv_r, b, 1)
                for k, f in enumerate((F2, F3)):
                    for i in range(2):
                        t = 2 * k + i
                        last = pe.matmul(f[:, i * 256:i * 256 + P + H0], qe[:, t * P:(t + 1) * P], kv[:, :], start=True, stop=True)
                    last.then_inc(num_ps[0], 1)
                yield 11
                wait(pe, att0_r, b, 1)
                transposes(F1, lambda i: att[:, i, :]).then_inc(att0_T[0], 1)
                pe.matmul(F0[:, :], ones_row[:, :], proj_b_row[:, :, :].rearrange("o i c -> o (i c)"), start=True, stop=False, skip_group_check=True)
                yield 12
                wait(pe, attT0_r, b, 1)
                for i in range(NT):
                    last = pe.matmul(F0[:, i * P:(i + 1) * P], attT[:, i * P:(i + 1) * P], projT[:, :], start=False, stop=(i == NT - 1), skip_group_check=True)
                last.then_inc(proj_ps[0], 1)
                yield 15
                ln_turn(b, 2, F1)
                yield 16
                wait(pe, ln_evac, b, 2)
                for j in range(NJ + 1):
                    if j < NJ:
                        if j >= 2:
                            wait(pe, hid_r, b, j - 1)
                        pe.matmul((F2, F3)[j % 2][:, :], fc1T[:, j * P:(j + 1) * P], h2T[:, :], start=True, stop=True).then_inc(fc1_ps[0], 1)
                    if j >= 1:
                        wait(pe, hid_r, b, j)
                        last = pe.matmul(F1[:, :], fc2T[:, j - 1, :], hid[:, j - 1, :], start=(j == 1), stop=(j == NJ))
                    if j < NJ:
                        yield 17 + j
                last.then_inc(fc2_ps[0], 1)
                yield 22
                wait(pe, y0_r, b, 1)
                transposes(F0, lambda i: yS[:, i * P:(i + 1) * P]).then_inc(y0_T[0], 1)
                yield 24

            h2T = h1T

            def moe_in(b):
                yield 2
                ln_turn(b, 3, F1)
                yield 3

            def experts(b):
                hbT = h1T
                n_all = NE * NJ
                wait(pe, ln_evac, b, 3)
                wait(pe, x3_r, b, 1)
                for n in range(n_all + 2):
                    if n < n_all:
                        e, j = n // NJ, n % NJ
                        if n >= 1:
                            wait(pe, silu_r, b, n)
                        if j == 0:
                            wait(pe, experts_in[e % 2], b, 48 * (e // 2 + 1))
                        pe.matmul(F0[:, :], Wg[:, e % 2, j * P:(j + 1) * P], hbT[:, :], start=True, stop=True).then_inc(gu_g[0], 1)
                        if n >= 2:
                            wait(pe, act_r, b, n - 1)
                        pe.matmul((F2, F3)[n % 2][:, :], Wu[:, e % 2, j * P:(j + 1) * P], hbT[:, :], start=True, stop=True).then_inc(gu_u[0], 1)
                    if n >= 2:
                        m = n - 2
                        e, j = m // NJ, m % NJ
                        wait(pe, act_r, b, m + 1)
                        pe.matmul(F1[:, :], Wd[:, e % 2, j, :], act[:, m % 3, :], start=(m == 0), stop=(m == n_all - 1)).then_inc(down_ps[0], 1)
                    if n < n_all - 1:
                        yield n + 1
                yield n_all

            def attn1(b):
                yield 1
                wait(pe, y1_r, b, 1)
                transposes(F0, lambda i: yS[:, i * P:(i + 1) * P]).then_inc(y1_T[0], 1)
                yield 4
                ln_turn(b, 4, F1)
                yield 5
                wait(pe, ln_evac, b, 4)
                wait(pe, x4_r, b, 1)
                hcT = h1T
                pe.matmul(F0[:, :], W1[:, 0:P], hcT[:, :], start=True, stop=True).then_inc(qkv1_ps[0], 1)
                pe.matmul(F2[:, :], W1[:, P:2 * P], hcT[:, :], start=True, stop=True).then_inc(qkv1_ps[0], 1)
                for i in range(NT):
                    last = pe.matmul(F3[:, i * P:(i + 1) * P], hcT[:, i * P:(i + 1) * P], W1[:, 2 * P:3 * P], start=True, stop=True)
                last.then_inc(qkv1_ps[0], 1)
                yield A1
                wait(pe, q1_r, b, 1)
                wait(pe, v1_r, b, 1)
                for n in range(N1 + 3):
                    if n < N1:
                        i, h = n // H1, n % H1
                        w = (i + 1) * P
                        f = (F0, F2)[n % 2]
                        if i == 0:
                            wait(pe, k1z_r[h // (H1 // 2)], b, h % (H1 // 2) + 1)
                        if n >= 2:
                            wait(pe, p1_r, b, n - 1)
                        pe.matmul(f[:, 0:w], q1T[:, i * P:(i + 1) * P], k1z[:, h, 0:w], start=True, stop=False, skip_group_check=True)
                        pe.matmul(f[:, w - P:w], ident_bf[:, :], causal_bf[:, :], start=False, stop=True, skip_group_check=True).then_inc(s1_ps[0], 1)
                    if 2 <= n <= N1 + 1:
                        m = n - 2
                        i = m // H1
                        wait(pe, p1_r, b, m + 1)
                        if m >= 1:
                            wait(pe, p1T_r, b, m)
                        transposes(F3, lambda j: p1[:, m % 2, j * P:(j + 1) * P], i + 1).then_inc(p1_T[0], 1)
                    if n >= 3:
                        m = n - 3
                        i, h = m // H1, m % H1
                        if h == 0 and i >= 1:
                            wait(pe, o1_r, b, i)
                        wait(pe, p1T_r, b, m + 1)
                        for j in range(i + 1):
                            last = pe.matmul(F1[:, h * (D1 + 1):(h + 1) * (D1 + 1)], p1T[:, m % 2, j * P:(j + 1) * P], v1[:, j, h, :], start=(j == 0), stop=(j == i))
                        if h == H1 - 1:
                            last.then_inc(o1_ps[0], 1)
                    yield A1 + 1 + n
                yield E1 + 1
                wait(pe, att1_r, b, 1)
                transposes(F0, lambda i: att[:, i, :]).then_inc(att1_T[0], 1)
                yield E1 + 2
                wait(pe, attT1_r, b, 1)
                wait(pe, WoutG_r, b, 1)
                for i in range(NT):
                    last = pe.matmul(F2[:, i * P:(i + 1) * P], attT[:, i * P:(i + 1) * P], WoutG[:, :], start=True, stop=True)
                last.then_inc(out1_ps[0], 1)
                yield E1 + 5
                ln_turn(b, 5, F1)
                yield MARKS["attn1"]

            def gates(b):
                wait(pe, ln_evac, b, 5)
                wait(pe, x5_r, b, 1)
                for k, f in enumerate((F0, F2)):
                    for i in range(2):
                        t = 2 * k + i
                        last = pe.matmul(f[:, i * 256:(i + 1) * 256], hdT[:, t * P:(t + 1) * P], gatesT[:, :], start=True, stop=True)
                    last.then_inc(gate_ps[0], 1)
                yield MARKS["gates"]

            def values(b):
                wait(pe, pT_r, b, 0)
                wait(pe, oa_r, b, 0)
                for n in range(NQ * NT):
                    if n == 0:
                        for i in range(2):
                            pe.matmul((TB, OB)[i][:, :], hdT[:, i * P:(i + 1) * P], WvT[:, :], start=True, stop=True).then_inc(pv_ps[0], 1)
                    if n % NQ == 0 and n // NQ in (1, 2):
                        i = n // NQ + 1
                        if i == 2:
                            wait(pe, s_out, b, 0)
                        pe.matmul((S0, S1)[i % 2][:, :], hdT[:, i * P:(i + 1) * P], WvT[:, :], start=True, stop=True).then_inc(pv_ps[0], 1)
                    if n % 4 == 2:
                        p = n // 4
                        if p < 2:
                            wait(pe, hdB_r, b, 1)
                            wait(pe, pv_r, b, p + 1)
                        if p >= 2:
                            wait(pe, ks_r, b, p - 1)
                        pe.matmul((TB, OB)[p % 2][:, :], WkT[:, p * P:(p + 1) * P], hdB[:, :], start=True, stop=True).then_inc(k_ps[0], 1)
                    yield n + 1

            def begin(b):
                wait(pe, pv_r, b, NT)
                yield from steps(b, 0, BEGIN)

            def heads(b):
                wait(pe, ks_r, b, NP)
                yield from steps(b, BEGIN, FINISH_AT)

            def finish(b):
                yield from steps(b, FINISH_AT, CLOSE_AT)

            def close(b):
                yield from steps(b, CLOSE_AT, len(HEAD_STEPS) + 1)

            def steps(b, first, end):
                for k in range(first, end):
                    kind, x, turn = step_of(k)
                    bank_k = (S0, S1)[turn % 2]
                    if kind != "rest" and turn > 2:
                        wait(pe, s_out, b, turn - 2)
                        if HEAD_STEPS[TURN.index(turn - 2)][0] == "queries":
                            wait(pe, ql_r, b, HEAD_STEPS[TURN.index(turn - 2)][1] + 1)
                    if kind == "queries":
                        for p in range(4):
                            last = pe.matmul(bank_k[:, p * P:(p + 1) * P], WqT[:, (4 * (x % 2) + p) * P:(4 * (x % 2) + p + 1) * P], hdB[:, (x // 2) * P:(x // 2 + 1) * P], start=True, stop=True)
                        last.then_inc(s_ps[0], 1)
                    if kind == "head":
                        i, h = x // HS, x % HS
                        j = 2 * i + h // (HS // 2)
                        h2 = h % (HS // 2)
                        if h2 == 0:
                            wait(pe, q_both, b, j + 1)
                        pe.matmul(bank_k[:, :], q_high[:, j % 3, h2, :], keys[:, h, :], start=True, stop=False)
                        pe.matmul(bank_k[:, :], q_low[:, j % 3, h2, :], keys[:, h, :], start=False, stop=True).then_inc(s_ps[0], 1)
                    if kind == "mixed":
                        wait(pe, ym_r, b, NQ * (x + 1))
                        transposes(bank_k, lambda j: ym[:, j * P:(j + 1) * P]).then_inc(s_ps[0], 1)
                    if kind == "result":
                        wait(pe, s_out, b, TURN[HEAD_STEPS.index(("mixed", x))])
                        for j in range(NJ):
                            last = pe.matmul(bank_k[:, 0:P], ymT[:, j, :], WoT[:, j, :], start=(j == 0), stop=(j == NJ - 1))
                        last.then_inc(s_ps[0], 1)
                    kind, m, turn = step_of(k - 2)
                    if kind == "head":
                        wait(pe, s_out, b, turn)
                        if m >= 1:
                            wait(pe, pT_r, b, m)
                        transposes(TB, lambda j: pr[:, m % 2, j * P:(j + 1) * P]).then_inc(p_T[0], 1)
                    kind, m, turn = step_of(k - 3)
                    if kind == "head":
                        i, h = m // HS, m % HS
                        if m == 0:
                            wait(pe, vals_r, b, NQ * NT)
                        if h % GROUP == 0 and m >= GROUP:
                            wait(pe, oa_r, b, m // GROUP)
                        wait(pe, pT_r, b, m + 1)
                        for j in range(NT):
                            last = pe.matmul(OB[:, (h % GROUP) * VW:(h % GROUP + 1) * VW], prT[:, m % 2, j * P:(j + 1) * P], vals[:, j, h, :], start=(j == 0), stop=(j == NT - 1))
                        if h % GROUP == GROUP - 1:
                            last.then_inc(o_ps[0], 1)
                    if k + 1 == end or mark_of(k + 1) > mark_of(k):
                        yield mark_of(k)

            program(pe, {"attn0": attn0, "moe_in": moe_in, "experts": experts, "attn1": attn1, "gates": gates,
                      "values": values, "begin": begin,
                        "heads": heads, "finish": finish, "close": close})

        @block.scalar
        def _(s):
            s.dma_start(raw_qkv, a["L0_attn_qkv_w"].rearrange("(i p) c -> p i c", p=P)).then_inc(raw_in[0], 16)
            s.dma_start(raw_proj, a["L0_attn_proj_w"]).then_inc(raw_in[0], 16)
            s.dma_start(raw_fc1, a["L0_attn_fc1_w"].rearrange("(i p) c -> p i c", p=P)).then_inc(raw_in[0], 16)
            s.dma_start(raw_fc2, a["L0_attn_fc2_w"].rearrange("p (i c) -> p i c", c=P)).then_inc(raw_in[0], 16)
            s.dma_start(raw_wq, a["L1_ffn_Wq"].rearrange("(i a) d c -> (a d) i c", a=2)).then_inc(raw_in[0], 16)
            s.dma_start(raw_wk, a["L1_ffn_Wk"].rearrange("(i a) d c -> (a d) i c", a=2)).then_inc(raw_in[0], 16)
            s.dma_start(raw_wv, a["L1_ffn_Wv"].rearrange("(i a) d c -> (a d) i c", a=2)).then_inc(raw_in[0], 16)
            s.dma_start(raw_wo.rearrange("p i (a d) -> p (i a) d", a=2), a["L1_ffn_Wo"].rearrange("e f d -> f e d")).then_inc(raw_in[0], 16)
            s.dma_start(raw_gates[:, 0, :], a["L1_ffn_Ws"].rearrange("h e c -> (h e) c")).then_inc(raw_in[0], 16)
            s.dma_start(raw_gates[:, 1, :], a["L1_ffn_Wd"].rearrange("h e c -> (h e) c")).then_inc(raw_in[0], 16)
            s.dma_start(W1[:, :], a["L1_attn_Wqkv"]).then_inc(raw_in[0], 16)
            s.dma_start(Wout[:, :], a["L1_attn_Wout"]).then_inc(raw_in[0], 16)
            s.wait_ge(small_in[0], 16 * 16)
            for l in range(2):
                s.activation(cexp[l], crow[l], ACT.Exp, scale=-1.0).then_inc(const_v[0], 1)
            s.wait_ge(setup_done[0], 1)

            def ln_out(b, n, dst, src, scale, bias):
                wait(s, ln_T, b, n)
                s.activation(dst, src, ACT.Identity, scale=scale, bias=bias).then_inc(ln_evac[0], 1)

            def attn0(b):
                yield 3
                ln_out(b, 1, h1T[:, :], F0[:, :], cols[:, 0:1], cols[:, 1:2])
                yield 5
                wait(s, emin_r, b, 1)
                s.activation(qexp, qmin, ACT.Exp).then_inc(eexp_r[0], 1)
                for k in range(2):
                    wait(s, emin_r, b, 2 + k)
                    s.activation(kexp[:, 2 * k:2 * k + 2, :], kmin[:, 2 * k:2 * k + 2, :], ACT.Exp).then_inc(eexp_r[0], 1)
                    s.activation(v0[:, 2 * k:2 * k + 2, 0:P], (F2, F3)[k][:, :].rearrange("p (i c) -> p i c", i=2)[:, :, P:2 * P], ACT.Copy).then_inc(v0_r[0], 1)
                yield 11
                wait(s, att0_T, b, 1)
                s.activation(attT[:, :], F1[:, :], ACT.Copy).then_inc(attT0_r[0], 1)
                yield 15
                ln_out(b, 2, h1T[:, :], F1[:, :], cols[:, 2:3], cols[:, 3:4])
                yield 16
                for j in range(NJ):
                    wait(s, fc1_ps, b, j + 1)
                    s.activation(hid[:, j, :], (F2, F3)[j % 2][:, :], ACT.Gelu, bias=cols[:, 4 + j:5 + j]).then_inc(hid_r[0], 1)
                    yield 17 + j
                yield 24

            def moe_in(b):
                yield 2
                wait(s, modB_r, b, 1)
                ln_out(b, 3, h1T[:, :], F1[:, :], modB[:, CB0:CB0 + 1], modB[:, SB0:SB0 + 1])
                yield 3

            def experts(b):
                for n in range(NE * NJ):
                    wait(s, gu_g, b, n + 1)
                    if n >= 2:
                        wait(s, act_r, b, n - 1)
                    s.activation(silu[:, n % 2, :], F0[:, :], ACT.Silu).then_inc(silu_r[0], 1)
                    yield n + 1
                yield MARKS["experts"]

            def attn1(b):
                yield 4
                ln_out(b, 4, h1T[:, :], F1[:, :], modB[:, CA1:CA1 + 1], modB[:, SA1:SA1 + 1])
                yield 5
                wait(s, qkv1_ps, b, 1)
                s.activation(q1T[:, :], F0[:, :], ACT.Copy).then_inc(q1_r[0], 1)
                wait(s, qkv1_ps, b, 3)
                s.activation(v1[:, :, :, 0:D1], F3[:, :].rearrange("p (i h d) -> p i h d", i=NT, h=H1), ACT.Copy).then_inc(v1_r[0], 1)
                wait(s, k1_r, b, 1)
                for h in range(H1 // 2):
                    s.activation(k1z[:, h, :], k1T, ACT.Copy, scale=head_of16[:, h:h + 1]).then_inc(k1z_r[0][0], 1)
                yield A1
                for n in range(N1 + 2):
                    if n >= 2:
                        m = n - 2
                        w = (m // H1 + 1) * P
                        wait(s, p1_T, b, m + 1)
                        s.activation(p1T[:, m % 2, 0:w], F3[:, 0:w], ACT.Copy).then_inc(p1T_r[0], 1)
                    if n < N1:
                        w = (n // H1 + 1) * P
                        wait(s, nmax1_r, b, n + 1)
                        if n >= 2:
                            wait(s, p1_T, b, n - 1)
                        s.activation(p1[:, n % 2, 0:w], (F0, F2)[n % 2][:, 0:w], ACT.Exp, bias=nmax1[:, n % 2:n % 2 + 1]).then_inc(p1_r[0], 1)
                    yield A1 + 1 + n
                yield E1 + 1
                wait(s, att1_T, b, 1)
                s.activation(attT[:, :], F0[:, :], ACT.Copy).then_inc(attT1_r[0], 1)
                yield E1 + 5
                wait(s, pv_ps, b, 0)
                ln_out(b, 5, hdT[:, :], F1[:, :], modB[:, CB1:CB1 + 1], modB[:, SB1:SB1 + 1])
                yield MARKS["attn1"]

            def gates(b):
                for k, f in enumerate((F0, F2)):
                    wait(s, gate_ps, b, k + 1)
                    for i in range(2):
                        last = s.activation(gate[:, :, 2 * k + i, :, :].rearrange("p g h e -> p g (h e)"),
                                            f[:, i * 256:(i + 1) * 256].rearrange("p (g c) -> p g c", g=2), ACT.Copy)
                    last.then_inc(gate_r[0], 1)
                yield 7
                wait(s, topk_v, b, 6)
                s.activation(sigd[:, :, :], top[:, :, 0:NT * HS], ACT.Exp, scale=-1.0).then_inc(sig_e[0], 1)
                yield MARKS["gates"]

            def values(b):
                wait(s, vals_r, b, 0)
                for n in range(NQ * NT):
                    if n == 0 or n % NQ == NQ // 2:
                        for i in (0, 1) if n == 0 else (n // NQ + 1,) if 1 <= n // NQ < NT - 1 else ():
                            wait(s, pv_ps, b, i + 1)
                            if i >= 2:
                                wait(s, vals_r, b, NQ * (i - 1))
                            s.activation(pv[:, i % 2, :], (TB, OB, S0, S1)[i][:, :], ACT.Copy).then_inc(pv_r[0], 1)
                    if n % 4 == 3:
                        p = n // 4
                        wait(s, k_ps, b, p + 1)
                        for odd in range(2):
                            r = DS * odd
                            s.activation(keys[r:r + DS, 2 * p + odd, :], (TB, OB)[p % 2][r:r + DS, :], ACT.Copy).then_inc(kh_r[0], 1)
                    if n == 0:
                        wait(s, ql_r, b, 0)
                        s.activation(hdB[:, :], hdT[:, :], ACT.Copy).then_inc(hdB_r[0], 1)
                        wait(s, coef_r, b, 0)
                        wait(s, masko_r, b, 1)
                        s.activation(maskB[:, :, :, :].rearrange("p i h e -> p (i h e)"), masko[:, :, :, :].rearrange("p i h e -> p (i h e)"), ACT.Copy).then_inc(maskB_r[0], 1)
                    if n == NQ * NT // 2:
                        wait(s, stored, b, 0)
                        s.activation(xout[:, :, :], x5[:, :, :], ACT.Copy).then_inc(xcopy_r[0], 1)
                    yield n + 1

            def begin(b):
                yield from steps(b, 0, BEGIN)

            def heads(b):
                yield from steps(b, BEGIN, FINISH_AT)

            def finish(b):
                yield from steps(b, FINISH_AT, CLOSE_AT)

            def close(b):
                yield from steps(b, CLOSE_AT, len(HEAD_STEPS) + 1)

            def steps(b, first, end):
                for k in range(first, end):
                    kind, m, _ = step_of(k - 4)
                    if kind == "head" and m % GROUP == GROUP - 1:
                        c, i = m // GROUP, m // HS
                        wait(s, o_ps, b, c + 1)
                        if c % NG == 0 and i >= 2:
                            wait(s, ym_r, b, NQ * (i - 1))
                        s.activation(oa[:, i % 2, GROUP * (c % NG):GROUP * (c % NG + 1), :].rearrange("p h d -> p (h d)"), OB[:, 0:GROUP * VW], ACT.Copy).then_inc(oa_r[0], 1)
                    kind, m, _ = step_of(k - 2)
                    if kind == "head":
                        wait(s, p_T, b, m + 1)
                        s.activation(prT[:, m % 2, :], TB[:, :], ACT.Copy).then_inc(pT_r[0], 1)
                    kind, x, _ = step_of(k - 2)
                    if kind == "queries":
                        wait(s, ql_r, b, x + 1)
                        for part in (q_high, q_low):
                            for odd in range(2):
                                last = s.activation(other_half(part, x, odd), own_half(part, x, odd), ACT.Copy)
                        last.then_inc(q_both[0], 1)
                    kind, x, turn = step_of(k)
                    bank_k = (S0, S1)[turn % 2]
                    if kind == "queries":
                        wait(s, s_ps, b, turn)
                        for odd in range(2):
                            last = s.activation(own_half(q_high, x, odd), queries_of(bank_k, odd), ACT.Copy)
                        last.then_inc(s_out[0], 1)
                    if kind == "head":
                        wait(s, nmax_r, b, x + 1)
                        if x >= 2:
                            wait(s, p_T, b, x - 1)
                        s.activation(pr[:, x % 2, :], bank_k[:, :], ACT.Exp, bias=nmax[:, x % 2:x % 2 + 1]).then_inc(s_out[0], 1)
                    if kind == "mixed":
                        wait(s, s_ps, b, turn)
                        s.activation(ymT[:, :, :].rearrange("p j t -> p (j t)"), bank_k[:, :], ACT.Copy).then_inc(s_out[0], 1)
                    if kind == "result":
                        wait(s, s_ps, b, turn)
                        wait(s, xout_r, b, x)
                        s.activation(resc[:, :], bank_k[:, 0:P], ACT.Copy).then_inc(s_out[0], 1)
                    if k + 1 == end or mark_of(k + 1) > mark_of(k):
                        yield mark_of(k)

            program(s, {"attn0": attn0, "moe_in": moe_in, "experts": experts, "attn1": attn1, "gates": gates,
                     "values": values, "begin": begin,
                        "heads": heads, "finish": finish, "close": close})

        @block.vector
        def _(v):
            v.wait_ge(small_in[0], 16 * 16)
            v.wait_ge(const_v[0], 2)
            for l in range(2):
                v.tensor_scalar(cexp[l], cexp[l], 1.0, None, ALU.add)
            v.tensor_tensor(sdirs.rearrange("o (h d) -> o h d", h=H1), dirs.rearrange("o (h d) -> o h d", h=H1),
                            scales.unsqueeze(2).to_broadcast([1, H1, D1]), ALU.mult).then_inc(const_v[0], 3)
            v.wait_ge(const_v[0], 5)
            for l in range(2):
                last = v.reciprocal(crec[l], cexp[l])
            last.then_inc(const_v[0], 2)
            v.wait_ge(const_v[0], 7)
            for l in range(2):
                last = v.tensor_tensor(csil[l], crow[l], crec[l], ALU.mult)
            last.then_inc(const_v[0], 2)
            for n in range((NTURN + 3) // 4):
                part = turns[4 * n:4 * n + 4]
                v.wait_ge(setup_pe[0], n + 1)
                for i, (_, dst) in enumerate(part):
                    src = bank[n % 2][:, i * P:(i + 1) * P]
                    if 12 <= 4 * n + i < 20:
                        last = v.tensor_scalar(dst, src, DS ** -0.5, None, ALU.mult)
                    else:
                        last = v.tensor_copy(dst, src)
                last.then_inc(setup_v[0], 1)
            n = (NTURN + 3) // 4
            v.wait_ge(setup_pe[0], n + 1)
            v.tensor_copy(stage[:, 6, 0:2 * NB], bank[2][:, 0:2 * NB])
            v.tensor_copy(cols[:, :], bank[2][:, 2 * NB:2 * NB + 9])
            v.wait_ge(const_g[0], 12)
            v.tensor_tensor(bias_m, bank[3][:, 0:P], block16, ALU.mult).then_inc(setup_v[0], 1)
            v.wait_ge(setup_v[0], n + 1)
            v.scalar_tensor_tensor(out=bias_m, in0=ident[:, :], scalar=D1 ** -0.5, in1=bias_m, op0=ALU.mult, op1=ALU.add).then_inc(setup_v[0], 1)
            v.wait_ge(setup_pe[0], n + 2)
            v.tensor_copy(mod[:, :, :].rearrange("p b m -> p m b"), bank[4][:, 0:96].rearrange("p (m b) -> p m b", m=12)).then_inc(setup_v[0], 1)
            v.wait_ge(setup_pe[0], n + 3)
            v.tensor_copy(W1[:, 0:P], bank[5][:, 0:P])

            def floor_gate(g, s, w, k):
                v.tensor_scalar(s, g, 0.0, 2.0, ALU.is_ge, ALU.mult).then_inc(setup_v[0], 1)
                v.wait_ge(setup_v[0], k + 1)
                v.tensor_scalar(s, s, -1.0, None, ALU.add).then_inc(setup_v[0], 1)
                v.wait_ge(setup_v[0], k + 2)
                v.tensor_tensor(w, g, s, ALU.mult).then_inc(setup_v[0], 1)
                v.wait_ge(setup_v[0], k + 3)
                v.tensor_scalar(w, w, 0.25, None, ALU.max).then_inc(setup_v[0], 1)
                v.wait_ge(setup_v[0], k + 4)
                v.tensor_tensor(g, w, s, ALU.mult).then_inc(setup_v[0], 1)
                v.wait_ge(setup_v[0], k + 5)

            v.wait_ge(setup_v[0], n + 3)
            k = n + 3
            for m in (CA0, CB0, CA1, CB1):
                v.tensor_scalar(mod[:, :, m], mod[:, :, m], 1.0, None, ALU.add)
            floor_gate(mod[:, :, GA0::3], sgn, gab, k)
            k += 5
            v.wait_ge(setup_pe[0], n + 4)
            v.tensor_copy(rtab[:, 0:3, :].rearrange("p m c -> p (m c)"), bank[6][0:NB, 0:3 * P])
            v.tensor_copy(rtab[:, 3:5, :].rearrange("p m c -> p (m c)"), bank[7][0:NB, 0:2 * P]).then_inc(setup_v[0], 1)
            k += 1
            v.wait_ge(setup_v[0], k)
            v.tensor_scalar(rtab[:, 1, :], rtab[:, 1, :], 1.0, None, ALU.add)
            floor_gate(rtab[:, 2:5, :], rsgn, rabs, k)
            v.memset(nmax1[:, :], 0.0).then_inc(setup_done[0], 1)
            v.memset(vals[:, :, :, DS:DS + 1], 1.0)

            def stats_of(b, n, src):
                for i in range(NT):
                    last = v.bn_stats(stats[:, i, :], src[:, i, :])
                last.then_inc(ln_stats[0], 1)
                wait(v, ln_stats, b, n + 1)
                v.memset(pause[:, :], 0.0)
                for i in range(NT):
                    last = v.bn_aggr(mv[:, i, :], stats[:, i, :])
                last.then_inc(ln_mv[0], 1)
                wait(v, ln_mv, b, n + 1)
                v.tensor_scalar(vareps[:, :], mv[:, :, 1], EPS_LN, None, ALU.add).then_inc(ln_eps[0], 1)

            def norm_of(b, n, src):
                wait(v, ln_rstd, b, n + 1)
                for i in range(NT):
                    last = v.tensor_scalar(nrm[:, i, :], src[:, i, :], mv[:, i, 0:1], rstd[:, i:i + 1], ALU.subtract, ALU.mult)
                last.then_inc(ln_n[0], 1)

            def attn0(b):
                wait(v, x5_r, b, 0)
                v.tensor_scalar(modA[:, :], mod[:, bass.ds(b[0] + b[1], 1), :].rearrange("p o m -> p (o m)"), 1.0, None, ALU.mult).then_inc(modA_r[0], 1)
                wait(v, x_in, b, 32)
                stats_of(b, 0, xin)
                yield 1
                norm_of(b, 0, xin)
                wait(v, ln_n, b, 1)
                wait(v, mix_g, b, 0)
                v.tensor_tensor(h0m, nrm[:, :, :], rows0[:, 1:2, :].to_broadcast([P, NT, P]), ALU.mult).then_inc(h0m_r[0], 1)
                wait(v, h0m_r, b, 1)
                v.tensor_tensor(h0[:, :, :], h0m, rows0[:, 0:1, :].to_broadcast([P, NT, P]), ALU.add).then_inc(h0_r[0], 1)
                wait(v, h0_r, b, 1)
                stats_of(b, 1, h0)
                yield 2
                norm_of(b, 1, h0)
                yield 5
                kview = [f[:, :].rearrange("p (i c) -> p i c", i=2)[:, :, 0:P] for f in (F2, F3)]
                wait(v, qkv0_r, b, 1)
                v.tensor_scalar(qmin, F1[:, :], 0.0, None, ALU.min).then_inc(emin_r[0], 1)
                for k in range(2):
                    wait(v, qkv0_r, b, 2 + k)
                    v.tensor_scalar(kmin[:, 2 * k:2 * k + 2, :], kview[k], 0.0, None, ALU.min).then_inc(emin_r[0], 1)
                yield 6
                v.memset(v0[:, :, P:P + 1], 1.0)
                wait(v, eexp_r, b, 1)
                v.scalar_tensor_tensor(out=qe, in0=F1[:, :], scalar=0.0, in1=qexp, op0=ALU.max, op1=ALU.add).then_inc(elu_r[0], 1)
                for k in range(2):
                    wait(v, eexp_r, b, 2 + k)
                    wait(v, v0_r, b, 1 + k)
                    v.scalar_tensor_tensor(out=ke[:, 2 * k:2 * k + 2, :], in0=kview[k], scalar=0.0, in1=kexp[:, 2 * k:2 * k + 2, :], op0=ALU.max, op1=ALU.add).then_inc(elu_r[0], 1)
                yield 8
                wait(v, kv_ps, b, 1)
                v.tensor_tensor(kv[:, 0:P], F0[:, 0:P], block8[:, :], ALU.mult)
                v.tensor_scalar(kv[:, P:P + H0], head_of8[:, :], F0[:, P:P + 1], None, ALU.mult).then_inc(kv_r[0], 1)
                yield 10
                nview = [f[:, :].rearrange("p (i c) -> p i c", i=2) for f in (F2, F3)]
                wait(v, num_ps, b, 2)
                for k in range(2):
                    last = v.tensor_scalar(den0[:, 2 * k:2 * k + 2, :], nview[k][:, :, P:P + H0], EPS_ATTN, None, ALU.add)
                last.then_inc(den0_r[0], 1)
                wait(v, den0_r, b, 1)
                v.reciprocal(rden0[:, :, :], den0[:, :, :]).then_inc(rden0_r[0], 1)
                wait(v, rden0_r, b, 1)
                for t in range(NT):
                    last = v.tensor_tensor(att[:, t, :].rearrange("p (h d) -> p h d", h=H0),
                                           nview[t // 2][:, t % 2, 0:P].rearrange("p (h d) -> p h d", h=H0),
                                           rden0[:, t, :].unsqueeze(2).to_broadcast([P, H0, D0]), ALU.mult)
                last.then_inc(att0_r[0], 1)
                yield 13
                wait(v, proj_ps, b, 1)
                v.tensor_tensor(x2[:, :, :], tiles(F0), h0[:, :, :], ALU.add).then_inc(x2_r[0], 1)
                wait(v, x2_r, b, 1)
                stats_of(b, 2, x2)
                yield 14
                norm_of(b, 2, x2)
                yield 21
                wait(v, fc2_ps, b, 1)
                v.tensor_scalar(yS, F1[:, :], cols[:, 8:9], modA[:, GA0:GA0 + 1], ALU.add, ALU.mult).then_inc(y0_r[0], 1)
                yield 23
                wait(v, y0_T, b, 1)
                wait(v, xg_r, b, 1)
                v.tensor_tensor(x3[:, :, :], tiles(F0), xg[:, :, :], ALU.add).then_inc(x3_r[0], 1)
                yield 24

            def moe_in(b):
                wait(v, ln_evac, b, 0)
                v.tensor_scalar(modB[:, :], mod[:, bass.ds(b[0] + b[1], 1), :].rearrange("p o m -> p (o m)"), 1.0, None, ALU.mult).then_inc(modB_r[0], 1)
                wait(v, x3_r, b, 1)
                stats_of(b, 3, x3)
                yield 1
                norm_of(b, 3, x3)
                yield 3

            def experts(b):
                for n in range(NE * NJ):
                    wait(v, silu_r, b, n + 1)
                    wait(v, gu_u, b, n + 1)
                    if n >= 3:
                        wait(v, down_ps, b, n - 2)
                    v.tensor_tensor(act[:, n % 3, :], (F2, F3)[n % 2][:, :], silu[:, n % 2, :], ALU.mult).then_inc(act_r[0], 1)
                    yield n + 1

            def attn1(b):
                wait(v, down_ps, b, NE * NJ)
                v.tensor_scalar(yS, F1[:, :], modB[:, GB0:GB0 + 1], None, ALU.mult).then_inc(y1_r[0], 1)
                yield 1
                wait(v, y1_T, b, 1)
                v.tensor_tensor(x4[:, :, :], tiles(F0), x3[:, :, :], ALU.add).then_inc(x4_r[0], 1)
                yield 2
                wait(v, x4_r, b, 1)
                stats_of(b, 4, x4)
                yield 3
                norm_of(b, 4, x4)
                yield 5
                wait(v, qkv1_ps, b, 2)
                v.tensor_copy(k1T, F2[:, :]).then_inc(k1_r[0], 1)
                yield A1
                for n in range(N1 + 3):
                    if n >= H1 + 3 and n % H1 == 3:
                        i = n // H1 - 1
                        wait(v, o1_ps, b, i + 1)
                        v.tensor_copy(o1[:, i, :, :].rearrange("p h d -> p (h d)"), F1[:, 0:H1 * (D1 + 1)]).then_inc(o1_r[0], 1)
                    if n < N1:
                        w = (n // H1 + 1) * P
                        wait(v, s1_ps, b, n + 1)
                        if n >= 2:
                            wait(v, p1_r, b, n - 1)
                        v.tensor_reduce(nmax1[:, n % 2:n % 2 + 1], (F0, F2)[n % 2][:, 0:w], X_AXIS, ALU.max, negate=True).then_inc(nmax1_r[0], 1)
                    yield A1 + 1 + n
                wait(v, o1_ps, b, NT)
                v.tensor_copy(o1[:, NT - 1, :, :].rearrange("p h d -> p (h d)"), F1[:, 0:H1 * (D1 + 1)]).then_inc(o1_r[0], 1)
                wait(v, o1_r, b, NT)
                v.reciprocal(rden1[:, :, :], o1[:, :, :, D1]).then_inc(rden1_r[0], 1)
                wait(v, rden1_r, b, 1)
                v.tensor_tensor(att[:, :, :].rearrange("p i (h d) -> p i h d", h=H1), o1[:, :, :, 0:D1],
                                rden1[:, :, :].unsqueeze(3).to_broadcast([P, NT, H1, D1]), ALU.mult).then_inc(att1_r[0], 1)
                yield E1 + 3
                wait(v, out1_ps, b, 1)
                wait(v, xcopy_r, b, 0)
                v.tensor_tensor(x5[:, :, :], tiles(F2), x4[:, :, :], ALU.add).then_inc(x5_r[0], 1)
                wait(v, x5_r, b, 1)
                stats_of(b, 5, x5)
                yield E1 + 4
                norm_of(b, 5, x5)
                yield MARKS["attn1"]

            def gates(b):
                g = gate.rearrange("p g i h e -> p (g i h) e")
                n = 2 * NT * HS
                half = NT * HS

                def wide(t):
                    return t.unsqueeze(2).to_broadcast([P, n, NE])

                wait(v, gate_r, b, 2)
                v.tensor_reduce(top[:, 0, :], g, X_AXIS, ALU.max).then_inc(topk_v[0], 1)
                for r in range(2):
                    one = (oh1, oh2)[r]
                    k = 5 * r
                    wait(v, topk_v, b, k + 1)
                    if r == 0:
                        yield 1
                    v.tensor_tensor(eq, g, wide(top[:, r, :]), ALU.is_ge).then_inc(topk_v[0], 1)
                    yield 3 + 6 * r
                    wait(v, topk_g, b, r + 1)
                    v.tensor_reduce(pick[:, :], cand, X_AXIS, ALU.max).then_inc(topk_v[0], 1)
                    yield 4 + 6 * r
                    wait(v, topk_v, b, k + 3)
                    v.tensor_tensor(one, cand, wide(pick[:, :]), ALU.is_equal).then_inc(topk_v[0], 1)
                    yield 5 + 6 * r
                    if r == 0:
                        wait(v, topk_v, b, 4)
                        v.scalar_tensor_tensor(out=g, in0=oh1, scalar=-BIG, in1=g, op0=ALU.mult, op1=ALU.add).then_inc(topk_v[0], 1)
                        yield 6
                        wait(v, topk_v, b, 5)
                        v.tensor_reduce(top[:, 1, :], g, X_AXIS, ALU.max).then_inc(topk_v[0], 1)
                        yield 7
                wait(v, sig_e, b, 1)
                v.tensor_scalar(sigd[:, :, :], sigd[:, :, :], 1.0, None, ALU.add).then_inc(sig_v[0], 1)
                wait(v, sig_v, b, 1)
                v.reciprocal(sig[:, :, :], sigd[:, :, :]).then_inc(sig_v[0], 1)
                yield 12
                wait(v, topk_v, b, 9)
                wait(v, maskB_r, b, 0)
                v.tensor_tensor(masko[:, :, :, :].rearrange("p i h e -> p (i h) e"), oh1[:, half:n, :], oh2[:, half:n, :], ALU.add).then_inc(masko_r[0], 1)
                yield MARKS["gates"]

            def values(b):
                wait(v, mix_g, b, 3)
                wait(v, ym_r, b, 0)
                for n in range(NQ * NT + 1):
                    if n in values_v(b):
                        wait(v, pv_r, b, n // NQ + 1)
                        if n >= NPROD:
                            wait(v, vals_r, b, n - NPROD + 1)
                        v.tensor_tensor(*value_piece(n), ALU.mult).then_inc(vprod_v[0], 1)
                    if n >= 1:
                        m = n - 1
                        i, q = m // NQ, m % NQ
                        if m not in values_v(b):
                            wait(v, vprod_r, b, by_pool(m + 1, values_v(b)))
                        else:
                            wait(v, vprod_v, b, by_vector(m + 1, values_v(b)))
                        v.tensor_reduce(vals[:, i, HQ * q:HQ * q + HQ, 0:DS], prod[:, m % NPROD, :].rearrange("p (h d e) -> p h d e", h=HQ, e=NE), X_AXIS, ALU.add).then_inc(vals_r[0], 1)
                    if n % 4 == 3:
                        p = n // 4
                        for odd in range(2):
                            r = DS * odd
                            wait(v, kh_r, b, 2 * p + odd + 1)
                            last = v.tensor_tensor(keys[DS - r:2 * DS - r, 2 * p + odd, :], (TB, OB)[p % 2][r:r + DS, :], keys[r:r + DS, 2 * p + odd, :], ALU.subtract)
                        last.then_inc(ks_r[0], 1)
                    yield n + 1

            def begin(b):
                yield from steps(b, 0, BEGIN)

            def heads(b):
                wait(v, rows1b_in, b, 16)
                wait(v, xcopy_r, b, 1)
                yield from steps(b, BEGIN, FINISH_AT)

            def finish(b):
                yield from steps(b, FINISH_AT, CLOSE_AT)

            def close(b):
                yield from steps(b, CLOSE_AT, len(HEAD_STEPS) + 1)

            def steps(b, first, end):
                def piece(n):
                    if n not in OUTPUTS_V:
                        wait(v, oprod_r, b, by_pool(n + 1, OUTPUTS_V))
                    else:
                        if n >= NPROD:
                            wait(v, ym_r, b, n - NPROD + 1)
                        v.tensor_tensor(*output_piece(n), ALU.mult).then_inc(oprod_v[0], 1)
                        wait(v, oprod_v, b, by_vector(n + 1, OUTPUTS_V))
                    if n % NQ == 0:
                        wait(v, s_ps, b, TURN[HEAD_STEPS.index(("mixed", n // NQ - 1))] if n else 0)
                    v.tensor_reduce(ym[:, (n % NQ) * DS:(n % NQ + 1) * DS], prod[:, n % NPROD, :].rearrange("p (d h) -> p d h", h=HS), X_AXIS, ALU.add).then_inc(ym_r[0], 1)

                def out_tile(i):
                    wait(v, s_out, b, TURN[HEAD_STEPS.index(("result", i))])
                    v.tensor_tensor(resg[:, :], resc[:, :], rows1b[:, :], ALU.mult).then_inc(resg_r[0], 1)
                    wait(v, resg_r, b, i + 1)
                    v.tensor_tensor(xout[:, i, :], resg[:, :], xout[:, i, :], ALU.add).then_inc(xout_r[0], 1)


                for k in range(first, end):
                    kind, m, _ = step_of(k - 4)
                    if kind == "head" and m % HS == HS - 1:
                        i = m // HS
                        wait(v, oa_r, b, NG * (i + 1))
                        v.reciprocal(rden[:, i % 2, :], oa[:, i % 2, :, DS]).then_inc(rden_r[0], 1)
                    kind, m, _ = step_of(k - 1)
                    if kind == "result":
                        out_tile(m)
                    kind, m, turn = step_of(k)
                    if kind == "head":
                        wait(v, s_ps, b, turn)
                        if m >= 2:
                            wait(v, s_out, b, TURN[HEAD_STEPS.index(("head", m - 2))])
                        v.tensor_reduce(nmax[:, m % 2:m % 2 + 1], (S0, S1)[turn % 2][:, :], X_AXIS, ALU.max, negate=True).then_inc(nmax_r[0], 1)
                    kind, m, turn = step_of(k - 1)
                    if kind == "queries":
                        wait(v, s_out, b, turn)
                        for odd in range(2):
                            last = v.tensor_tensor(own_half(q_low, m, odd), queries_of((S0, S1)[turn % 2], odd), own_half(q_high, m, odd), ALU.subtract)
                        last.then_inc(ql_r[0], 1)
                    if k in PIECE_AT:
                        piece(PIECE_AT[k])
                    if k + 1 == end or mark_of(k + 1) > mark_of(k):
                        yield mark_of(k)

            program(v, {"attn0": attn0, "moe_in": moe_in, "experts": experts, "attn1": attn1, "gates": gates,
                     "values": values, "begin": begin,
                        "heads": heads, "finish": finish, "close": close})


NAMES = ['L0_attn_x', 'L0_attn_norm1_g', 'L0_attn_norm1_b', 'L0_attn_qkv_w', 'L0_attn_proj_w', 'L0_attn_proj_b',
         'L0_attn_norm2_g', 'L0_attn_norm2_b', 'L0_attn_fc1_w', 'L0_attn_fc1_b', 'L0_attn_fc2_w', 'L0_attn_fc2_b',
         'L0_ffn_Wg', 'L0_ffn_Wu', 'L0_ffn_Wd', 'L0_c', 'L0_wmod', 'L1_attn_Wqkv', 'L1_attn_Wout',
         'L1_attn_head_scales', 'L1_attn_head_dirs', 'L1_ffn_Wq', 'L1_ffn_Wk', 'L1_ffn_Wv', 'L1_ffn_Ws', 'L1_ffn_Wd',
         'L1_ffn_Wo', 'L1_c', 'L1_wmod']


def kernel(**inputs):
    import numpy as _np
    import concourse.bacc as _bacc
    from concourse import mybir as _mybir
    from concourse.bass_utils import run_bass_kernel_spmd as _run

    nc = _bacc.Bacc("TRN2", target_bir_lowering=False, num_devices=1)
    arrays, aps = {}, {}
    for name in NAMES:
        x = _np.ascontiguousarray(inputs[name])
        arrays[f"in_{name}"] = x
        aps[name] = nc.dram_tensor(f"in_{name}", x.shape, _mybir.dt.from_np(x.dtype), kind="ExternalInput").ap()
    out = nc.dram_tensor("out_0", (NB, T, P), F32, kind="ExternalOutput").ap()
    row_table = nc.dram_tensor("row_table", (NB, 5 * P), F32, kind="Internal").ap()
    build(nc, aps, row_table, out)
    r = _run(nc, [arrays], core_ids=[0])
    return r.results[0]["out_0"]
```
